# Optimizing a Trainium2 kernel written in Bass

```python
import numpy as np
import jax
import jax.numpy as jnp

def _softmax(x, axis=-1):
    return jax.nn.softmax(x, axis=axis)

def _gelu(x):
    return jax.nn.gelu(x, approximate=True)

def _silu(x):
    return jax.nn.silu(x)

def _sigmoid(x):
    return jax.nn.sigmoid(x)

def _layernorm(x, axis=-1, eps=1e-05):
    m = jnp.mean(x, axis=axis, keepdims=True)
    v = jnp.var(x, axis=axis, keepdims=True)
    return (x - m) / jnp.sqrt(v + eps)

def _scatter_add(tgt, idx, src, axis=0):
    return tgt.at[idx].add(src)

def _segment_sum(src, seg, n):
    return jax.ops.segment_sum(src, seg, n)
kernel_name = 'mk_adaln_d1_jaxref_r4_489817'

def setup_inputs(seed: int=0):
    np.random.seed(seed)
    _w = jnp.asarray

    def _L0_attn_setup():
        import jax, jax.numpy as jnp
        import numpy as np
        D_MODEL = 512
        N_QUERY = 4
        N_HEAD = 8
        D_HEAD = D_MODEL // (N_QUERY * N_HEAD)
        D_KV = D_HEAD * N_HEAD
        BATCH, SEQ = (2, 512)
        key = jax.random.key(seed)
        ks = jax.random.split(key, 5)
        w_scale = 1.0 / np.sqrt(D_MODEL).astype(np.float32)
        x = jax.random.normal(ks[0], (BATCH, SEQ, D_MODEL), jnp.float32)
        Wq = jax.random.normal(ks[1], (D_MODEL, D_MODEL), jnp.float32) * w_scale
        Wk = jax.random.normal(ks[2], (D_KV, D_MODEL), jnp.float32) * w_scale
        Wv = jax.random.normal(ks[3], (D_KV, D_MODEL), jnp.float32) * w_scale
        memory = jax.random.normal(ks[4], (D_KV, D_KV), jnp.float32) * 0.02
        memory_norm = jnp.ones((D_KV, 1), jnp.float32)
        memory_weight = jnp.ones((1,), jnp.float32)
        return dict(x=x, Wq=Wq, Wk=Wk, Wv=Wv, memory=memory, memory_norm=memory_norm, memory_weight=memory_weight)
    _L0_attn_in = _L0_attn_setup()

    def _L0_ffn_setup():
        import jax, jax.numpy as jnp
        import numpy as np
        B, S, D, M, E, K = (4, 512, 512, 1024, 8, 2)

        def _routed_moe(x, gate_w, w0, w1, wo):
            T = x.shape[0]
            logits = jnp.einsum('td,de->te', x, gate_w)
            top_logits, top_idx = jax.lax.top_k(logits, K)
            top_w = jax.nn.softmax(top_logits, axis=-1)
            cw = jnp.zeros((T, E), dtype=x.dtype).at[jnp.arange(T)[:, None], top_idx].add(top_w)
            out = jnp.zeros_like(x)
            for e in range(E):
                h = jax.nn.silu(x @ w0[e]) * (x @ w1[e])
                out = out + cw[:, e:e + 1] * (h @ wo[e])
            return out
        key = jax.random.key(seed)
        ks = jax.random.split(key, 5)
        inputs = jax.random.normal(ks[0], (B, S, D), dtype=jnp.float32)
        gate_w = jax.random.normal(ks[1], (D, E), dtype=jnp.float32) * D ** (-0.5)
        w0 = jax.random.normal(ks[2], (E, D, M), dtype=jnp.float32) * D ** (-0.5)
        w1 = jax.random.normal(ks[3], (E, D, M), dtype=jnp.float32) * D ** (-0.5)
        wo = jax.random.normal(ks[4], (E, M, D), dtype=jnp.float32) * M ** (-0.5)
        decoder_segment_ids = jax.random.randint(jax.random.fold_in(key, 1), (B, S), 0, 2).astype(jnp.int32)
        decoder_positions = jnp.tile(jnp.arange(S, dtype=jnp.int32)[None, :], (B, 1))
        return {'inputs': inputs, 'gate_w': gate_w, 'w0': w0, 'w1': w1, 'wo': wo, 'decoder_segment_ids': decoder_segment_ids, 'decoder_positions': decoder_positions}
    _L0_ffn_in = _L0_ffn_setup()
    _L0_c = _w((lambda *s: np.random.randn(*s).astype(np.float32) * 0.05)(2, 512))
    _L0_wmod = _w((lambda *s: np.random.randn(*s).astype(np.float32) * 0.05)(512, 6 * 512) * 512 ** (-0.5))
    _d = {'L0_attn_x': _L0_attn_in['x'], 'L0_attn_Wq': _L0_attn_in['Wq'], 'L0_attn_Wk': _L0_attn_in['Wk'], 'L0_attn_Wv': _L0_attn_in['Wv'], 'L0_attn_memory': _L0_attn_in['memory'], 'L0_attn_memory_norm': _L0_attn_in['memory_norm'], 'L0_attn_memory_weight': _L0_attn_in['memory_weight'], 'L0_ffn_gate_w': _L0_ffn_in['gate_w'], 'L0_ffn_w0': _L0_ffn_in['w0'], 'L0_ffn_w1': _L0_ffn_in['w1'], 'L0_ffn_wo': _L0_ffn_in['wo'], 'L0_ffn_decoder_segment_ids': _L0_ffn_in['decoder_segment_ids'], 'L0_ffn_decoder_positions': _L0_ffn_in['decoder_positions'], 'L0_c': _L0_c, 'L0_wmod': _L0_wmod}
    _x0 = _d['L0_attn_x']
    _d['L0_attn_x'] = jax.random.normal(jax.random.fold_in(jax.random.key(seed), 1), (2, 1024, 512), dtype=_x0.dtype)
    del _x0
    return _d

def reference(L0_attn_x, L0_attn_Wq, L0_attn_Wk, L0_attn_Wv, L0_attn_memory, L0_attn_memory_norm, L0_attn_memory_weight, L0_ffn_gate_w, L0_ffn_w0, L0_ffn_w1, L0_ffn_wo, L0_ffn_decoder_segment_ids, L0_ffn_decoder_positions, L0_c, L0_wmod):

    def _L0_attn_ref(x, Wq, Wk, Wv, memory, memory_norm, memory_weight):
        import jax, jax.numpy as jnp
        import numpy as np
        D_MODEL = 512
        N_QUERY = 4
        N_HEAD = 8
        D_HEAD = D_MODEL // (N_QUERY * N_HEAD)
        D_KV = D_HEAD * N_HEAD
        BATCH, SEQ = (2, 512)
        b, s, d = x.shape
        q = x @ Wq.T
        k = x @ Wk.T
        v = x @ Wv.T
        qh = q.reshape(b, s, N_QUERY, N_HEAD, D_HEAD)
        kh = k.reshape(b, s, N_HEAD, D_HEAD)
        vh = v.reshape(b, s, N_HEAD, D_HEAD)
        scale = np.float32(1.0 / np.sqrt(np.float32(D_HEAD)))
        scores = jnp.einsum('bsqhd,bthd->bqhst', qh, kh) * scale
        probs = jax.nn.softmax(scores, axis=-1)
        a_dot = jnp.einsum('bqhst,bthd->bsqhd', probs, vh)
        a_dot = a_dot.reshape(b, s, N_QUERY * N_HEAD, D_HEAD)
        sigma_q = jax.nn.elu(q.reshape(b, s, N_QUERY, D_KV))
        a_mem = sigma_q @ memory / (sigma_q @ memory_norm)
        a_mem = a_mem.reshape(b, s, N_QUERY * N_HEAD, D_HEAD)
        w = jax.nn.sigmoid(memory_weight)
        out = a_dot * (1.0 - w) + a_mem * w
        return out.reshape(b, s, D_MODEL)

    def _L0_ffn_ref(inputs, gate_w, w0, w1, wo, decoder_segment_ids, decoder_positions):
        import jax, jax.numpy as jnp
        import numpy as np
        B, S, D, M, E, K = (4, 512, 512, 1024, 8, 2)

        def _routed_moe(x, gate_w, w0, w1, wo):
            T = x.shape[0]
            logits = jnp.einsum('td,de->te', x, gate_w)
            top_logits, top_idx = jax.lax.top_k(logits, K)
            top_w = jax.nn.softmax(top_logits, axis=-1)
            cw = jnp.zeros((T, E), dtype=x.dtype).at[jnp.arange(T)[:, None], top_idx].add(top_w)
            out = jnp.zeros_like(x)
            for e in range(E):
                h = jax.nn.silu(x @ w0[e]) * (x @ w1[e])
                out = out + cw[:, e:e + 1] * (h @ wo[e])
            return out
        b, s, d = inputs.shape
        x = inputs.reshape(b * s, d)
        out = _routed_moe(x, gate_w, w0, w1, wo)
        return out.reshape(b, s, d)
    x = L0_attn_x
    mod = (_silu(L0_c) @ L0_wmod).reshape(L0_c.shape[0], 6, 1, -1)
    sa, ca, ga, sb, cb, gb = (mod[:, 0], mod[:, 1], mod[:, 2], mod[:, 3], mod[:, 4], mod[:, 5])
    ga = (2 * (ga >= 0) - 1) * jnp.maximum(jnp.abs(ga), 0.25)
    gb = (2 * (gb >= 0) - 1) * jnp.maximum(jnp.abs(gb), 0.25)
    h = _layernorm(x, axis=-1) * (1 + ca) + sa
    x = x + ga * _L0_attn_ref(h, L0_attn_Wq, L0_attn_Wk, L0_attn_Wv, L0_attn_memory, L0_attn_memory_norm, L0_attn_memory_weight)
    h = _layernorm(x, axis=-1) * (1 + cb) + sb
    x = x + gb * _L0_ffn_ref(h, L0_ffn_gate_w, L0_ffn_w0, L0_ffn_w1, L0_ffn_wo, L0_ffn_decoder_segment_ids, L0_ffn_decoder_positions)
    return x

_drawn_inputs = setup_inputs


def setup_inputs(seed=0):
    import zlib

    import numpy as np

    out = dict(_drawn_inputs(seed))
    spreads = {'L0_attn_memory_norm': (1.0, 0.2)}
    factors = {'L0_attn_Wk': 7.128, 'L0_attn_Wv': 6.873}
    for name, (base, spread) in spreads.items():
        noise = np.random.default_rng([zlib.crc32(name.encode()), seed]).standard_normal(out[name].shape)
        drawn = base * np.exp(spread * noise) if base else spread * noise
        out[name] = jnp.asarray(drawn.astype(out[name].dtype))
    for name, factor in factors.items():
        out[name] = (out[name] * factor).astype(out[name].dtype)
    return out
```

```python
from contextlib import ExitStack

import concourse.bass as bass
from concourse import mybir

F32 = mybir.dt.float32
BF16 = mybir.dt.bfloat16
I32 = mybir.dt.int32
ALU = mybir.AluOpType
ACT = mybir.ActivationFunctionType
AX = mybir.AxisListType.X

P = 128
BATCH, SEQ, D = 2, 1024, 512
TILES = BATCH * SEQ // P
TPB = SEQ // P
KD = D // P
NQ, NH, DH = 4, 8, 16
KV = NH * DH
GROUPS = BATCH * NH
PARTS = 6
ROWS = PARTS * DH
SHIFT = 3
CHUNK = 512
STEPS = (SEQ // CHUNK) * TPB
EXPERTS, HIDDEN = 8, 1024
KH = HIDDEN // P
SLOT_TILES = 2 * TILES + EXPERTS - 1
EPS = 1e-5
SHIFT_A, SCALE_A, GATE_A, SHIFT_B, SCALE_B, GATE_B = range(6)


def wait(engine, semaphore, value):
    if not isinstance(value, int) or value > 0:
        engine.wait_ge(semaphore, value)


class Chain:

    def __init__(self, engine, semaphore, base=0):
        self.engine, self.semaphore, self.base, self.count = engine, semaphore, base, 0

    def done(self, instruction):
        instruction.then_inc(self.semaphore, 1)
        self.count += 1

    def sync(self):
        self.engine.wait_ge(self.semaphore, self.base + self.count)


class Core:

    def __init__(self, nc, stack):
        self.nc, self.stack = nc, stack
        self.arena = stack.enter_context(nc.sbuf_tensor("arena", [P, ARENA], F32))
        self.psum = stack.enter_context(nc.psum_tensor("psum", [P, 8, 512], F32))

    def sb(self, name, shape, dtype=F32):
        return self.stack.enter_context(self.nc.sbuf_tensor(name, shape, dtype))

    def sem(self, name):
        return self.stack.enter_context(self.nc.semaphore(name))

    def at(self, word, shape, dtype=F32):
        n = 1
        for s in shape:
            n *= s
        words = n if dtype is not BF16 else n // 2
        assert word + words <= ARENA
        view = self.arena[:, word:word + words]
        if dtype is not F32:
            view = view.bitcast(dtype)
        if len(shape) > 1:
            names = "abcd"[:len(shape)]
            view = view.rearrange(f"p ({' '.join(names)}) -> p {' '.join(names)}",
                                  **dict(zip(names[1:], shape[1:])))
        return view


WEIGHT_WORDS = 3 * KD * HIDDEN
ARENA = 2 * WEIGHT_WORDS + 10 * 1024 + 256
AT_Q = 2 * WEIGHT_WORDS - TILES * D
AT_KV = 2 * WEIGHT_WORDS
AT_STAGE = 2 * WEIGHT_WORDS + TILES * 2 * KV


def modulate_and_project(nc, core, m, dram):
    wmod = core.at(0, [6, KD, D])
    wqkv = core.at(6 * KD * D, [KD, D + 2 * KV])
    memn = core.at(6 * KD * D + KD * (D + 2 * KV), [KV + 2])
    h_tok = [core.at(AT_STAGE + 512 * u, [D]) for u in range(2)]
    hT = [core.at(AT_STAGE + 1024 + 512 * u, [KD, P]) for u in range(2)]
    q_min = core.at(AT_STAGE + 2048, [D])
    q_max = core.at(AT_STAGE + 2560, [D])
    elu = core.at(AT_STAGE + 3072, [D])
    eluT = core.at(AT_STAGE + 3584, [NQ, P])
    mem_out = core.at(AT_STAGE + 4096, [D])
    m.gate_mem = core.at(AT_STAGE + 4608, [BATCH, D])
    m.zeros = core.at(AT_STAGE + 5632, [D])
    silu_c = core.at(6 * KD * D + KD * (D + 2 * KV) + 256, [BATCH, KD, P])
    mod_tmp = core.at(6 * KD * D + KD * (D + 2 * KV) + 256 + BATCH * KD * P, [BATCH, D])

    ps_hT = core.psum[:, 0, :]
    ps_q = core.psum[:, 1, :]
    ps_kv = core.psum[:, 2, 0:2 * KV]
    ps_eluT = core.psum[:, 3, :]
    ps_mem = core.psum[:, 4:6, :].rearrange("p b (g n) -> p (b g) n", g=2)
    ps_mod = core.psum[:, 6:8, :]

    c_loaded, mw_loaded, consts_loaded, wqkv_loaded, memn_loaded = (
        core.sem(n) for n in ("c_loaded", "mw_loaded", "consts_loaded", "wqkv_loaded", "memn_loaded"))
    x_loaded = [core.sem(f"x_loaded{b}") for b in range(BATCH)]
    wmod_loaded = [core.sem(f"wmod_loaded{n}") for n in range(6)]
    exp_c, exp_mw, silu_ready, mod_psum, mod_stored, mod_signed = (
        core.sem(n) for n in ("exp_c", "exp_mw", "silu_ready", "mod_psum", "mod_stored", "mod_signed"))
    var_ready, std_ready, h_ready, hT_psum, hT_ready, q_psum, kv_psum, q_stored, kv_stored = (
        core.sem(n) for n in ("var_ready", "std_ready", "h_ready", "hT_psum", "hT_ready", "q_psum",
                              "kv_psum", "q_stored", "kv_stored"))
    min_ready, exp_ready, elu_ready, eluT_psum, eluT_ready, mem_psum, mem_used = (
        core.sem(n) for n in ("min_ready", "exp_ready", "elu_ready", "eluT_psum", "eluT_ready",
                              "mem_psum", "mem_used"))
    dve_own, act_own, zeros_set, slots_zeroed = (
        core.sem(n) for n in ("dve_own_a", "act_own_a", "zeros_set", "slots_zeroed"))
    order = [SCALE_A, SHIFT_A, GATE_A, SCALE_B, SHIFT_B, GATE_B]

    with nc.Block() as block:
        @block.sync
        def _(sp):
            sp.dma_start(m.consts[:, :], dram.consts).then_inc(consts_loaded, 16)
            sp.dma_start(m.c_cols[:, :], dram.c).then_inc(c_loaded, 16)
            sp.dma_start(m.mw[:, 0:1], dram.mw.partition_broadcast(P)).then_inc(mw_loaded, 16)
            xs = dram.x.rearrange("(i p) d -> p i d", p=P)
            wm = dram.wmod.rearrange("(k p) (n d) -> n p k d", p=P, n=6)
            sp.dma_start(m.x[:, 0:TPB, :], xs[:, 0:TPB, :]).then_inc(x_loaded[0], 16)
            for n in order[:2]:
                sp.dma_start(wmod[:, n], wm[n]).then_inc(wmod_loaded[n], 16)
            sp.dma_start(wqkv, dram.wqkv.rearrange("(k p) n -> p k n", p=P)).then_inc(wqkv_loaded, 16)
            for n in order[2:3]:
                sp.dma_start(wmod[:, n], wm[n]).then_inc(wmod_loaded[n], 16)
            sp.dma_start(m.x[:, TPB:TILES, :], xs[:, TPB:TILES, :]).then_inc(x_loaded[1], 16)
            sp.dma_start(memn, dram.memn).then_inc(memn_loaded, 16)
            for n in order[3:]:
                sp.dma_start(wmod[:, n], wm[n]).then_inc(wmod_loaded[n], 16)
            sp.dma_start(m.gate[:, :, :], dram.gate.rearrange("(k p) e -> p k e", p=P)).then_inc(m.gate_loaded, 16)
            sp.wait_ge(zeros_set, 1)
            sp.dma_start(dram.slots_x.rearrange("(r p) d -> p r d", p=P),
                         m.zeros[:, None, :].to_broadcast([P, SLOT_TILES, D])).then_inc(slots_zeroed, 16)
            sp.wait_ge(slots_zeroed, 16)

        @block.gpsimd
        def _(pool):
            nc.gpsimd.memset(m.zeros, 0.0).then_inc(zeros_set, 1)

        @block.scalar
        def _(act):
            act.wait_ge(c_loaded, 16)
            nc.scalar.activation(m.c_exp[:, :], m.c_cols[:, :], ACT.Exp, scale=-1.0).then_inc(exp_c, 1)
            act.wait_ge(mw_loaded, 16)
            nc.scalar.activation(m.mw[:, 1:2], m.mw[:, 0:1], ACT.Exp, scale=-1.0).then_inc(exp_mw, 1)
            act.wait_ge(consts_loaded, 16)
            nc.scalar.copy(m.ident16[:, :], m.ident[:, :]).then_inc(act_own, 1)
            for n, piece in enumerate(order):
                for b in range(BATCH):
                    act.wait_ge(mod_psum, 2 * n + b + 1)
                    one = 1.0 if piece in (SCALE_A, SCALE_B) else 0.0
                    nc.scalar.activation(m.mod[:, b, piece, :], ps_mod[:, b, :], ACT.Copy,
                                         bias=one).then_inc(mod_stored, 1)
            act.wait_ge(var_ready, 1)
            nc.scalar.activation(m.std[:, :], m.var[:, :], ACT.Sqrt).then_inc(std_ready, 1)

            def project_tile(i, u):
                act.wait_ge(hT_psum, i + 1)
                wait(act, kv_psum, i - 1)
                nc.scalar.copy(hT[u], ps_hT.rearrange("p (k s) -> p k s", k=KD)).then_inc(hT_ready, 1)

            def store_tile(i):
                act.wait_ge(q_psum, i + 1)
                nc.scalar.copy(m.q[:, i, :], ps_q).then_inc(q_stored, 1)
                act.wait_ge(kv_psum, i + 1)
                nc.scalar.copy(m.kv[:, i, :], ps_kv).then_inc(kv_stored, 1)

            def elu_exp(i):
                act.wait_ge(min_ready, i + 1)
                nc.scalar.activation(q_min, q_min, ACT.Exp).then_inc(exp_ready, 1)

            def elu_turned(i):
                act.wait_ge(eluT_psum, i + 1)
                wait(act, mem_psum, i)
                nc.scalar.copy(eluT, ps_eluT.rearrange("p (k s) -> p k s", k=NQ)).then_inc(eluT_ready, 1)

            def step(i, u):
                project_tile(i, u)
                elu_exp(i - 1)
                store_tile(i)
                elu_turned(i - 1)

            project_tile(0, 0)
            store_tile(0)
            step(1, 1)
            with act.Fori(1, TILES // 2) as j:
                step(2 * j, 0)
                step(2 * j + 1, 1)
            elu_exp(TILES - 1)
            elu_turned(TILES - 1)

        @block.vector
        def _(dve):
            own = Chain(dve, dve_own)
            dve.wait_ge(exp_c, 1)
            own.done(nc.vector.tensor_scalar(m.c_exp[:, :], m.c_exp[:, :], 1.0, None, ALU.add))
            own.sync()
            own.done(nc.vector.reciprocal(m.c_exp[:, :], m.c_exp[:, :]))
            own.sync()
            own.done(nc.vector.tensor_tensor(m.c_exp[:, :], m.c_exp[:, :], m.c_cols[:, :], ALU.mult))
            own.sync()
            nc.vector.tensor_copy(
                silu_c, m.c_exp[:, :].rearrange("p (k b) -> p b k", b=BATCH)[:, :, :, None]
                .to_broadcast([P, BATCH, KD, P])).then_inc(silu_ready, 1)
            dve.wait_ge(exp_mw, 1)
            own.done(nc.vector.tensor_scalar(m.mw[:, 1:2], m.mw[:, 1:2], 1.0, None, ALU.add))
            own.sync()
            own.done(nc.vector.reciprocal(m.mw[:, 2:3], m.mw[:, 1:2]))
            own.sync()
            own.done(nc.vector.tensor_scalar(m.mw[:, 3:4], m.mw[:, 2:3], -1.0, 1.0, ALU.mult, ALU.add))
            for b in range(BATCH):
                dve.wait_ge(x_loaded[b], 16)
                for i in range(b * TPB, (b + 1) * TPB):
                    own.done(nc.vector.bn_stats(m.stats[:, i, :], m.x[:, i, :]))
            own.sync()
            mean_and_variance(nc, own, m)
            own.sync()
            nc.vector.tensor_scalar(m.var[:, :], m.var[:, :], EPS, None, ALU.add).then_inc(var_ready, 1)
            dve.wait_ge(std_ready, 1)
            own.done(nc.vector.reciprocal(m.rstd[:, :], m.std[:, :]))
            dve.wait_ge(mod_stored, 2 * len(order))
            for gate in (GATE_A, GATE_B):
                g = m.mod[:, :, gate, :]
                own.done(nc.vector.tensor_scalar(mod_tmp, g, 0.0, 2.0, ALU.is_ge, ALU.mult))
                own.sync()
                own.done(nc.vector.tensor_scalar(mod_tmp, mod_tmp, -1.0, None, ALU.add))
                own.done(nc.vector.scalar_tensor_tensor(g, g, -1.0, g, ALU.mult, ALU.max))
                own.sync()
                own.done(nc.vector.scalar_tensor_tensor(g, g, 0.25, mod_tmp, ALU.max, ALU.mult))
                own.sync()
            own.done(nc.vector.tensor_scalar(m.gate_mem[:, :, :], m.mod[:, :, GATE_A, :], m.mw[:, 2:3],
                                             None, ALU.mult))
            own.done(nc.vector.tensor_scalar(m.gate_att[:, :, :], m.mod[:, :, GATE_A, :], m.mw[:, 3:4],
                                             None, ALU.mult))
            own.sync()
            start = own.count

            def normalise(i, u, own):
                wait(dve, hT_psum, i - 1)
                own.done(nc.vector.tensor_scalar(h_tok[u], m.x[:, i, :], m.mean[:, bass.ds(i, 1)],
                                                 m.rstd[:, bass.ds(i, 1)], ALU.subtract, ALU.mult))
                own.sync()
                own.done(nc.vector.tensor_tensor(h_tok[u], h_tok[u], m.mod[:, i // TPB, SCALE_A, :],
                                                 ALU.mult))
                own.sync()
                nc.vector.tensor_tensor(h_tok[u], h_tok[u], m.mod[:, i // TPB, SHIFT_A, :],
                                        ALU.add).then_inc(h_ready, 1)

            def elu_tile(i, own):
                dve.wait_ge(q_stored, i + 1)
                nc.vector.tensor_scalar(q_min, m.q[:, i, :], 0.0, None, ALU.min).then_inc(min_ready, 1)
                own.done(nc.vector.tensor_scalar(q_max, m.q[:, i, :], 0.0, -1.0, ALU.max, ALU.add))
                dve.wait_ge(exp_ready, i + 1)
                wait(dve, eluT_psum, i)
                own.sync()
                nc.vector.tensor_tensor(elu, q_max, q_min, ALU.add).then_inc(elu_ready, 1)

            def add_memory(i, own):
                dve.wait_ge(mem_psum, i + 1)
                own.done(nc.vector.reciprocal(m.mem_den[:, :], ps_mem[:, :, KV]))
                own.sync()
                for g in range(NQ):
                    last = nc.vector.scalar_tensor_tensor(
                        mem_out[:, g * KV:(g + 1) * KV], ps_mem[:, g, 0:KV], m.mem_den[:, g:g + 1],
                        m.gate_mem[:, i // TPB, g * KV:(g + 1) * KV], ALU.mult, ALU.mult)
                last.then_inc(mem_used, 1)
                dve.wait_ge(mem_used, i + 1)
                own.done(nc.vector.tensor_tensor(m.x[:, i, :], m.x[:, i, :], mem_out, ALU.add))
                own.sync()

            def step(i, u, own):
                normalise(i, u, own)
                add_memory(i - 2, own)
                elu_tile(i - 1, own)

            normalise(0, 0, own)
            normalise(1, 1, own)
            elu_tile(0, own)
            own.sync()
            per_step = 5
            with dve.Fori(1, TILES // 2) as j:
                in_loop = Chain(dve, dve_own, own.count + (j - 1) * (2 * per_step))
                step(2 * j, 0, in_loop)
                step(2 * j + 1, 1, in_loop)
                assert in_loop.count == 2 * per_step
            own.count += (TILES - 2) * per_step
            add_memory(TILES - 2, own)
            elu_tile(TILES - 1, own)
            add_memory(TILES - 1, own)

        @block.tensor
        def _(pe):
            pe.wait_ge(silu_ready, 1)
            for n, piece in enumerate(order):
                pe.wait_ge(wmod_loaded[piece], 16)
                for b in range(BATCH):
                    wait(pe, mod_stored, 2 * (n - 1) + b + 1)
                    for k in range(KD):
                        last = nc.tensor.matmul(ps_mod[:, b, :], silu_c[:, b, k, :], wmod[:, piece, k, :],
                                                start=k == 0, stop=k == KD - 1)
                    last.then_inc(mod_psum, 1)
            pe.wait_ge(wqkv_loaded, 16)
            pe.wait_ge(memn_loaded, 16)
            pe.wait_ge(act_own, 1)

            def project(i, u):
                pe.wait_ge(h_ready, i + 1)
                wait(pe, hT_ready, i)
                for k in range(KD):
                    last = nc.tensor.transpose(ps_hT[:, k * P:(k + 1) * P], h_tok[u][:, k * P:(k + 1) * P],
                                               m.ident)
                last.then_inc(hT_psum, 1)
                pe.wait_ge(hT_ready, i + 1)
                wait(pe, q_stored, i)
                for k in range(KD):
                    last = nc.tensor.matmul(ps_q, hT[u][:, k, :], wqkv[:, k, 0:D], start=k == 0, stop=k == KD - 1)
                last.then_inc(q_psum, 1)
                wait(pe, kv_stored, i)
                for k in range(KD):
                    last = nc.tensor.matmul(ps_kv, hT[u][:, k, :], wqkv[:, k, D:], start=k == 0, stop=k == KD - 1)
                last.then_inc(kv_psum, 1)

            def remember(i):
                pe.wait_ge(elu_ready, i + 1)
                wait(pe, eluT_ready, i)
                for g in range(NQ):
                    last = nc.tensor.transpose(ps_eluT[:, g * P:(g + 1) * P], elu[:, g * P:(g + 1) * P], m.ident)
                last.then_inc(eluT_psum, 1)
                pe.wait_ge(eluT_ready, i + 1)
                wait(pe, mem_used, i)
                for g in range(NQ):
                    last = nc.tensor.matmul(ps_mem[:, g, 0:KV + 1], eluT[:, g, :], memn[:, 0:KV + 1],
                                            start=True, stop=True)
                last.then_inc(mem_psum, 1)

            project(0, 0)
            project(1, 1)
            remember(0)
            with pe.Fori(1, TILES // 2) as j:
                for u in range(2):
                    project(2 * j + u, u)
                    remember(2 * j + u - 1)
            remember(TILES - 1)


def mean_and_variance(nc, own, m):
    even, odd = m.stats[:, :, 1], m.stats[:, :, 4]
    own.done(nc.vector.tensor_tensor(m.mean[:, :], even, odd, ALU.add))
    own.done(nc.vector.tensor_tensor(m.var[:, :], even, odd, ALU.subtract))
    own.done(nc.vector.tensor_tensor(m.std[:, :], m.stats[:, :, 2], m.stats[:, :, 5], ALU.add))
    own.sync()
    own.done(nc.vector.tensor_scalar(m.mean[:, :], m.mean[:, :], 0.5, None, ALU.mult))
    own.done(nc.vector.scalar_tensor_tensor(m.var[:, :], m.var[:, :], 0.25, m.var[:, :], ALU.mult, ALU.mult))
    own.sync()
    own.done(nc.vector.scalar_tensor_tensor(m.var[:, :], m.std[:, :], 1.0 / D, m.var[:, :], ALU.mult, ALU.add))


def attention_order(now, ahead, behind):
    if not now and ahead:
        return ([("turn", j) for j in range(NQ + 1)] + [("peak", n) for n in range(48)] + [("shift", 0)]
                + [("peak", n) for n in range(48, 64)])
    if not now:
        return [("out", -1), ("give", -1)]
    events, peaks = [], iter(range(64))

    def peak(n):
        if ahead:
            events.extend(("peak", x) for _, x in zip(range(n), peaks))

    between = {(0, 0): ("turn", 0), (0, 4): ("turn", 1), (1, 4): ("give", -1), (2, 2): ("turn", 2),
               (3, 1): ("turn", 3), (4, 1): ("shift", 1), (5, 1): ("turn", 4), (9, 1): ("give", 0),
               (10, 1): ("shift", 0)}
    peaks_in_step = {0: (0, 0, 0, 0, 0), 1: (0, 1, 1, 1, 1), 3: (1, 1, 1, 1, 1), 4: (1, 1, 1, 1, 1),
                     5: (1, 1, 1, 1, 1), 10: (1, 1, 1, 1, 1), 15: (1, 1, 1, 0, 1)}
    for k in range(STEPS):
        for n in range(NQ + 1):
            if n == NQ and (k or behind):
                events.append(("out", k - 1))
            peak(peaks_in_step.get(k, (1, 1, 1, 1, 0))[n])
            if n < NQ:
                events.append(("score", NQ * k + n))
            event = between.get((k, n))
            if event and {"turn": ahead, "give": behind or event[1] == 0,
                          "shift": ahead or event[1] == 1}[event[0]]:
                events.append(event)
    return events


def attend(nc, core, m, dram):
    qT = core.at(0, [2, NQ, SEQ], BF16)
    kT = core.at(4096, [2, SEQ], BF16)
    q_parts = core.at(5120, [TPB, NQ, ROWS], BF16)
    k_parts = core.at(6656, [TPB, ROWS], BF16)
    rest = core.at(7040, [TPB, NQ, DH])
    rest_k = core.at(7552, [TPB, DH])
    probs = [core.at(8192 + 2048 * u, [NQ, CHUNK]) for u in range(2)]
    values = core.at(12288, [TPB, 32])
    out_T = core.at(12544, [CHUNK])
    peaks = core.at(13056, [64])
    peak = core.at(13120, [16])
    peak_rest = core.at(13136, [16])
    peak_parts = core.at(13152, [4, SHIFT, NQ], BF16)
    shift_T = core.at(13184, [CHUNK], BF16)
    denom = core.at(13440, [4, NQ])
    minus_peak = core.at(13456, [16])
    no_peak = core.at(13472, [16])

    ps_scores = [core.psum[:, u, :] for u in range(3)]
    ps_peak = [core.psum[:, 3 + u, :] for u in range(3)]
    ps_out = core.psum[:, 6, :]
    ps_turn = core.psum[:, 7, :]
    ps_turn16 = ps_turn.bitcast(BF16)

    (ready_to_turn, in_turn_bank, out_of_turn_bank, peak_psum, peak_used, peak_found, shift_ready,
     shift_loaded, score_psum, exp_done, out_done, values_ready, out_stored, given, taken, kT_ones,
     dve_own) = (
        core.sem(n) for n in (
            "ready_to_turn", "in_turn_bank", "out_of_turn_bank", "peak_psum", "peak_used", "peak_found",
            "shift_ready", "shift_loaded", "score_psum", "exp_done", "out_done", "values_ready",
            "out_stored", "given", "taken", "kT_ones", "dve_own_b"))
    FREE = 2
    UNITS = 64

    def turns_before(g):
        return 0 if isinstance(g, int) and g < 0 else 7 * g + 6

    def unit(n):
        return n // 32, n % 32 // 8, n % 8 // 2, n % 2

    def before_in_bank(n):
        return n - 2 if n >= 3 else (0, -2, -1)[n]

    def all_turns(engine, turn):
        turn(-1, False, True, False)
        turn(0, True, True, False)
        with engine.Fori(1, GROUPS - 1) as g:
            turn(g, True, True, True)
        turn(GROUPS - 1, True, False, True)
        turn(GROUPS, False, False, True)

    with nc.Block() as block:
        @block.sync
        def _(sp):
            def load_shift(n, par, c, passed):
                sp.wait_ge(out_of_turn_bank, passed)
                sp.dma_start(qT[ROWS:ROWS + SHIFT, par, :, c * CHUNK:(c + 1) * CHUNK],
                             shift_T[0:SHIFT * NQ, :]).then_inc(shift_loaded, 16)

            def turn(g, *parts):
                passed = turns_before(g)
                for what, n in attention_order(*parts):
                    if what in ("turn", "shift"):
                        passed = passed + 1
                    if what == "shift":
                        load_shift(2 * g + (1 if n else 2), (g if n else g + 1) % 2, n, passed)

            all_turns(sp, turn)
            sp.wait_ge(shift_loaded, 16 * 2 * GROUPS)

        @block.gpsimd
        def _(pool):
            def split(n):
                b, h = n // NH, n % NH
                q = m.q[:, bass.ds(b * TPB, TPB), :].rearrange("p t (g w) -> p t g w", g=NQ)[:, :, :, bass.ds(h * DH, DH)]
                k = m.kv[:, bass.ds(b * TPB, TPB), bass.ds(h * DH, DH)]
                qp = q_parts.rearrange("p t g (j d) -> p t g j d", j=PARTS)
                kp = k_parts.rearrange("p t (j d) -> p t j d", j=PARTS)
                if not isinstance(n, int) or n > 1:
                    pool.wait_ge(in_turn_bank, turns_before(n - 2) + turn_place(True, True, NQ))
                elif n == 1:
                    pool.wait_ge(in_turn_bank, turn_place(False, True, NQ))
                pool.wait_ge(kT_ones, 3)
                nc.gpsimd.tensor_copy(qp[:, :, :, 0, :], q)
                nc.gpsimd.tensor_copy(kp[:, :, 0, :], k)
                pool.drain()
                nc.gpsimd.tensor_tensor(rest, q, qp[:, :, :, 0, :], ALU.subtract)
                nc.gpsimd.tensor_tensor(rest_k, k, kp[:, :, 0, :], ALU.subtract)
                for j in (1, 2):
                    nc.gpsimd.tensor_copy(qp[:, :, :, j, :], qp[:, :, :, 0, :])
                for j in (3, 5):
                    nc.gpsimd.tensor_copy(kp[:, :, j, :], kp[:, :, 0, :])
                pool.drain()
                nc.gpsimd.tensor_copy(qp[:, :, :, 3, :], rest)
                nc.gpsimd.tensor_copy(kp[:, :, 1, :], rest_k)
                pool.drain()
                nc.gpsimd.tensor_tensor(qp[:, :, :, 5, :], rest, qp[:, :, :, 3, :], ALU.subtract)
                nc.gpsimd.tensor_tensor(kp[:, :, 2, :], rest_k, kp[:, :, 1, :], ALU.subtract)
                nc.gpsimd.tensor_copy(kp[:, :, 4, :], kp[:, :, 1, :])
                nc.gpsimd.tensor_copy(qp[:, :, :, 4, :], qp[:, :, :, 3, :])
                pool.drain().then_inc(ready_to_turn, 1)

            def stage_values(n):
                wait(pool, out_done, STEPS * n + FREE if not isinstance(n, int) or n else 0)
                pool.wait_ge(kT_ones, 3)
                b, h = n // NH, n % NH
                nc.gpsimd.tensor_copy(values[:, :, 0:DH],
                                      m.kv[:, bass.ds(b * TPB, TPB), bass.ds(h * DH + KV, DH)]).then_inc(values_ready, 1)

            def find_shift(n, c, passed):
                wait(pool, in_turn_bank, passed)
                pool.wait_ge(peak_found, 2 * n + c + 1)
                part = [peak_parts[:, :, j, :] for j in range(SHIFT)]
                whole, left = (v.rearrange("p (h t) -> p t h", t=4) for v in (minus_peak, peak_rest))
                nc.gpsimd.tensor_tensor(minus_peak, no_peak, peak, ALU.subtract)
                pool.drain()
                nc.gpsimd.tensor_copy(part[0], whole)
                pool.drain()
                nc.gpsimd.tensor_tensor(left, whole, part[0], ALU.subtract)
                pool.drain()
                nc.gpsimd.tensor_copy(part[1], left)
                pool.drain()
                nc.gpsimd.tensor_tensor(part[2], left, part[1], ALU.subtract).then_inc(shift_ready, 1)

            nc.gpsimd.memset(values[:, :, :], 0.0).then_inc(kT_ones, 1)
            pool.wait_ge(kT_ones, 1)
            nc.gpsimd.memset(values[:, :, DH:DH + 1], 1.0).then_inc(kT_ones, 1)
            pool.wait_ge(kT_ones, 2)
            nc.gpsimd.memset(kT[ROWS:ROWS + SHIFT, :, :], 1.0).then_inc(kT_ones, 1)
            pool.wait_ge(kT_ones, 3)
            nc.gpsimd.memset(no_peak, 0.0)
            split(0)
            split(1)
            find_shift(0, 0, 0)

            def turn(g, ahead, prepare):
                find_shift(g, 1, turns_before(g))
                stage_values(g)
                if ahead:
                    find_shift(g + 1, 0, turns_before(g) + turn_place(True, True, "shift1"))
                if prepare:
                    split(g + 2)

            with pool.Fori(0, GROUPS - 2) as g:
                turn(g, True, True)
            turn(GROUPS - 2, True, False)
            turn(GROUPS - 1, False, False)

        @block.tensor
        def _(pe):
            def into_turn_bank(before, g, passed):
                if before == "give":
                    pe.wait_ge(taken, passed)
                elif before == "turn":
                    wait(pe, out_of_turn_bank, passed)

            def turn(g, now, ahead, behind):
                passed = turns_before(g)
                takes = 2 * g - 1 if behind else 0
                before = "turn" if now or ahead else "give"
                for what, n in attention_order(now, ahead, behind):
                    if what == "turn":
                        into_turn_bank(before, g, takes if before == "give" else passed)
                        if n == 0:
                            pe.wait_ge(ready_to_turn, g + 2)
                        for t in range(TPB):
                            source = k_parts[:, t, :] if n == 0 else q_parts[:, t, n - 1, :]
                            last = nc.tensor.transpose(ps_turn16[0:ROWS, t * P:(t + 1) * P], source, m.ident16[:, :])
                        last.then_inc(in_turn_bank, 1)
                        passed, before = passed + 1, "turn"
                    elif what == "shift":
                        into_turn_bank(before, g, takes if before == "give" else passed)
                        pe.wait_ge(shift_ready, 2 * g + (2 if n else 3))
                        for t in range(4):
                            last = nc.tensor.transpose(ps_turn16[0:SHIFT * NQ, t * P:(t + 1) * P],
                                                       peak_parts[:, t].rearrange("p j h -> p (j h)"),
                                                       m.ident16[:, :])
                        last.then_inc(in_turn_bank, 1)
                        passed, before = passed + 1, "turn"
                    elif what == "peak":
                        c, head, tile, keys = unit(n)
                        par = (g + 1) % 2
                        if n % 8 == 0 and n < 32:
                            pe.wait_ge(out_of_turn_bank, turns_before(g) + turn_place(now, ahead, head + 1))
                        wait(pe, peak_used, UNITS * (g + 1) + before_in_bank(n))
                        s = (c * 4 + tile) * P
                        nc.tensor.matmul(ps_peak[n % 3], qT[0:ROWS, par, head, s:s + P],
                                         kT[0:ROWS, par, keys * CHUNK:(keys + 1) * CHUNK],
                                         start=True, stop=True).then_inc(peak_psum, 1)
                    elif what == "score":
                        k, head = n // NQ, n % NQ
                        c, t = k // TPB, k % TPB
                        par = g % 2
                        if n == 0:
                            pe.wait_ge(kT_ones, 3)
                        if n % (NQ * TPB) == 0:
                            pe.wait_ge(shift_loaded, 16 * (2 * g + c + 1))
                        wait(pe, exp_done, UNITS * g + before_in_bank(n))
                        nc.tensor.matmul(
                            ps_scores[n % 3], kT[0:ROWS + SHIFT, par, t * P:(t + 1) * P],
                            qT[0:ROWS + SHIFT, par, head, c * CHUNK:(c + 1) * CHUNK],
                            start=True, stop=True).then_inc(score_psum, 1)
                    elif what == "out":
                        c, t = n // TPB, n % TPB
                        if n == 0:
                            pe.wait_ge(values_ready, g + 1)
                        if t == 0:
                            pe.wait_ge(out_stored, 2 * g + c + 1)
                        pe.wait_ge(exp_done, UNITS * g + NQ * (n + 1))
                        for head in range(NQ):
                            last = nc.tensor.matmul(ps_out[32 * head:32 * head + 32, :], values[:, t, :],
                                                    probs[n % 2][:, head, :], start=t == 0, stop=t == TPB - 1)
                        last.then_inc(out_done, 1)
                    elif what == "give":
                        into_turn_bank(before, g, takes if before == "give" else passed)
                        pe.wait_ge(out_stored, 2 * g + n + 2)
                        for t in range(4):
                            last = nc.tensor.transpose(ps_turn[:, t * P:(t + 1) * P], out_T[:, t * P:(t + 1) * P],
                                                       m.ident)
                        last.then_inc(given, 1)
                        takes, before = takes + 1, "give"

            pe.sem_inc(out_done, FREE)
            all_turns(pe, turn)

        @block.scalar
        def _(act):
            def turn(g, *parts):
                passed = turns_before(g)
                par = (g + 1) % 2
                for what, n in attention_order(*parts):
                    if what == "turn":
                        if n >= 2:
                            act.wait_ge(in_turn_bank, passed + 1)
                            nc.scalar.copy(qT[0:ROWS, par, n - 1, :], ps_turn16[0:ROWS, :]).then_inc(out_of_turn_bank, 1)
                        passed = passed + 1
                    elif what == "shift":
                        act.wait_ge(in_turn_bank, passed + 1)
                        wait(act, shift_loaded, 16 * (2 * g + (1 if n else 2)))
                        nc.scalar.copy(shift_T[0:SHIFT * NQ, :], ps_turn16[0:SHIFT * NQ, 0:CHUNK]).then_inc(out_of_turn_bank, 1)
                        passed = passed + 1
                    elif what == "score":
                        k, head = n // NQ, n % NQ
                        act.wait_ge(score_psum, UNITS * g + n + 1)
                        if head == 0:
                            act.wait_ge(out_done, STEPS * g + k - 1 + FREE)
                        nc.scalar.activation(probs[k % 2][:, head, :], ps_scores[n % 3],
                                             ACT.Exp, scale=DH ** -0.5).then_inc(exp_done, 1)
                    elif what == "out" and n in (TPB - 1, -1):
                        act.wait_ge(out_done, STEPS * g + n + 1 + FREE)
                        wait(act, given, 2 * g + n // TPB)
                        nc.scalar.copy(out_T, ps_out).then_inc(out_stored, 1)

            act.sem_inc(out_stored, 1)
            all_turns(act, turn)

        @block.vector
        def _(dve):
            def turn(g, *parts):
                own = Chain(dve, dve_own, 2 * g - 1 if parts[2] else 0)
                passed = turns_before(g)
                par = (g + 1) % 2
                for what, n in attention_order(*parts):
                    if what == "turn" and n < 2:
                        dve.wait_ge(in_turn_bank, passed + 1)
                        target = kT[0:ROWS, par, :] if n == 0 else qT[0:ROWS, par, 0, :]
                        nc.vector.tensor_copy(target, ps_turn16[0:ROWS, :]).then_inc(out_of_turn_bank, 1)
                    if what in ("turn", "shift"):
                        passed = passed + 1
                    if what == "peak":
                        dve.wait_ge(peak_psum, UNITS * (g + 1) + n + 1)
                        nc.vector.reduce_max(peaks[:, n:n + 1], ps_peak[n % 3], AX).then_inc(peak_used, 1)
                        if n % 32 == 31:
                            c = n // 32
                            dve.wait_ge(peak_used, UNITS * (g + 1) + n + 1)
                            wait(dve, shift_ready, 2 * (g + 1) + c)
                            pairs = peaks[:, 32 * c:32 * c + 32].rearrange("p (n k) -> p n k", k=2)
                            nc.vector.tensor_reduce(peak, pairs, AX, ALU.max).then_inc(peak_found, 1)
                    elif what == "give":
                        dve.wait_ge(given, 2 * g + n + 1)
                        o = ps_turn.rearrange("p (t h w) -> p t h w", t=4, h=NQ)
                        own.done(nc.vector.reciprocal(denom, o[:, :, :, DH]))
                        own.sync()
                        of, c = (g, 0) if n == 0 else (g - 1, 1)
                        b, h = of // NH, of % NH
                        target = m.q[:, bass.ds(b * TPB + 4 * c, 4), :].rearrange(
                            "p t (h w) -> p t h w", h=NQ)[:, :, :, bass.ds(h * DH, DH)]
                        nc.vector.tensor_tensor(target, o[:, :, :, 0:DH],
                                                denom[:, :, :, None].to_broadcast([P, 4, NQ, DH]),
                                                ALU.mult).then_inc(taken, 1)

            all_turns(dve, turn)


def turn_place(now, ahead, what):
    count = 0
    for name, n in attention_order(now, ahead, False):
        if name in ("turn", "shift"):
            count += 1
            if (name, n) == ("turn", what) or (name == "shift" and what == f"shift{n}"):
                return count
    raise ValueError(what)


def route(nc, core, m, dram):
    h_tok = [core.at(AT_STAGE + 512 * u, [D]) for u in range(2)]
    hT = core.at(AT_STAGE + 1024, [KD, P])
    ps_hT = core.psum[:, 0, :]
    ps_logits = core.psum[:, 1, 0:EXPERTS]
    ps_rank = core.psum[:, 2, 0:(TILES + 1) * EXPERTS].rearrange("p (i e) -> p i e", e=EXPERTS)
    R = [P, TILES, EXPERTS]
    lg, pick1, pick2, masked, base = (core.at(AT_STAGE + 2048 + 128 * n, [TILES, EXPERTS]) for n in range(5))
    chosen = core.at(AT_STAGE + 2688, [TILES + 1, EXPERTS])
    top1, top2, slot_f, expo = (core.at(AT_STAGE + 2848 + 16 * n, [TILES]) for n in range(4))
    over = core.at(AT_STAGE + 2912, [EXPERTS, 16])
    lower = core.at(AT_STAGE + 3040, [EXPERTS, EXPERTS])
    counts, starts_f = (core.at(AT_STAGE + 3104 + 8 * n, [EXPERTS]) for n in range(2))
    tile_ge = core.at(AT_STAGE + 3120, [SLOT_TILES, EXPERTS - 1])
    tile_f = core.at(AT_STAGE + 3120 + SLOT_TILES * 7, [SLOT_TILES])

    (gated, var_ready, std_ready, h_ready, h_kept, hT_psum, hT_ready, logit_psum, logit_used, diff_ready,
     exp_ready, chosen_ready, ranked, scattered, dve_own) = (
        core.sem(n) for n in ("gated", "var_ready_b", "std_ready_b", "h_ready_b", "h_kept", "hT_psum_b",
                              "hT_ready_b", "logit_psum", "logit_used", "diff_ready", "exp_ready_b",
                              "chosen_ready", "ranked", "scattered", "dve_own_c"))

    with nc.Block() as block:
        @block.gpsimd
        def _(pool):
            with pool.Fori(0, TILES) as i:
                nc.gpsimd.tensor_tensor(m.q[:, i, :], m.q[:, i, :], m.gate_att[:, i // TPB, :],
                                        ALU.mult).then_inc(gated, 1)
            with pool.Fori(0, TILES // 2) as j:
                for u in range(2):
                    pool.wait_ge(h_ready, 2 * j + u + 1)
                    pool.wait_ge(gated, TILES)
                    nc.gpsimd.tensor_copy(m.q[:, 2 * j + u, :], h_tok[u]).then_inc(h_kept, 1)
            pool.wait_ge(h_kept, TILES)
            pool.wait_ge(m.slots_ready, 1)
            for i in range(TILES):
                for j in range(2):
                    nc.gpsimd.indirect_dma_start(
                        out=dram.slots_x,
                        out_offset=bass.IndirectOffsetOnAxis(ap=m.slots[:, j, i:i + 1], axis=0),
                        in_=m.q[:, i, :], in_offset=None).then_inc(scattered, 16)
            pool.wait_ge(scattered, 16 * 2 * TILES)

        @block.vector
        def _(dve):
            with dve.Fori(0, TILES) as i:
                dve.wait_ge(gated, i + 1)
                own = Chain(dve, dve_own, 2 * i)
                own.done(nc.vector.tensor_tensor(m.x[:, i, :], m.x[:, i, :], m.q[:, i, :], ALU.add))
                own.sync()
                own.done(nc.vector.bn_stats(m.stats[:, i, :], m.x[:, i, :]))
            own = Chain(dve, dve_own, 0)
            own.count = 2 * TILES
            own.sync()
            mean_and_variance(nc, own, m)
            own.sync()
            nc.vector.tensor_scalar(m.var[:, :], m.var[:, :], EPS, None, ALU.add).then_inc(var_ready, 1)
            dve.wait_ge(std_ready, 1)
            own.done(nc.vector.reciprocal(m.rstd[:, :], m.std[:, :]))
            own.sync()

            def normalise(i, u, own, first):
                if not first:
                    dve.wait_ge(hT_psum, i - 1)
                    dve.wait_ge(h_kept, i - 1)
                own.done(nc.vector.tensor_scalar(h_tok[u], m.x[:, i, :], m.mean[:, bass.ds(i, 1)],
                                                 m.rstd[:, bass.ds(i, 1)], ALU.subtract, ALU.mult))
                own.sync()
                own.done(nc.vector.tensor_tensor(h_tok[u], h_tok[u], m.mod[:, i // TPB, SCALE_B, :], ALU.mult))
                own.sync()
                nc.vector.tensor_tensor(h_tok[u], h_tok[u], m.mod[:, i // TPB, SHIFT_B, :],
                                        ALU.add).then_inc(h_ready, 1)

            def keep_logits(i):
                dve.wait_ge(logit_psum, i + 1)
                nc.vector.tensor_copy(lg[:, i, :], ps_logits).then_inc(logit_used, 1)

            normalise(0, 0, own, True)
            normalise(1, 1, own, True)
            keep_logits(0)
            with dve.Fori(1, TILES // 2) as j:
                loop = Chain(dve, dve_own, own.count + (j - 1) * 4)
                for u in range(2):
                    normalise(2 * j + u, u, loop, False)
                    keep_logits(2 * j + u - 1)
            own.count += 4 * (TILES // 2 - 1)
            keep_logits(TILES - 1)
            dve.wait_ge(logit_used, TILES)

            def pick(source, best, one_hot):
                own.done(nc.vector.tensor_reduce(best, source, AX, ALU.max))
                own.sync()
                own.done(nc.vector.tensor_tensor(one_hot, source, best[:, :, None].to_broadcast(R), ALU.is_equal))
                own.sync()
                own.done(nc.vector.tensor_tensor(one_hot, one_hot, m.falling[:, None, :].to_broadcast(R), ALU.mult))
                own.sync()
                own.done(nc.vector.tensor_reduce(slot_f, one_hot, AX, ALU.max))
                own.sync()
                own.done(nc.vector.tensor_tensor(one_hot, one_hot, slot_f[:, :, None].to_broadcast(R), ALU.is_equal))
                own.sync()

            pick(lg, top1, pick1)
            own.done(nc.vector.scalar_tensor_tensor(masked, pick1, -3e38, lg, ALU.mult, ALU.add))
            own.sync()
            pick(masked, top2, pick2)
            nc.vector.tensor_tensor(expo, top2, top1, ALU.subtract).then_inc(diff_ready, 1)
            own.done(nc.vector.memset(chosen[:, TILES, :], 0.0))
            nc.vector.tensor_tensor(chosen[:, 0:TILES, :], pick1, pick2, ALU.add).then_inc(chosen_ready, 1)
            dve.wait_ge(exp_ready, 1)
            own.done(nc.vector.tensor_scalar(top1, expo, 1.0, None, ALU.add))
            own.sync()
            own.done(nc.vector.reciprocal(m.choice[:, 0, :], top1))
            own.sync()
            own.done(nc.vector.tensor_tensor(m.choice[:, 1, :], m.choice[:, 0, :], expo, ALU.mult))
            dve.wait_ge(ranked, 1)
            own.done(nc.vector.tensor_copy(counts, ps_rank[:, TILES, :]))
            own.sync()
            own.done(nc.vector.tensor_tensor(over, counts[:, :, None].to_broadcast([P, EXPERTS, 16]),
                                             m.steps_of_128[:, None, :].to_broadcast([P, EXPERTS, 16]), ALU.is_gt))
            own.sync()
            own.done(nc.vector.tensor_reduce(counts, over, AX, ALU.add))
            own.sync()
            own.done(nc.vector.tensor_tensor(lower, counts[:, None, :].to_broadcast([P, EXPERTS, EXPERTS]),
                                             m.below, ALU.mult))
            own.sync()
            own.done(nc.vector.tensor_reduce(starts_f, lower, AX, ALU.add))
            own.sync()
            own.done(nc.vector.tensor_copy(m.starts[:, :], starts_f))
            own.done(nc.vector.tensor_tensor(
                tile_ge, m.tile_ids[:, :, None].to_broadcast([P, SLOT_TILES, EXPERTS - 1]),
                starts_f[:, None, 1:EXPERTS].to_broadcast([P, SLOT_TILES, EXPERTS - 1]), ALU.is_ge))
            own.sync()
            own.done(nc.vector.tensor_reduce(tile_f, tile_ge, AX, ALU.add))
            own.sync()
            own.done(nc.vector.tensor_copy(m.tile_expert[:, :], tile_f))
            own.done(nc.vector.tensor_scalar(starts_f, starts_f, float(P), None, ALU.mult))
            own.sync()
            own.done(nc.vector.tensor_tensor(base, ps_rank[:, 0:TILES, :], starts_f[:, None, :].to_broadcast(R), ALU.add))
            own.sync()
            for j, one_hot in enumerate((pick1, pick2)):
                own.done(nc.vector.tensor_tensor(masked, one_hot, base, ALU.mult))
                own.sync()
                own.done(nc.vector.tensor_reduce(slot_f, masked, AX, ALU.add))
                own.sync()
                own.done(nc.vector.tensor_copy(m.slots[:, j, :], slot_f))
            own.sync()
            dve.sem_inc(m.slots_ready, 1)

        @block.scalar
        def _(act):
            act.wait_ge(var_ready, 1)
            nc.scalar.activation(m.std[:, :], m.var[:, :], ACT.Sqrt).then_inc(std_ready, 1)

            def turned(i):
                act.wait_ge(hT_psum, i + 1)
                wait(act, logit_psum, i)
                nc.scalar.copy(hT, ps_hT.rearrange("p (k s) -> p k s", k=KD)).then_inc(hT_ready, 1)

            turned(0)
            with act.Fori(1, TILES) as i:
                turned(i)
            act.wait_ge(diff_ready, 1)
            nc.scalar.activation(expo, expo, ACT.Exp).then_inc(exp_ready, 1)

        @block.tensor
        def _(pe):
            pe.wait_ge(m.gate_loaded, 16)

            def logits(i, u):
                pe.wait_ge(h_ready, i + 1)
                wait(pe, hT_ready, i)
                for k in range(KD):
                    last = nc.tensor.transpose(ps_hT[:, k * P:(k + 1) * P], h_tok[u][:, k * P:(k + 1) * P], m.ident)
                last.then_inc(hT_psum, 1)
                pe.wait_ge(hT_ready, i + 1)
                wait(pe, logit_used, i)
                for k in range(KD):
                    last = nc.tensor.matmul(ps_logits, hT[:, k, :], m.gate[:, k, :], start=k == 0, stop=k == KD - 1)
                last.then_inc(logit_psum, 1)

            logits(0, 0)
            logits(1, 1)
            with pe.Fori(1, TILES // 2) as j:
                for u in range(2):
                    logits(2 * j + u, u)
            pe.wait_ge(chosen_ready, 1)
            nc.tensor.matmul(ps_rank[:, 0:TILES, :], m.before, chosen[:, 0:TILES, :], start=True, stop=False,
                             skip_group_check=True)
            for i in range(TILES):
                last = nc.tensor.matmul(ps_rank[:, i + 1:TILES + 1, :], m.ones[:, :],
                                        chosen[:, i:i + 1, :].to_broadcast([P, TILES - i, EXPERTS]),
                                        start=False, stop=i == TILES - 1, skip_group_check=True)
            last.then_inc(ranked, 1)


def experts(nc, core, m, dram):
    w_in = core.at(0, [2, WEIGHT_WORDS])
    at = 2 * WEIGHT_WORDS
    x_rows = [core.at(at + 512 * u, [D]) for u in range(2)]
    xT = [core.at(at + 1024 + 512 * u, [KD, P]) for u in range(2)]
    silu = [core.at(at + 2048 + 512 * c, [CHUNK]) for c in range(2)]
    hidden = [core.at(at + 3072 + 512 * c, [CHUNK]) for c in range(2)]
    hiddenT = [core.at(at + 4096 + 512 * c, [4, P]) for c in range(2)]
    y_rows = [core.at(at + 5120 + 512 * u, [D]) for u in range(2)]

    ps_gate = [core.psum[:, 2 * c, :] for c in range(2)]
    ps_up = [core.psum[:, 2 * c + 1, :] for c in range(2)]
    ps_xT = core.psum[:, 4, :]
    ps_hT = [core.psum[:, 5 + c, :] for c in range(2)]
    ps_y = core.psum[:, 7, :]

    x_loaded = [core.sem(f"x_rows_loaded{u}") for u in range(2)]
    w_dma = [core.sem(f"w_dma{u}") for u in range(2)]
    y_out = [core.sem(f"y_out{u}") for u in range(2)]
    (weights_ready, xT_psum, xT_ready, gate_psum, up_psum, silu_ready, hidden_ready, hT_psum, hT_ready,
     y_psum, y_ready) = (
        core.sem(n) for n in ("weights_ready", "xT_psum", "xT_ready", "gate_psum", "up_psum", "silu_ready_m",
                              "hidden_ready", "hidT_psum", "hidT_ready", "y_psum", "y_ready"))
    slots_x = dram.slots_x.rearrange("(r p) d -> r p d", p=P)
    slots_y = dram.slots_y.rearrange("(r p) d -> r p d", p=P)
    PAIRS = SLOT_TILES // 2

    with nc.Block() as block:
        @block.sync
        def _(sp):
            def load(e):
                buffer, words = w_in[:, e % 2], KD * HIDDEN
                for n, (source, k) in enumerate(((dram.w0[e], KD), (dram.w1[e], KD), (dram.wo[e], KH))):
                    sp.dma_start(buffer[:, n * words:(n + 1) * words].rearrange("p (k n) -> p k n", k=k),
                                 source.rearrange("(k p) n -> p k n", p=P)).then_inc(w_dma[e % 2], 16)

            def announce(e):
                sp.wait_ge(w_dma[e % 2], 48 * (e // 2 + 1))
                sp.sem_inc(weights_ready, 1)

            load(0)
            load(1)
            announce(0)
            announce(1)
            for e in range(2, EXPERTS):
                tiles = sp.value_load(m.starts[0:1, e - 1:e], min_val=0, max_val=SLOT_TILES)
                sp.wait_ge(y_psum, tiles + 1)
                load(e)
                announce(e)

        @block.gpsimd
        def _(pool):
            def load(r, u):
                wait(pool, xT_psum, r - 1)
                pool.dma_start(x_rows[u], slots_x[r]).then_inc(x_loaded[u], 16)

            load(0, 0)
            load(1, 1)
            with pool.Fori(1, PAIRS) as j:
                for u in range(2):
                    load(2 * j + u, u)
            load(SLOT_TILES - 1, 0)

        @block.tensor
        def _(pe):
            def turn_rows(r, u, j):
                pe.wait_ge(x_loaded[u], 16 * (j + 1))
                wait(pe, xT_ready, r)
                for k in range(KD):
                    last = nc.tensor.transpose(ps_xT[:, k * P:(k + 1) * P], x_rows[u][:, k * P:(k + 1) * P], m.ident)
                last.then_inc(xT_psum, 1)

            def weights_of(r):
                e = pe.value_load(m.tile_expert[0:1, bass.ds(r, 1)], min_val=0, max_val=EXPERTS - 1)
                pe.wait_ge(weights_ready, e + 1)
                return e % 2

            def widen(r, u, c, buffer):
                words = KD * HIDDEN
                wait(pe, hidden_ready, 2 * r - 1 + c)
                for ps, n, psum_sem in ((ps_gate[c], 0, gate_psum), (ps_up[c], 1, up_psum)):
                    for k in range(KD):
                        at = n * words + k * HIDDEN + c * CHUNK
                        last = nc.tensor.matmul(ps, xT[u][:, k, :], w_in[:, buffer, at:at + CHUNK],
                                                start=k == 0, stop=k == KD - 1)
                    last.then_inc(psum_sem, 1)

            def turn_hidden(r, c):
                pe.wait_ge(hidden_ready, 2 * r + c + 1)
                wait(pe, hT_ready, 2 * r - 1 + c)
                for k in range(4):
                    last = nc.tensor.transpose(ps_hT[c][:, k * P:(k + 1) * P], hidden[c][:, k * P:(k + 1) * P], m.ident)
                last.then_inc(hT_psum, 1)

            def narrow(r, buffer):
                wait(pe, y_ready, r)
                for k in range(KH):
                    if k % 4 == 0:
                        pe.wait_ge(hT_ready, 2 * r + k // 4 + 1)
                    at = 2 * KD * HIDDEN + k * D
                    last = nc.tensor.matmul(ps_y, hiddenT[k // 4][:, k % 4, :], w_in[:, buffer, at:at + D],
                                            start=k == 0, stop=k == KH - 1)
                last.then_inc(y_psum, 1)

            def step(r, u, j, more):
                turn_hidden(r - 1, 0)
                now = weights_of(r)
                pe.wait_ge(xT_ready, r + 1)
                widen(r, u, 0, now)
                turn_hidden(r - 1, 1)
                widen(r, u, 1, now)
                if more:
                    turn_rows(r + 1, 1 - u, j + u)
                narrow(r - 1, weights_of(r - 1))

            pe.sem_inc(y_psum, 1)
            turn_rows(0, 0, 0)
            first = weights_of(0)
            pe.wait_ge(xT_ready, 1)
            widen(0, 0, 0, first)
            widen(0, 0, 1, first)
            turn_rows(1, 1, 0)
            step(1, 1, 0, True)
            with pe.Fori(1, PAIRS) as j:
                step(2 * j, 0, j, True)
                step(2 * j + 1, 1, j, True)
            step(SLOT_TILES - 1, 0, PAIRS, False)
            turn_hidden(SLOT_TILES - 1, 0)
            turn_hidden(SLOT_TILES - 1, 1)
            narrow(SLOT_TILES - 1, weights_of(SLOT_TILES - 1))

        @block.scalar
        def _(act):
            def turned_rows(r, u):
                act.wait_ge(xT_psum, r + 1)
                wait(act, up_psum, 2 * (r - 1))
                nc.scalar.copy(xT[u], ps_xT.rearrange("p (k s) -> p k s", k=KD)).then_inc(xT_ready, 1)

            def gate(r, c):
                act.wait_ge(gate_psum, 2 * r + c + 1)
                wait(act, hidden_ready, 2 * r - 1 + c)
                nc.scalar.activation(silu[c], ps_gate[c], ACT.Silu).then_inc(silu_ready, 1)

            def turned_hidden(r, c):
                act.wait_ge(hT_psum, 2 * r + c + 1)
                wait(act, y_psum, r + 1)
                nc.scalar.copy(hiddenT[c], ps_hT[c].rearrange("p (k s) -> p k s", k=4)).then_inc(hT_ready, 1)

            def store(r, u, j, first):
                act.wait_ge(y_psum, r + 2)
                if not first:
                    act.wait_ge(y_out[u], 16 * j)
                nc.scalar.copy(y_rows[u], ps_y).then_inc(y_ready, 1)
                act.wait_ge(y_ready, r + 1)
                act.dma_start(slots_y[r], y_rows[u]).then_inc(y_out[u], 16)

            def step(r, u, j, more, first=False):
                turned_hidden(r - 1, 0)
                gate(r, 0)
                turned_hidden(r - 1, 1)
                gate(r, 1)
                if more:
                    turned_rows(r + 1, 1 - u)
                store(r - 1, 1 - u, j, first)

            turned_rows(0, 0)
            gate(0, 0)
            gate(0, 1)
            turned_rows(1, 1)
            step(1, 1, 0, True, True)
            step(2, 0, 0, True, True)
            step(3, 1, 1, True)
            with act.Fori(2, PAIRS) as j:
                step(2 * j, 0, j - 1, True)
                step(2 * j + 1, 1, j, True)
            step(SLOT_TILES - 1, 0, PAIRS - 1, False)
            turned_hidden(SLOT_TILES - 1, 0)
            turned_hidden(SLOT_TILES - 1, 1)
            store(SLOT_TILES - 1, 0, PAIRS, False)
            act.wait_ge(y_out[0], 16 * (PAIRS + 1))
            act.wait_ge(y_out[1], 16 * PAIRS)

        @block.vector
        def _(dve):
            def tile(r, first):
                for c in range(2):
                    dve.wait_ge(silu_ready, 2 * r + c + 1)
                    dve.wait_ge(up_psum, 2 * r + c + 1)
                    if not first:
                        dve.wait_ge(hT_psum, 2 * r - 1 + c)
                    nc.vector.tensor_tensor(hidden[c], silu[c], ps_up[c], ALU.mult).then_inc(hidden_ready, 1)

            tile(0, True)
            with dve.Fori(1, SLOT_TILES) as r:
                tile(r, False)


def combine(nc, core, m, dram):
    RING = 4
    rows = core.at(0, [RING, 2, D])
    result = core.at(RING * 2 * D, [RING, D])
    gathered = [core.sem(f"gathered{n}") for n in range(RING)]
    scaled, combined, stored, dve_own = (core.sem(n) for n in ("scaled", "combined", "stored", "dve_own_d"))
    out = dram.out.rearrange("(i p) d -> p i d", p=P)

    with nc.Block() as block:
        @block.gpsimd
        def _(pool):
            for i in range(TILES):
                wait(pool, combined, i - RING + 1)
                for j in range(2):
                    nc.gpsimd.indirect_dma_start(
                        out=rows[:, i % RING, j, :], out_offset=None, in_=dram.slots_y,
                        in_offset=bass.IndirectOffsetOnAxis(ap=m.slots[:, j, i:i + 1], axis=0)
                    ).then_inc(gathered[i % RING], 16)

        @block.scalar
        def _(act):
            for i in range(TILES):
                act.wait_ge(gathered[i % RING], 32 * (i // RING + 1))
                row = rows[:, i % RING, 0, :]
                nc.scalar.activation(row, row, ACT.Copy, scale=m.choice[:, 0, i:i + 1]).then_inc(scaled, 1)

        @block.vector
        def _(dve):
            for i in range(TILES):
                own = Chain(dve, dve_own, 2 * i)
                first, second = rows[:, i % RING, 0, :], rows[:, i % RING, 1, :]
                dve.wait_ge(scaled, i + 1)
                own.done(nc.vector.scalar_tensor_tensor(first, second, m.choice[:, 1, i:i + 1], first,
                                                        ALU.mult, ALU.add))
                own.sync()
                own.done(nc.vector.tensor_tensor(first, first, m.mod[:, i // TPB, GATE_B, :], ALU.mult))
                own.sync()
                nc.vector.tensor_tensor(m.x[:, i, :], m.x[:, i, :], first, ALU.add).then_inc(combined, 1)

        @block.sync
        def _(sp):
            for i in range(TILES):
                sp.wait_ge(combined, i + 1)
                sp.dma_start(out[:, i, :], m.x[:, i, :]).then_inc(stored, 16)
            sp.wait_ge(stored, 16 * TILES)


class Names:
    pass


def constants():
    import numpy as np
    cols = [np.eye(P), np.triu(np.ones((P, P)), 1), np.ones((P, P)),
            np.tile(np.arange(EXPERTS, 0, -1), (P, 1)), np.tile(P * np.arange(16), (P, 1)),
            np.tile(np.tril(np.ones((EXPERTS, EXPERTS)), -1).ravel(), (P, 1)),
            np.tile(np.arange(SLOT_TILES), (P, 1))]
    return np.concatenate(cols, 1).astype(np.float32)


def build(nc, dram):
    with ExitStack() as stack:
        core, m = Core(nc, stack), Names()
        width = 3 * P + EXPERTS + 16 + EXPERTS * EXPERTS + SLOT_TILES
        m.consts = core.sb("consts", [P, width])
        m.ident, m.before, m.ones = (m.consts[:, n * P:(n + 1) * P] for n in range(3))
        at = 3 * P
        m.falling = m.consts[:, at:at + EXPERTS]
        m.steps_of_128 = m.consts[:, at + 8:at + 24]
        m.below = m.consts[:, at + 24:at + 88].rearrange("p (a b) -> p a b", b=EXPERTS)
        m.tile_ids = m.consts[:, at + 88:at + 88 + SLOT_TILES]
        m.ident16 = core.sb("ident16", [P, P], BF16)
        m.x = core.sb("x_tokens", [P, TILES, D])
        m.mod = core.sb("mod", [P, BATCH, 6, D])
        m.gate_att = core.sb("gate_att", [P, BATCH, D])
        m.gate = core.sb("gate", [P, KD, EXPERTS])
        m.c_cols = core.sb("c_cols", [P, KD * BATCH])
        m.c_exp = core.sb("c_exp", [P, KD * BATCH])
        m.mw = core.sb("mw", [P, 4])
        m.mem_den = core.sb("mem_den", [P, NQ])
        m.stats = core.sb("stats", [P, TILES, 6])
        m.mean, m.var, m.std, m.rstd = (core.sb(n, [P, TILES]) for n in ("mean", "var", "std", "rstd"))
        m.choice = core.sb("choice", [P, 2, TILES])
        m.slots = core.sb("slots", [P, 2, TILES], I32)
        m.starts = core.sb("starts", [P, EXPERTS], I32)
        m.tile_expert = core.sb("tile_expert", [P, SLOT_TILES], I32)
        m.gate_loaded, m.slots_ready = core.sem("gate_loaded"), core.sem("slots_ready")
        m.q = core.at(AT_Q, [TILES, D])
        m.kv = core.at(AT_KV, [TILES, 2 * KV])
        modulate_and_project(nc, core, m, dram)
        attend(nc, core, m, dram)
        route(nc, core, m, dram)
        experts(nc, core, m, dram)
        combine(nc, core, m, dram)


def kernel(**inputs):
    import numpy as np
    from concourse import bacc
    from concourse.bass_utils import run_bass_kernel_spmd

    a = {k[3:]: np.asarray(v) for k, v in inputs.items()}
    c = a["c"].T.reshape(KD, P, BATCH).transpose(1, 0, 2).reshape(P, KD * BATCH)
    memn = np.concatenate([a["attn_memory"], a["attn_memory_norm"], a["attn_memory_norm"]], 1)
    arrays = {
        "x": a["attn_x"].reshape(BATCH * SEQ, D),
        "wqkv": np.concatenate([a["attn_Wq"].T, a["attn_Wk"].T, a["attn_Wv"].T], 1),
        "memn": memn, "mw": a["attn_memory_weight"], "gate": a["ffn_gate_w"],
        "w0": a["ffn_w0"], "w1": a["ffn_w1"], "wo": a["ffn_wo"], "c": c, "wmod": a["wmod"],
        "consts": constants(),
    }
    arrays = {k: np.ascontiguousarray(v) for k, v in arrays.items()}
    nc = bacc.Bacc("TRN2", target_bir_lowering=False, num_devices=1)
    dram = Names()
    for name, v in arrays.items():
        dram.__dict__[name] = nc.dram_tensor("in_" + name, v.shape, F32, kind="ExternalInput").ap()
    dram.slots_x = nc.dram_tensor("slots_x", (SLOT_TILES * P, D), F32, kind="Internal").ap()
    dram.slots_y = nc.dram_tensor("slots_y", (SLOT_TILES * P, D), F32, kind="Internal").ap()
    dram.out = nc.dram_tensor("out", (BATCH * SEQ, D), F32, kind="ExternalOutput").ap()
    build(nc, dram)
    result = run_bass_kernel_spmd(nc, [{"in_" + k: v for k, v in arrays.items()}], core_ids=[0])
    return result.results[0]["out"].reshape(BATCH, SEQ, D)
```

```python
from contextlib import ExitStack

import concourse.bass as bass
from concourse import mybir

F32 = mybir.dt.float32
BF16 = mybir.dt.bfloat16
F32R = mybir.dt.float32r
I32 = mybir.dt.int32
ALU = mybir.AluOpType
ACT = mybir.ActivationFunctionType
AX = mybir.AxisListType.X

P = 128
BATCH, SEQ, D = 2, 1024, 512
TILES = BATCH * SEQ // P
TPB = SEQ // P
KD = D // P
NQ, NH, DH = 4, 8, 16
KV = NH * DH
GROUPS = BATCH * NH
PARTS = 6
ROWS = PARTS * DH
SHIFT = 3
CHUNK = 512
STEPS = (SEQ // CHUNK) * TPB
EXPERTS, HIDDEN = 8, 1024
KH = HIDDEN // P
SLOT_TILES = 2 * TILES + EXPERTS - 1
EPS = 1e-5
SHIFT_A, SCALE_A, GATE_A, SHIFT_B, SCALE_B, GATE_B = range(6)


def wait(engine, semaphore, value):
    if not isinstance(value, int) or value > 0:
        engine.wait_ge(semaphore, value)


class Chain:

    def __init__(self, engine, semaphore, base=0):
        self.engine, self.semaphore, self.base, self.count = engine, semaphore, base, 0

    def done(self, instruction):
        instruction.then_inc(self.semaphore, 1)
        self.count += 1

    def sync(self):
        self.engine.wait_ge(self.semaphore, self.base + self.count)


class Core:

    def __init__(self, nc, stack):
        self.nc, self.stack = nc, stack
        self.psum = stack.enter_context(nc.psum_tensor("psum", [P, 8, 512], F32))

    def sb(self, name, shape, dtype=F32):
        return self.stack.enter_context(self.nc.sbuf_tensor(name, shape, dtype))

    def place_arena(self):
        self.base = -(-self.nc.sbuf_base // 64) * 64
        self.arena = self.place("arena", 0, [ARENA])

    def place(self, name, word, shape, dtype=F32):
        return self.nc.alloc_sbuf_tensor_at(name, [P] + shape, dtype, offset=self.base + 4 * word)

    def sem(self, name):
        return self.stack.enter_context(self.nc.semaphore(name))

    def at(self, word, shape, dtype=F32):
        n = 1
        for s in shape:
            n *= s
        words = n if dtype is not BF16 else n // 2
        assert word + words <= ARENA
        view = self.arena[:, word:word + words]
        if dtype is not F32:
            view = view.bitcast(dtype)
        if len(shape) > 1:
            names = "abcd"[:len(shape)]
            view = view.rearrange(f"p ({' '.join(names)}) -> p {' '.join(names)}",
                                  **dict(zip(names[1:], shape[1:])))
        return view


ARENA = 35072
AT_Q = 16384
AT_KV = AT_Q + TILES * D
AT_STAGE = AT_KV + TILES * 2 * KV
AT_MOD = ARENA
AT_X = AT_MOD + BATCH * 6 * D
AT_GATE_ATT = AT_X + TILES * D
MATRIX = KD * HIDDEN
AT_WO = 2 * 4 * MATRIX
AT_ROWS = AT_WO + 2 * MATRIX


def modulate_and_project(nc, core, m, dram):
    wmod = core.at(0, [3, KD, D])
    wmod_b = core.at(3 * KD * D, [6, KD, D // 2])
    wqkv = core.at(6 * KD * D, [KD, D + 2 * KV])
    memn = core.at(AT_STAGE + 6144, [KV + 2])
    h_tok = [core.at(AT_STAGE + 512 * u, [D]) for u in range(2)]
    hT = [core.at(AT_STAGE + 1024 + 512 * u, [KD, P]) for u in range(2)]
    q_min = core.at(AT_STAGE + 2048, [D])
    q_max = core.at(AT_STAGE + 2560, [D])
    elu = core.at(AT_STAGE + 3072, [D])
    eluT = core.at(AT_STAGE + 3584, [NQ, P])
    mem_out = core.at(AT_STAGE + 4096, [D])
    m.gate_mem = core.at(AT_STAGE + 4608, [BATCH, D])
    m.zeros = core.at(AT_STAGE + 5632, [D])
    silu_c = core.at(6 * KD * D + KD * (D + 2 * KV), [BATCH, KD, P])
    mod_tmp = core.at(AT_STAGE + 3072, [BATCH, D])

    ps_hT = core.psum[:, 0, :]
    ps_q = core.psum[:, 1, :]
    ps_kv = core.psum[:, 2, 0:2 * KV]
    ps_eluT = core.psum[:, 3, :]
    ps_mem = core.psum[:, 4:6, :].rearrange("p b (g n) -> p (b g) n", g=2)
    ps_mod = core.psum[:, 6:8, :]

    c_loaded, mw_loaded, consts_loaded, wqkv_loaded, memn_loaded = (
        core.sem(n) for n in ("c_loaded", "mw_loaded", "consts_loaded", "wqkv_loaded", "memn_loaded"))
    x_loaded = [core.sem(f"x_loaded{b}") for b in range(BATCH)]
    wmod_loaded = [core.sem(f"wmod_loaded{n}") for n in range(3)]
    wmod_b_loaded = core.sem("wmod_b_loaded")
    exp_c, exp_mw, silu_ready, mod_psum, mod_stored, mod_signed = (
        core.sem(n) for n in ("exp_c", "exp_mw", "silu_ready", "mod_psum", "mod_stored", "mod_signed"))
    var_ready, std_ready, h_ready, hT_psum, hT_ready, q_psum, kv_psum, q_stored, kv_stored = (
        core.sem(n) for n in ("var_ready", "std_ready", "h_ready", "hT_psum", "hT_ready", "q_psum",
                              "kv_psum", "q_stored", "kv_stored"))
    min_ready, exp_ready, elu_ready, eluT_psum, eluT_ready, mem_psum, mem_used = (
        core.sem(n) for n in ("min_ready", "exp_ready", "elu_ready", "eluT_psum", "eluT_ready",
                              "mem_psum", "mem_used"))
    dve_own, zeros_set, slots_zeroed = (
        core.sem(n) for n in ("dve_own_a", "zeros_set", "slots_zeroed"))
    order = [SCALE_A, SHIFT_A, GATE_A]
    HALF = D // 2

    with nc.Block() as block:
        @block.sync
        def _(sp):
            sp.dma_start(m.consts[:, :], dram.consts).then_inc(consts_loaded, 16)
            sp.dma_start(m.c_cols[:, :], dram.c).then_inc(c_loaded, 16)
            sp.dma_start(m.mw[:, 0:1], dram.mw.partition_broadcast(P)).then_inc(mw_loaded, 16)
            xs = dram.x.rearrange("(i p) d -> p i d", p=P)
            wm = dram.wmod.rearrange("(k p) (n d) -> n p k d", p=P, n=6)
            sp.dma_start(m.x[:, 0:TPB, :], xs[:, 0:TPB, :]).then_inc(x_loaded[0], 16)
            for n in order[:2]:
                sp.dma_start(wmod[:, n], wm[n]).then_inc(wmod_loaded[n], 16)
            sp.dma_start(m.x[:, TPB:TILES, :], xs[:, TPB:TILES, :]).then_inc(x_loaded[1], 16)
            sp.dma_start(wmod[:, GATE_A], wm[GATE_A]).then_inc(wmod_loaded[GATE_A], 16)
            sp.dma_start(wqkv, dram.wqkv.rearrange("(k p) n -> p k n", p=P)).then_inc(wqkv_loaded, 16)
            sp.dma_start(memn, dram.memn).then_inc(memn_loaded, 16)
            for t in range(6):
                sp.dma_start(wmod_b[:, t], wm[3 + t // 2][:, :, t % 2 * HALF:(t % 2 + 1) * HALF]).then_inc(wmod_b_loaded, 16)
            sp.dma_start(m.gate[:, :, :], dram.gate.rearrange("(k p) e -> p k e", p=P)).then_inc(m.gate_loaded, 16)
            sp.wait_ge(zeros_set, 1)
            sp.dma_start(dram.slots_x.rearrange("(r p) d -> p r d", p=P),
                         m.zeros[:, None, :].to_broadcast([P, SLOT_TILES, D])).then_inc(slots_zeroed, 16)
            sp.wait_ge(slots_zeroed, 16)

        @block.gpsimd
        def _(pool):
            nc.gpsimd.memset(m.zeros, 0.0).then_inc(zeros_set, 1)
            pool.wait_ge(mod_stored, 2 * len(order))
            pool.wait_ge(q_stored, TPB)
            pool.wait_ge(kv_stored, TPB)
            split_group(nc, pool, m, 0)
            pool.wait_ge(mod_stored, 2 * 3 + 2 * 6)
            scale, g, sign = m.mod[:, :, SCALE_B, :], m.mod[:, :, GATE_B, :], core.at(3 * KD * D, [BATCH, D])
            nc.gpsimd.tensor_scalar(scale, scale, 1.0, None, ALU.add)
            nc.gpsimd.tensor_scalar(sign, g, 0.0, 2.0, ALU.is_ge, ALU.mult)
            pool.drain()
            nc.gpsimd.tensor_scalar(sign, sign, -1.0, None, ALU.add)
            pool.drain()
            nc.gpsimd.tensor_tensor(g, g, sign, ALU.mult)
            pool.drain()
            nc.gpsimd.tensor_scalar(g, g, 0.25, None, ALU.max)
            pool.drain()
            nc.gpsimd.tensor_tensor(m.gate_b[:, :, :], g, sign, ALU.mult)
            pool.drain()

        @block.scalar
        def _(act):
            act.wait_ge(c_loaded, 16)
            nc.scalar.activation(m.c_exp[:, :], m.c_cols[:, :], ACT.Exp, scale=-1.0).then_inc(exp_c, 1)
            act.wait_ge(mw_loaded, 16)
            nc.scalar.activation(m.mw[:, 1:2], m.mw[:, 0:1], ACT.Exp, scale=-1.0).then_inc(exp_mw, 1)
            act.wait_ge(consts_loaded, 16)
            nc.scalar.copy(m.ident16[:, :], m.ident[:, :])
            def keep_modulation(pieces):
                for n in pieces:
                    for b in range(BATCH):
                        act.wait_ge(mod_psum, 2 * n + b + 1)
                        one = 1.0 if order[n] == SCALE_A else 0.0
                        nc.scalar.activation(m.mod[:, b, order[n], :], ps_mod[:, b, :], ACT.Copy,
                                             bias=one).then_inc(mod_stored, 1)

            def keep_half(t, b):
                act.wait_ge(mod_psum, 6 + 2 * t + b + 1)
                halves = m.mod[:, b].rearrange("p n (h w) -> p (n h) w", h=2)
                nc.scalar.copy(halves[:, 6 + t, :], ps_mod[:, b, 0:HALF]).then_inc(mod_stored, 1)

            act.wait_ge(var_ready, 1)
            nc.scalar.activation(m.std[:, :], m.var[:, :], ACT.Sqrt).then_inc(std_ready, 1)
            keep_modulation((0, 1))

            def turned_tile(i, u):
                act.wait_ge(hT_psum, i + 1)
                wait(act, kv_psum, i - 1)
                nc.scalar.copy(hT[u], ps_hT.rearrange("p (k s) -> p k s", k=KD)).then_inc(hT_ready, 1)

            def store_tile(i):
                act.wait_ge(q_psum, i + 1)
                nc.scalar.copy(m.q[:, i, :], ps_q).then_inc(q_stored, 1)
                act.wait_ge(kv_psum, i + 1)
                nc.scalar.copy(m.kv[:, i, :], ps_kv).then_inc(kv_stored, 1)

            def elu_exp(i):
                act.wait_ge(min_ready, i + 1)
                nc.scalar.activation(q_min, q_min, ACT.Exp).then_inc(exp_ready, 1)

            def elu_turned(i):
                act.wait_ge(eluT_psum, i + 1)
                wait(act, mem_psum, i)
                nc.scalar.copy(eluT, ps_eluT.rearrange("p (k s) -> p k s", k=NQ)).then_inc(eluT_ready, 1)

            def step(i, u):
                turned_tile(i + 1, 1 - u)
                elu_exp(i - 1)
                store_tile(i)
                elu_turned(i - 1)

            turned_tile(0, 0)
            keep_modulation((2,))
            turned_tile(1, 1)
            store_tile(0)
            step(1, 1)
            with act.Fori(1, TILES // 2 - 1) as j:
                for u in range(2):
                    step(2 * j + u, u)
                    keep_half(j - 1, u)
            step(TILES - 2, 0)
            elu_exp(TILES - 2)
            store_tile(TILES - 1)
            elu_turned(TILES - 2)
            elu_exp(TILES - 1)
            elu_turned(TILES - 1)

        @block.vector
        def _(dve):
            own = Chain(dve, dve_own)
            dve.wait_ge(exp_c, 1)
            own.done(nc.vector.tensor_scalar(m.c_exp[:, :], m.c_exp[:, :], 1.0, None, ALU.add))
            own.sync()
            own.done(nc.vector.reciprocal(m.c_exp[:, :], m.c_exp[:, :]))
            own.sync()
            own.done(nc.vector.tensor_tensor(m.c_exp[:, :], m.c_exp[:, :], m.c_cols[:, :], ALU.mult))
            own.sync()
            nc.vector.tensor_copy(
                silu_c, m.c_exp[:, :].rearrange("p (k b) -> p b k", b=BATCH)[:, :, :, None]
                .to_broadcast([P, BATCH, KD, P])).then_inc(silu_ready, 1)
            dve.wait_ge(exp_mw, 1)
            own.done(nc.vector.tensor_scalar(m.mw[:, 1:2], m.mw[:, 1:2], 1.0, None, ALU.add))
            own.sync()
            own.done(nc.vector.reciprocal(m.mw[:, 2:3], m.mw[:, 1:2]))
            own.sync()
            own.done(nc.vector.tensor_scalar(m.mw[:, 3:4], m.mw[:, 2:3], -1.0, 1.0, ALU.mult, ALU.add))
            for b in range(BATCH):
                dve.wait_ge(x_loaded[b], 16)
                for i in range(b * TPB, (b + 1) * TPB):
                    own.done(nc.vector.bn_stats(m.stats[:, i, :], m.x[:, i, :]))
            own.sync()
            mean_and_variance(nc, own, m)
            own.sync()
            nc.vector.tensor_scalar(m.var[:, :], m.var[:, :], EPS, None, ALU.add).then_inc(var_ready, 1)
            dve.wait_ge(std_ready, 1)
            own.done(nc.vector.reciprocal(m.rstd[:, :], m.std[:, :]))
            own.sync()

            def find_gates():
                dve.wait_ge(mod_stored, 2 * len(order))
                g = m.mod[:, :, GATE_A, :]
                own.done(nc.vector.tensor_scalar(mod_tmp, g, 0.0, 2.0, ALU.is_ge, ALU.mult))
                own.sync()
                own.done(nc.vector.tensor_scalar(mod_tmp, mod_tmp, -1.0, None, ALU.add))
                own.done(nc.vector.scalar_tensor_tensor(g, g, -1.0, g, ALU.mult, ALU.max))
                own.sync()
                own.done(nc.vector.scalar_tensor_tensor(g, g, 0.25, mod_tmp, ALU.max, ALU.mult))
                own.sync()
                own.done(nc.vector.tensor_scalar(m.gate_mem[:, :, :], g, m.mw[:, 2:3], None, ALU.mult))
                own.done(nc.vector.tensor_scalar(m.gate_att[:, :, :], g, m.mw[:, 3:4], None, ALU.mult))
                own.sync()

            def normalise(i, u, own):
                wait(dve, hT_psum, i - 1)
                own.done(nc.vector.scalar_tensor_tensor(
                    h_tok[u], m.x[:, i, :], m.mean[:, bass.ds(i, 1)], m.mod[:, i // TPB, SCALE_A, :],
                    ALU.subtract, ALU.mult))
                own.sync()
                nc.vector.scalar_tensor_tensor(
                    h_tok[u], h_tok[u], m.rstd[:, bass.ds(i, 1)], m.mod[:, i // TPB, SHIFT_A, :],
                    ALU.mult, ALU.add).then_inc(h_ready, 1)

            def elu_parts(i, own):
                dve.wait_ge(q_stored, i + 1)
                wait(dve, elu_ready, i)
                nc.vector.tensor_scalar(q_min, m.q[:, i, :], 0.0, None, ALU.min).then_inc(min_ready, 1)
                own.done(nc.vector.tensor_scalar(q_max, m.q[:, i, :], 0.0, -1.0, ALU.max, ALU.add))

            def elu_sum(i, own):
                dve.wait_ge(exp_ready, i + 1)
                wait(dve, eluT_psum, i)
                own.sync()
                nc.vector.tensor_tensor(elu, q_max, q_min, ALU.add).then_inc(elu_ready, 1)

            def add_memory(i, own):
                dve.wait_ge(mem_psum, i + 1)
                own.done(nc.vector.reciprocal(m.mem_den[:, :], ps_mem[:, :, KV]))
                own.sync()
                for g in range(NQ):
                    last = nc.vector.scalar_tensor_tensor(
                        mem_out[:, g * KV:(g + 1) * KV], ps_mem[:, g, 0:KV], m.mem_den[:, g:g + 1],
                        m.gate_mem[:, i // TPB, g * KV:(g + 1) * KV], ALU.mult, ALU.mult)
                last.then_inc(mem_used, 1)
                dve.wait_ge(mem_used, i + 1)
                own.done(nc.vector.tensor_tensor(m.x[:, i, :], m.x[:, i, :], mem_out, ALU.add))
                own.sync()

            def step(i, u, own):
                elu_parts(i - 1, own)
                normalise(i + 2, u, own)
                elu_sum(i - 1, own)
                add_memory(i - 2, own)

            dve.wait_ge(mod_stored, 4)
            normalise(0, 0, own)
            normalise(1, 1, own)
            normalise(2, 0, own)
            find_gates()
            elu_parts(0, own)
            normalise(3, 1, own)
            elu_sum(0, own)
            per_step = 4
            with dve.Fori(1, TILES // 2 - 1) as j:
                in_loop = Chain(dve, dve_own, own.count + (j - 1) * (2 * per_step))
                step(2 * j, 0, in_loop)
                step(2 * j + 1, 1, in_loop)
                assert in_loop.count == 2 * per_step
            own.count += (TILES - 4) * per_step
            for i in range(TILES - 2, TILES + 1):
                elu_parts(i - 1, own)
                elu_sum(i - 1, own)
                add_memory(i - 2, own)
            add_memory(TILES - 1, own)

        @block.tensor
        def _(pe):
            pe.wait_ge(silu_ready, 1)

            def modulate(pieces):
                for n in pieces:
                    pe.wait_ge(wmod_loaded[order[n]], 16)
                    for b in range(BATCH):
                        wait(pe, mod_stored, 2 * (n - 1) + b + 1)
                        for k in range(KD):
                            last = nc.tensor.matmul(ps_mod[:, b, :], silu_c[:, b, k, :],
                                                    wmod[:, order[n], k, :], start=k == 0, stop=k == KD - 1)
                        last.then_inc(mod_psum, 1)

            def modulate_half(t, b):
                pe.wait_ge(wmod_b_loaded, 6 * 16)
                pe.wait_ge(mod_stored, 6 + 2 * (t - 1) + b + 1)
                for k in range(KD):
                    last = nc.tensor.matmul(ps_mod[:, b, 0:HALF], silu_c[:, b, k, :], wmod_b[:, t, k, :],
                                            start=k == 0, stop=k == KD - 1)
                last.then_inc(mod_psum, 1)

            def turn_tile(i, u):
                pe.wait_ge(h_ready, i + 1)
                wait(pe, hT_ready, i)
                for k in range(KD):
                    last = nc.tensor.transpose(ps_hT[:, k * P:(k + 1) * P], h_tok[u][:, k * P:(k + 1) * P],
                                               m.ident)
                last.then_inc(hT_psum, 1)

            def project_q(i, u):
                pe.wait_ge(hT_ready, i + 1)
                wait(pe, q_stored, i)
                for k in range(KD):
                    last = nc.tensor.matmul(ps_q, hT[u][:, k, :], wqkv[:, k, 0:D], start=k == 0, stop=k == KD - 1)
                last.then_inc(q_psum, 1)

            def project_kv(i, u):
                wait(pe, kv_stored, i)
                for k in range(KD):
                    last = nc.tensor.matmul(ps_kv, hT[u][:, k, :], wqkv[:, k, D:], start=k == 0, stop=k == KD - 1)
                last.then_inc(kv_psum, 1)

            def turn_elu(i):
                pe.wait_ge(elu_ready, i + 1)
                wait(pe, eluT_ready, i)
                for g in range(NQ):
                    last = nc.tensor.transpose(ps_eluT[:, g * P:(g + 1) * P], elu[:, g * P:(g + 1) * P], m.ident)
                last.then_inc(eluT_psum, 1)

            def remember(i):
                pe.wait_ge(eluT_ready, i + 1)
                wait(pe, mem_used, i)
                for g in range(NQ):
                    last = nc.tensor.matmul(ps_mem[:, g, 0:KV + 1], eluT[:, g, :], memn[:, 0:KV + 1],
                                            start=True, stop=True)
                last.then_inc(mem_psum, 1)

            def step(i, u):
                turn_tile(i + 1, 1 - u)
                project_q(i, u)
                remember(i - 2)
                project_kv(i, u)
                turn_elu(i - 1)

            modulate((0, 1))
            pe.wait_ge(consts_loaded, 16)
            turn_tile(0, 0)
            modulate((2,))
            pe.wait_ge(wqkv_loaded, 16)
            pe.wait_ge(memn_loaded, 16)
            turn_tile(1, 1)
            project_q(0, 0)
            project_kv(0, 0)
            turn_tile(2, 0)
            project_q(1, 1)
            project_kv(1, 1)
            turn_elu(0)
            with pe.Fori(1, TILES // 2 - 1) as j:
                for u in range(2):
                    step(2 * j + u, u)
                    modulate_half(j - 1, u)
            step(TILES - 2, 0)
            project_q(TILES - 1, 1)
            remember(TILES - 3)
            project_kv(TILES - 1, 1)
            turn_elu(TILES - 2)
            remember(TILES - 2)
            turn_elu(TILES - 1)
            remember(TILES - 1)


def mean_and_variance(nc, own, m):
    even, odd = m.stats[:, :, 1], m.stats[:, :, 4]
    own.done(nc.vector.tensor_tensor(m.mean[:, :], even, odd, ALU.add))
    own.done(nc.vector.tensor_tensor(m.var[:, :], even, odd, ALU.subtract))
    own.done(nc.vector.tensor_tensor(m.std[:, :], m.stats[:, :, 2], m.stats[:, :, 5], ALU.add))
    own.sync()
    own.done(nc.vector.tensor_scalar(m.mean[:, :], m.mean[:, :], 0.5, None, ALU.mult))
    own.done(nc.vector.scalar_tensor_tensor(m.var[:, :], m.var[:, :], 0.25, m.var[:, :], ALU.mult, ALU.mult))
    own.sync()
    own.done(nc.vector.scalar_tensor_tensor(m.var[:, :], m.std[:, :], 1.0 / D, m.var[:, :], ALU.mult, ALU.add))


def split_group(nc, pool, m, n):
    b, h = n // NH, n % NH
    q = m.q[:, bass.ds(b * TPB, TPB), :].rearrange("p t (g w) -> p t g w", g=NQ)[:, :, :, bass.ds(h * DH, DH)]
    k = m.kv[:, bass.ds(b * TPB, TPB), bass.ds(h * DH, DH)]
    qp = m.q_parts.rearrange("p t g (j d) -> p t g j d", j=PARTS)
    kp = m.k_parts.rearrange("p t (j d) -> p t j d", j=PARTS)
    nc.gpsimd.tensor_copy(qp[:, :, :, 0, :], q)
    nc.gpsimd.tensor_copy(kp[:, :, 0, :], k)
    pool.drain()
    nc.gpsimd.tensor_tensor(m.rest, q, qp[:, :, :, 0, :], ALU.subtract)
    nc.gpsimd.tensor_tensor(m.rest_k, k, kp[:, :, 0, :], ALU.subtract)
    for j in (1, 2):
        nc.gpsimd.tensor_copy(qp[:, :, :, j, :], qp[:, :, :, 0, :])
    for j in (3, 5):
        nc.gpsimd.tensor_copy(kp[:, :, j, :], kp[:, :, 0, :])
    pool.drain()
    nc.gpsimd.tensor_copy(qp[:, :, :, 3, :], m.rest)
    nc.gpsimd.tensor_copy(kp[:, :, 1, :], m.rest_k)
    pool.drain()
    nc.gpsimd.tensor_tensor(qp[:, :, :, 5, :], m.rest, qp[:, :, :, 3, :], ALU.subtract)
    nc.gpsimd.tensor_tensor(kp[:, :, 2, :], m.rest_k, kp[:, :, 1, :], ALU.subtract)
    nc.gpsimd.tensor_copy(kp[:, :, 4, :], kp[:, :, 1, :])
    nc.gpsimd.tensor_copy(qp[:, :, :, 4, :], qp[:, :, :, 3, :])
    pool.drain().then_inc(m.ready_to_turn, 1)


def attention_order(now, ahead, behind):
    if not now and ahead:
        events = [("turn", 0), ("turn", 1)]
        for head in range(NQ):
            if head < NQ - 1:
                events.append(("turn", head + 2))
            events.extend(("peak", 8 * head + n) for n in range(8))
        return (events + [("peak", n) for n in range(32, 48)] + [("shift", 0)]
                + [("peak", n) for n in range(48, 64)])
    if not now:
        return [("out", -1), ("give", -1)]
    events, peaks = [], iter(range(64))

    def peak(n):
        if ahead:
            events.extend(("peak", x) for _, x in zip(range(n), peaks))

    between = {(0, 0): ("turn", 0), (0, 4): ("turn", 1), (1, 4): ("give", -1), (2, 2): ("turn", 2),
               (3, 1): ("turn", 3), (4, 1): ("shift", 1), (5, 1): ("turn", 4), (9, 1): ("give", 0),
               (10, 1): ("shift", 0)}
    peaks_in_step = {0: (0, 0, 0, 0, 0), 1: (0, 1, 1, 1, 1), 3: (1, 1, 1, 1, 1), 4: (1, 1, 1, 1, 1),
                     5: (1, 1, 1, 1, 1), 10: (1, 1, 1, 1, 1), 15: (1, 1, 1, 0, 1)}
    for k in range(STEPS):
        for n in range(NQ + 1):
            if n == NQ and (k or behind):
                events.append(("out", k - 1))
            peak(peaks_in_step.get(k, (1, 1, 1, 1, 0))[n])
            if n < NQ:
                events.append(("score", NQ * k + n))
            event = between.get((k, n))
            if event and {"turn": ahead, "give": behind or event[1] == 0,
                          "shift": ahead or event[1] == 1}[event[0]]:
                events.append(event)
    return events


def attend(nc, core, m, dram):
    q_parts, k_parts = m.q_parts, m.k_parts
    qT = core.at(2560, [2, NQ, SEQ], BF16)
    kT = core.at(6656, [2, SEQ], BF16)
    probs = [core.at(8192 + 2048 * u, [NQ, CHUNK]) for u in range(2)]
    values = core.at(12288, [TPB, 32])
    out_T = core.at(12544, [CHUNK])
    peaks = core.at(13056, [64])
    peak = core.at(13120, [16])
    peak_rest = core.at(13136, [16])
    peak_parts = core.at(13152, [4, SHIFT, NQ], BF16)
    shift_T = core.at(13184, [CHUNK], BF16)
    denom = core.at(13440, [4, NQ])
    minus_peak = core.at(13456, [16])
    no_peak = core.at(13472, [16])

    ps_scores = [core.psum[:, u, :] for u in range(3)]
    ps_peak = [core.psum[:, 3 + u, :] for u in range(3)]
    ps_out = core.psum[:, 6, :]
    ps_turn = core.psum[:, 7, :]
    ps_turn16 = ps_turn.bitcast(BF16)

    (in_turn_bank, out_of_turn_bank, peak_psum, peak_used, peak_found, shift_ready,
     shift_loaded, score_psum, exp_done, out_done, values_ready, out_stored, given, taken, kT_ones,
     dve_own) = (
        core.sem(n) for n in (
            "in_turn_bank", "out_of_turn_bank", "peak_psum", "peak_used", "peak_found",
            "shift_ready", "shift_loaded", "score_psum", "exp_done", "out_done", "values_ready",
            "out_stored", "given", "taken", "kT_ones", "dve_own_b"))
    FREE = 2
    UNITS = 64

    def turns_before(g):
        return 0 if isinstance(g, int) and g < 0 else 7 * g + 6

    def unit(n):
        return n // 32, n % 32 // 8, n % 8 // 2, n % 2

    def before_in_bank(n):
        return n - 2 if n >= 3 else (0, -2, -1)[n]

    def all_turns(engine, turn):
        turn(-1, False, True, False)
        turn(0, True, True, False)
        with engine.Fori(1, GROUPS - 1) as g:
            turn(g, True, True, True)
        turn(GROUPS - 1, True, False, True)
        turn(GROUPS, False, False, True)

    with nc.Block() as block:
        @block.sync
        def _(sp):
            def load_shift(n, par, c, passed):
                sp.wait_ge(out_of_turn_bank, passed)
                sp.dma_start(qT[ROWS:ROWS + SHIFT, par, :, c * CHUNK:(c + 1) * CHUNK],
                             shift_T[0:SHIFT * NQ, :]).then_inc(shift_loaded, 16)

            def turn(g, *parts):
                passed = turns_before(g)
                for what, n in attention_order(*parts):
                    if what in ("turn", "shift"):
                        passed = passed + 1
                    if what == "shift":
                        load_shift(2 * g + (1 if n else 2), (g if n else g + 1) % 2, n, passed)

            all_turns(sp, turn)
            sp.wait_ge(shift_loaded, 16 * 2 * GROUPS)

        @block.gpsimd
        def _(pool):
            def split(n):
                lead_in = isinstance(n, int) and n == 1
                pool.wait_ge(in_turn_bank, turns_before(n - 2) + turn_place(not lead_in, True, NQ))
                pool.wait_ge(kT_ones, 3)
                split_group(nc, pool, m, n)

            def stage_values(n):
                wait(pool, out_done, STEPS * n + FREE if not isinstance(n, int) or n else 0)
                pool.wait_ge(kT_ones, 3)
                b, h = n // NH, n % NH
                nc.gpsimd.tensor_copy(values[:, :, 0:DH],
                                      m.kv[:, bass.ds(b * TPB, TPB), bass.ds(h * DH + KV, DH)]).then_inc(values_ready, 1)

            def find_shift(n, c, passed):
                wait(pool, in_turn_bank, passed)
                pool.wait_ge(peak_found, 2 * n + c + 1)
                part = [peak_parts[:, :, j, :] for j in range(SHIFT)]
                whole, left = (v.rearrange("p (h t) -> p t h", t=4) for v in (minus_peak, peak_rest))
                nc.gpsimd.tensor_tensor(minus_peak, no_peak, peak, ALU.subtract)
                pool.drain()
                nc.gpsimd.tensor_copy(part[0], whole)
                pool.drain()
                nc.gpsimd.tensor_tensor(left, whole, part[0], ALU.subtract)
                pool.drain()
                nc.gpsimd.tensor_copy(part[1], left)
                pool.drain()
                nc.gpsimd.tensor_tensor(part[2], left, part[1], ALU.subtract).then_inc(shift_ready, 1)

            nc.gpsimd.memset(values[:, :, :], 0.0).then_inc(kT_ones, 1)
            pool.wait_ge(kT_ones, 1)
            nc.gpsimd.memset(values[:, :, DH:DH + 1], 1.0).then_inc(kT_ones, 1)
            pool.wait_ge(kT_ones, 2)
            nc.gpsimd.memset(kT[ROWS:ROWS + SHIFT, :, :], 1.0).then_inc(kT_ones, 1)
            pool.wait_ge(kT_ones, 3)
            nc.gpsimd.memset(no_peak, 0.0)
            split(1)
            find_shift(0, 0, 0)

            def add_output(g, c):
                pool.wait_ge(taken, 2 * g + c + 1)
                pool.wait_ge(kT_ones, 3)
                b, h = g // NH, g % NH
                tiles = bass.ds(b * TPB + 4 * c, 4)
                part, into = (v[:, tiles, :].rearrange("p t (h w) -> p t h w", h=NQ)[:, :, :, bass.ds(h * DH, DH)]
                              for v in (m.q, m.x))
                gate = m.gate_att[:, b, :].rearrange("p (h w) -> p h w", h=NQ)[:, :, bass.ds(h * DH, DH)]
                nc.gpsimd.tensor_tensor(part, part, gate[:, None].to_broadcast([P, 4, NQ, DH]), ALU.mult)
                pool.drain()
                nc.gpsimd.tensor_tensor(into, into, part, ALU.add)

            def turn(g, ahead, prepare, behind=True):
                find_shift(g, 1, turns_before(g))
                stage_values(g)
                if behind:
                    add_output(g - 1, 1)
                if ahead:
                    find_shift(g + 1, 0, turns_before(g) + turn_place(True, True, "shift1"))
                if prepare:
                    split(g + 2)
                add_output(g, 0)

            turn(0, True, True, False)
            with pool.Fori(1, GROUPS - 2) as g:
                turn(g, True, True)
            turn(GROUPS - 2, True, False)
            turn(GROUPS - 1, False, False)
            add_output(GROUPS - 1, 1)
            pool.drain()

        @block.tensor
        def _(pe):
            def into_turn_bank(before, g, passed):
                if before == "give":
                    pe.wait_ge(taken, passed)
                elif before == "turn":
                    wait(pe, out_of_turn_bank, passed)

            def turn(g, now, ahead, behind):
                passed = turns_before(g)
                takes = 2 * g - 1 if behind else 0
                before = "turn" if now or ahead else "give"
                for what, n in attention_order(now, ahead, behind):
                    if what == "turn":
                        into_turn_bank(before, g, takes if before == "give" else passed)
                        if n == 0:
                            pe.wait_ge(m.ready_to_turn, g + 2)
                        for t in range(TPB):
                            source = k_parts[:, t, :] if n == 0 else q_parts[:, t, n - 1, :]
                            last = nc.tensor.transpose(ps_turn16[0:ROWS, t * P:(t + 1) * P], source, m.ident16[:, :])
                        last.then_inc(in_turn_bank, 1)
                        passed, before = passed + 1, "turn"
                    elif what == "shift":
                        into_turn_bank(before, g, takes if before == "give" else passed)
                        pe.wait_ge(shift_ready, 2 * g + (2 if n else 3))
                        for t in range(4):
                            last = nc.tensor.transpose(ps_turn16[0:SHIFT * NQ, t * P:(t + 1) * P],
                                                       peak_parts[:, t].rearrange("p j h -> p (j h)"),
                                                       m.ident16[:, :])
                        last.then_inc(in_turn_bank, 1)
                        passed, before = passed + 1, "turn"
                    elif what == "peak":
                        c, head, tile, keys = unit(n)
                        par = (g + 1) % 2
                        if n % 8 == 0 and n < 32:
                            pe.wait_ge(out_of_turn_bank, turns_before(g) + turn_place(now, ahead, head + 1))
                        wait(pe, peak_used, UNITS * (g + 1) + before_in_bank(n))
                        s = (c * 4 + tile) * P
                        nc.tensor.matmul(ps_peak[n % 3], qT[0:ROWS, par, head, s:s + P],
                                         kT[0:ROWS, par, keys * CHUNK:(keys + 1) * CHUNK],
                                         start=True, stop=True).then_inc(peak_psum, 1)
                    elif what == "score":
                        k, head = n // NQ, n % NQ
                        c, t = k // TPB, k % TPB
                        par = g % 2
                        if n == 0:
                            pe.wait_ge(kT_ones, 3)
                        if n % (NQ * TPB) == 0:
                            pe.wait_ge(shift_loaded, 16 * (2 * g + c + 1))
                        wait(pe, exp_done, UNITS * g + before_in_bank(n))
                        nc.tensor.matmul(
                            ps_scores[n % 3], kT[0:ROWS + SHIFT, par, t * P:(t + 1) * P],
                            qT[0:ROWS + SHIFT, par, head, c * CHUNK:(c + 1) * CHUNK],
                            start=True, stop=True).then_inc(score_psum, 1)
                    elif what == "out":
                        c, t = n // TPB, n % TPB
                        if n == 0:
                            pe.wait_ge(values_ready, g + 1)
                        if t == 0:
                            pe.wait_ge(out_stored, 2 * g + c + 1)
                        pe.wait_ge(exp_done, UNITS * g + NQ * (n + 1))
                        for head in range(NQ):
                            last = nc.tensor.matmul(ps_out[32 * head:32 * head + 32, :], values[:, t, :],
                                                    probs[n % 2][:, head, :], start=t == 0, stop=t == TPB - 1)
                        last.then_inc(out_done, 1)
                    elif what == "give":
                        into_turn_bank(before, g, takes if before == "give" else passed)
                        pe.wait_ge(out_stored, 2 * g + n + 2)
                        for t in range(4):
                            last = nc.tensor.transpose(ps_turn[:, t * P:(t + 1) * P], out_T[:, t * P:(t + 1) * P],
                                                       m.ident)
                        last.then_inc(given, 1)
                        takes, before = takes + 1, "give"

            pe.sem_inc(out_done, FREE)
            all_turns(pe, turn)

        @block.scalar
        def _(act):
            def turn(g, *parts):
                passed = turns_before(g)
                par = (g + 1) % 2
                for what, n in attention_order(*parts):
                    if what == "turn":
                        if n >= 2:
                            act.wait_ge(in_turn_bank, passed + 1)
                            nc.scalar.copy(qT[0:ROWS, par, n - 1, :], ps_turn16[0:ROWS, :]).then_inc(out_of_turn_bank, 1)
                        passed = passed + 1
                    elif what == "shift":
                        act.wait_ge(in_turn_bank, passed + 1)
                        wait(act, shift_loaded, 16 * (2 * g + (1 if n else 2)))
                        nc.scalar.copy(shift_T[0:SHIFT * NQ, :], ps_turn16[0:SHIFT * NQ, 0:CHUNK]).then_inc(out_of_turn_bank, 1)
                        passed = passed + 1
                    elif what == "score":
                        k, head = n // NQ, n % NQ
                        act.wait_ge(score_psum, UNITS * g + n + 1)
                        if head == 0:
                            act.wait_ge(out_done, STEPS * g + k - 1 + FREE)
                        nc.scalar.activation(probs[k % 2][:, head, :], ps_scores[n % 3],
                                             ACT.Exp, scale=DH ** -0.5).then_inc(exp_done, 1)
                    elif what == "out" and n in (TPB - 1, -1):
                        act.wait_ge(out_done, STEPS * g + n + 1 + FREE)
                        wait(act, given, 2 * g + n // TPB)
                        nc.scalar.copy(out_T, ps_out).then_inc(out_stored, 1)

            act.sem_inc(out_stored, 1)
            all_turns(act, turn)

        @block.vector
        def _(dve):
            def turn(g, *parts):
                own = Chain(dve, dve_own, 2 * g - 1 if parts[2] else 0)
                passed = turns_before(g)
                par = (g + 1) % 2
                for what, n in attention_order(*parts):
                    if what == "turn" and n < 2:
                        dve.wait_ge(in_turn_bank, passed + 1)
                        target = kT[0:ROWS, par, :] if n == 0 else qT[0:ROWS, par, 0, :]
                        nc.vector.tensor_copy(target, ps_turn16[0:ROWS, :]).then_inc(out_of_turn_bank, 1)
                    if what in ("turn", "shift"):
                        passed = passed + 1
                    if what == "peak":
                        dve.wait_ge(peak_psum, UNITS * (g + 1) + n + 1)
                        nc.vector.reduce_max(peaks[:, n:n + 1], ps_peak[n % 3], AX).then_inc(peak_used, 1)
                        if n % 32 == 31:
                            c = n // 32
                            dve.wait_ge(peak_used, UNITS * (g + 1) + n + 1)
                            wait(dve, shift_ready, 2 * (g + 1) + c)
                            pairs = peaks[:, 32 * c:32 * c + 32].rearrange("p (n k) -> p n k", k=2)
                            nc.vector.tensor_reduce(peak, pairs, AX, ALU.max).then_inc(peak_found, 1)
                    elif what == "give":
                        dve.wait_ge(given, 2 * g + n + 1)
                        o = ps_turn.rearrange("p (t h w) -> p t h w", t=4, h=NQ)
                        own.done(nc.vector.reciprocal(denom, o[:, :, :, DH]))
                        own.sync()
                        of, c = (g, 0) if n == 0 else (g - 1, 1)
                        b, h = of // NH, of % NH
                        target = m.q[:, bass.ds(b * TPB + 4 * c, 4), :].rearrange(
                            "p t (h w) -> p t h w", h=NQ)[:, :, :, bass.ds(h * DH, DH)]
                        nc.vector.tensor_tensor(target, o[:, :, :, 0:DH],
                                                denom[:, :, :, None].to_broadcast([P, 4, NQ, DH]),
                                                ALU.mult).then_inc(taken, 1)

            all_turns(dve, turn)


def turn_place(now, ahead, what):
    count = 0
    for name, n in attention_order(now, ahead, False):
        if name in ("turn", "shift"):
            count += 1
            if (name, n) == ("turn", what) or (name == "shift" and what == f"shift{n}"):
                return count
    raise ValueError(what)


def route(nc, core, m, dram):
    RING = 4
    h_tok = [core.at(AT_STAGE + 3584 + 512 * u, [D]) for u in range(RING)]
    hT = [core.at(AT_STAGE + 1024 + 512 * u, [KD, P]) for u in range(2)]
    ps_hT = [core.psum[:, n, :] for n in (0, 6)]
    ps_logits = [core.psum[:, n, 0:EXPERTS] for n in (1, 3, 4, 5)]
    ps_rank = core.psum[:, 2, 0:(TILES + 1) * EXPERTS].rearrange("p (i e) -> p i e", e=EXPERTS)
    R = [P, TILES, EXPERTS]
    lg, pick1, pick2, masked, base = (core.at(AT_STAGE + 2048 + 128 * n, [TILES, EXPERTS]) for n in range(5))
    chosen = core.at(AT_STAGE + 2688, [TILES + 1, EXPERTS])
    top1, top2, slot_f, expo = (core.at(AT_STAGE + 2848 + 16 * n, [TILES]) for n in range(4))
    over = core.at(AT_STAGE + 2912, [EXPERTS, 16])
    lower = core.at(AT_STAGE + 3040, [EXPERTS, EXPERTS])
    counts, starts_f = (core.at(AT_STAGE + 3104 + 8 * n, [EXPERTS]) for n in range(2))
    tile_ge = core.at(AT_STAGE + 3120, [SLOT_TILES, EXPERTS - 1])
    tile_f = core.at(AT_STAGE + 3120 + SLOT_TILES * 7, [SLOT_TILES])

    (var_ready, std_ready, h_ready, h_kept, hT_psum, hT_ready, logit_psum, logit_used, diff_ready,
     exp_ready, chosen_ready, ranked, scattered, x1_kept, dve_own) = (
        core.sem(n) for n in ("var_ready_b", "std_ready_b", "h_ready_b", "h_kept", "hT_psum_b",
                              "hT_ready_b", "logit_psum", "logit_used", "diff_ready", "exp_ready_b",
                              "chosen_ready", "ranked", "scattered", "x1_kept", "dve_own_c"))

    with nc.Block() as block:
        @block.sync
        def _(sp):
            load_widening(sp, m, dram, 0)
            sp.dma_start(dram.x1.rearrange("(i p) d -> p i d", p=P), m.x[:, :, :]).then_inc(x1_kept, 16)
            sp.wait_ge(x1_kept, 16)

        @block.gpsimd
        def _(pool):
            split_weights(nc, pool, m, 0)
            pool.wait_ge(h_kept, TILES)
            pool.wait_ge(m.slots_ready, 1)
            for i in range(TILES):
                for j in range(2):
                    nc.gpsimd.indirect_dma_start(
                        out=dram.slots_x,
                        out_offset=bass.IndirectOffsetOnAxis(ap=m.slots[:, j, i:i + 1], axis=0),
                        in_=m.q[:, i, :], in_offset=None).then_inc(scattered, 16)
            pool.wait_ge(scattered, 16 * 2 * TILES)

        @block.vector
        def _(dve):
            own = Chain(dve, dve_own)
            for i in range(TILES):
                own.done(nc.vector.bn_stats(m.stats[:, i, :], m.x[:, i, :]))
            own.sync()
            mean_and_variance(nc, own, m)
            own.sync()
            nc.vector.tensor_scalar(m.var[:, :], m.var[:, :], EPS, None, ALU.add).then_inc(var_ready, 1)
            dve.wait_ge(std_ready, 1)
            own.done(nc.vector.reciprocal(m.rstd[:, :], m.std[:, :]))
            own.sync()

            def normalise(i, own):
                for u in range(RING):
                    wait(dve, hT_psum, i + u - RING + 1)
                    wait(dve, h_kept, i + u - RING + 1)
                    own.done(nc.vector.scalar_tensor_tensor(
                        h_tok[u], m.x[:, i + u, :], m.mean[:, bass.ds(i + u, 1)],
                        m.mod[:, (i + u) // TPB, SCALE_B, :], ALU.subtract, ALU.mult))
                    if u:
                        finish(i, u - 1, own)
                finish(i, RING - 1, own)

            def finish(i, u, own):
                dve.wait_ge(dve_own, own.base + own.count - (0 if u == RING - 1 else 1))
                nc.vector.scalar_tensor_tensor(
                    h_tok[u], h_tok[u], m.rstd[:, bass.ds(i + u, 1)], m.mod[:, (i + u) // TPB, SHIFT_B, :],
                    ALU.mult, ALU.add).then_inc(h_ready, 1)
                if not isinstance(i, int) or u >= 3:
                    keep_logits(i + u - 3, (u - 3) % RING)

            def keep_logits(i, u):
                dve.wait_ge(logit_psum, i + 1)
                nc.vector.tensor_copy(lg[:, i, :], ps_logits[u]).then_inc(logit_used, 1)

            normalise(0, own)
            with dve.Fori(1, TILES // RING) as j:
                normalise(RING * j, Chain(dve, dve_own, own.count + (j - 1) * RING))
            own.count += RING * (TILES // RING - 1)
            for i in range(TILES - 3, TILES):
                keep_logits(i, i % RING)
            dve.wait_ge(logit_used, TILES)

            def pick(source, best, one_hot):
                own.done(nc.vector.tensor_reduce(best, source, AX, ALU.max))
                own.sync()
                own.done(nc.vector.tensor_tensor(one_hot, source, best[:, :, None].to_broadcast(R), ALU.is_equal))
                own.sync()
                own.done(nc.vector.tensor_tensor(one_hot, one_hot, m.falling[:, None, :].to_broadcast(R), ALU.mult))
                own.sync()
                own.done(nc.vector.tensor_reduce(slot_f, one_hot, AX, ALU.max))
                own.sync()
                own.done(nc.vector.tensor_tensor(one_hot, one_hot, slot_f[:, :, None].to_broadcast(R), ALU.is_equal))
                own.sync()

            pick(lg, top1, pick1)
            own.done(nc.vector.scalar_tensor_tensor(masked, pick1, -3e38, lg, ALU.mult, ALU.add))
            own.sync()
            pick(masked, top2, pick2)
            nc.vector.tensor_tensor(expo, top2, top1, ALU.subtract).then_inc(diff_ready, 1)
            own.done(nc.vector.memset(chosen[:, TILES, :], 0.0))
            nc.vector.tensor_tensor(chosen[:, 0:TILES, :], pick1, pick2, ALU.add).then_inc(chosen_ready, 1)
            dve.wait_ge(exp_ready, 1)
            own.done(nc.vector.tensor_scalar(top1, expo, 1.0, None, ALU.add))
            own.sync()
            own.done(nc.vector.reciprocal(m.choice[:, 0, :], top1))
            own.sync()
            own.done(nc.vector.tensor_tensor(m.choice[:, 1, :], m.choice[:, 0, :], expo, ALU.mult))
            dve.wait_ge(ranked, 1)
            own.done(nc.vector.tensor_copy(counts, ps_rank[:, TILES, :]))
            own.sync()
            own.done(nc.vector.tensor_tensor(over, counts[:, :, None].to_broadcast([P, EXPERTS, 16]),
                                             m.steps_of_128[:, None, :].to_broadcast([P, EXPERTS, 16]), ALU.is_gt))
            own.sync()
            own.done(nc.vector.tensor_reduce(counts, over, AX, ALU.add))
            own.sync()
            own.done(nc.vector.tensor_tensor(lower, counts[:, None, :].to_broadcast([P, EXPERTS, EXPERTS]),
                                             m.below, ALU.mult))
            own.sync()
            own.done(nc.vector.tensor_reduce(starts_f, lower, AX, ALU.add))
            own.sync()
            own.done(nc.vector.tensor_copy(m.starts[:, :], starts_f))
            own.done(nc.vector.tensor_tensor(
                tile_ge, m.tile_ids[:, :, None].to_broadcast([P, SLOT_TILES, EXPERTS - 1]),
                starts_f[:, None, 1:EXPERTS].to_broadcast([P, SLOT_TILES, EXPERTS - 1]), ALU.is_ge))
            own.sync()
            own.done(nc.vector.tensor_reduce(tile_f, tile_ge, AX, ALU.add))
            own.sync()
            own.done(nc.vector.tensor_copy(m.tile_expert[:, :], tile_f))
            own.done(nc.vector.tensor_scalar(starts_f, starts_f, float(P), None, ALU.mult))
            own.sync()
            own.done(nc.vector.tensor_tensor(base, ps_rank[:, 0:TILES, :], starts_f[:, None, :].to_broadcast(R), ALU.add))
            own.sync()
            for j, one_hot in enumerate((pick1, pick2)):
                own.done(nc.vector.tensor_tensor(masked, one_hot, base, ALU.mult))
                own.sync()
                own.done(nc.vector.tensor_reduce(slot_f, masked, AX, ALU.add))
                own.sync()
                own.done(nc.vector.tensor_copy(m.slots[:, j, :], slot_f))
            own.sync()
            dve.sem_inc(m.slots_ready, 1)

        @block.scalar
        def _(act):
            act.wait_ge(var_ready, 1)
            nc.scalar.activation(m.std[:, :], m.var[:, :], ACT.Sqrt).then_inc(std_ready, 1)

            def turned(i, u):
                act.wait_ge(hT_psum, i + 1)
                wait(act, logit_psum, i - 1)
                nc.scalar.copy(hT[u], ps_hT[u].rearrange("p (k s) -> p k s", k=KD)).then_inc(hT_ready, 1)

            def keep(i, u):
                act.wait_ge(h_ready, i + 1)
                nc.scalar.copy(m.q[:, i, :], h_tok[u]).then_inc(h_kept, 1)

            for u in range(RING):
                turned(u, u % 2)
                keep(u, u)
            with act.Fori(1, TILES // RING) as j:
                for u in range(RING):
                    turned(RING * j + u, u % 2)
                    keep(RING * j + u, u)
            act.wait_ge(diff_ready, 1)
            nc.scalar.activation(expo, expo, ACT.Exp).then_inc(exp_ready, 1)

        @block.tensor
        def _(pe):
            pe.wait_ge(m.gate_loaded, 16)

            def turn_tile(i, u):
                pe.wait_ge(h_ready, i + 1)
                wait(pe, hT_ready, i - 1)
                for k in range(KD):
                    last = nc.tensor.transpose(ps_hT[u % 2][:, k * P:(k + 1) * P], h_tok[u][:, k * P:(k + 1) * P], m.ident)
                last.then_inc(hT_psum, 1)

            def logits(i, u):
                pe.wait_ge(hT_ready, i + 1)
                wait(pe, logit_used, i - RING + 1)
                for k in range(KD):
                    last = nc.tensor.matmul(ps_logits[u], hT[u % 2][:, k, :], m.gate[:, k, :], start=k == 0, stop=k == KD - 1)
                last.then_inc(logit_psum, 1)

            def ring(i):
                for u in range(RING):
                    turn_tile(i + u, u)
                    if not isinstance(i, int) or u:
                        logits(i + u - 1, (u - 1) % RING)

            ring(0)
            with pe.Fori(1, TILES // RING) as j:
                ring(RING * j)
            logits(TILES - 1, RING - 1)
            pe.wait_ge(chosen_ready, 1)
            nc.tensor.matmul(ps_rank[:, 0:TILES, :], m.before, chosen[:, 0:TILES, :], start=True, stop=False,
                             skip_group_check=True)
            for i in range(TILES):
                last = nc.tensor.matmul(ps_rank[:, i + 1:TILES + 1, :], m.ones[:, :],
                                        chosen[:, i:i + 1, :].to_broadcast([P, TILES - i, EXPERTS]),
                                        start=False, stop=i == TILES - 1, skip_group_check=True)
            last.then_inc(ranked, 1)


def load_widening(sp, m, dram, e):
    for n, source in enumerate((dram.w0[e], dram.w1[e])):
        sp.dma_start(m.w_raw[e % 2][:, n], source.rearrange("(k p) n -> p k n", p=P)).then_inc(m.w_dma[e % 2], 16)


def split_weights(nc, pool, m, e):
    pool.wait_ge(m.w_dma[e % 2], 32 * (e // 2 + 1))
    for n in range(2):
        nc.gpsimd.tensor_copy(m.w_parts[:, e % 2, 1, n], m.w_raw[e % 2][:, n])
    pool.drain()
    for n in range(2):
        nc.gpsimd.tensor_tensor(m.w_parts[:, e % 2, 0, n], m.w_raw[e % 2][:, n], m.w_parts[:, e % 2, 1, n],
                                ALU.subtract)
    pool.drain().then_inc(m.weights_ready, 1)


def experts(nc, core, m, dram):
    x_rows, silu, hidden, y_rows = (core.place(n, AT_ROWS + 1024 * u, [2, D]) for u, n in enumerate(
        ("x_rows", "silu", "hidden", "y_rows")))
    hiddenT = core.place("hiddenT", AT_ROWS + 4096, [2, 4, P])
    xT = core.place("xT_parts", AT_ROWS + 5120, [2, 2, KD, P], F32R)
    LOW, HIGH = 0, 1

    ps_gate = [core.psum[:, 2 * c, :] for c in range(2)]
    ps_up = [core.psum[:, 2 * c + 1, :] for c in range(2)]
    ps_xT = core.psum[:, 4, :]
    ps_hT = [core.psum[:, 5 + c, :] for c in range(2)]
    ps_y = core.psum[:, 7, :]

    x_loaded = [core.sem(f"x_rows_loaded{u}") for u in range(2)]
    wo_dma = [core.sem(f"wo_dma{u}") for u in range(2)]
    y_out = [core.sem(f"y_out{u}") for u in range(2)]
    (wo_ready, xT_psum, high_ready, low_ready, gate_psum, up_psum, silu_ready, hidden_ready, hT_psum, hT_ready,
     y_psum, y_ready) = (
        core.sem(n) for n in ("wo_ready", "xT_psum", "high_ready", "low_ready", "gate_psum", "up_psum", "silu_ready_m",
                              "hidden_ready", "hidT_psum", "hidT_ready", "y_psum", "y_ready"))
    slots_x = dram.slots_x.rearrange("(r p) d -> r p d", p=P)
    slots_y = dram.slots_y.rearrange("(r p) d -> r p d", p=P)
    PAIRS = SLOT_TILES // 2

    with nc.Block() as block:
        @block.sync
        def _(sp):
            def load_narrowing(e):
                sp.dma_start(m.wo[:, e % 2], dram.wo[e].rearrange("(k p) n -> p k n", p=P)).then_inc(wo_dma[e % 2], 16)

            def announce(e):
                sp.wait_ge(wo_dma[e % 2], 16 * (e // 2 + 1))
                sp.sem_inc(wo_ready, 1)

            sp.wait_ge(x_loaded[0], 16)
            load_narrowing(0)
            load_widening(sp, m, dram, 1)
            load_narrowing(1)
            announce(0)
            announce(1)
            for e in range(2, EXPERTS):
                tiles = sp.value_load(m.starts[0:1, e - 1:e], min_val=0, max_val=SLOT_TILES)
                sp.wait_ge(y_psum, tiles + 1)
                load_widening(sp, m, dram, e)
                load_narrowing(e)
                announce(e)

        @block.gpsimd
        def _(pool):
            for e in range(1, EXPERTS):
                split_weights(nc, pool, m, e)

        @block.tensor
        def _(pe):
            def turn_rows(r, u, j):
                pe.wait_ge(x_loaded[u], 16 * (j + 1))
                wait(pe, low_ready, r)
                for k in range(KD):
                    last = nc.tensor.transpose(ps_xT[:, k * P:(k + 1) * P], x_rows[:, u, k * P:(k + 1) * P], m.ident)
                last.then_inc(xT_psum, 1)

            def weights_of(r, ready):
                e = pe.value_load(m.tile_expert[0:1, bass.ds(r, 1)], min_val=0, max_val=EXPERTS - 1)
                pe.wait_ge(ready, e + 1)
                return e % 2

            def widen(r, u, c, buffer):
                wait(pe, hidden_ready, 2 * r - 1 + c)
                for ps, n, psum_sem in ((ps_gate[c], 0, gate_psum), (ps_up[c], 1, up_psum)):
                    for k in range(KD):
                        for p, (x_part, w_part) in enumerate(((HIGH, HIGH), (HIGH, LOW), (LOW, HIGH))):
                            at = ((w_part * 2 + n) * KD + k) * HIDDEN + c * CHUNK
                            last = nc.tensor.matmul(ps, xT[:, u, x_part, k, :],
                                                    parts[:, buffer, at:at + CHUNK],
                                                    start=k + p == 0, stop=k == KD - 1 and p == 2)
                    last.then_inc(psum_sem, 1)

            def turn_hidden(r, c):
                pe.wait_ge(hidden_ready, 2 * r + c + 1)
                wait(pe, hT_ready, 2 * r - 1 + c)
                for k in range(4):
                    last = nc.tensor.transpose(ps_hT[c][:, k * P:(k + 1) * P], hidden[:, c, k * P:(k + 1) * P], m.ident)
                last.then_inc(hT_psum, 1)

            def narrow(r, buffer):
                wait(pe, y_ready, r)
                for k in range(KH):
                    if k % 4 == 0:
                        pe.wait_ge(hT_ready, 2 * r + k // 4 + 1)
                    last = nc.tensor.matmul(ps_y, hiddenT[:, k // 4, k % 4, :], wo[:, buffer, k * D:(k + 1) * D],
                                            start=k == 0, stop=k == KH - 1)
                last.then_inc(y_psum, 1)

            def step(r, u, j, more):
                turn_hidden(r - 1, 0)
                now = weights_of(r, m.weights_ready)
                pe.wait_ge(low_ready, r + 1)
                widen(r, u, 0, now)
                turn_hidden(r - 1, 1)
                widen(r, u, 1, now)
                if more:
                    turn_rows(r + 1, 1 - u, j + u)
                narrow(r - 1, weights_of(r - 1, wo_ready))

            parts = m.w_parts[:, :, :, :, :, :].rearrange("p b h n k w -> p b (h n k w)")
            wo = m.wo[:, :, :, :].rearrange("p b k n -> p b (k n)")
            pe.sem_inc(y_psum, 1)
            turn_rows(0, 0, 0)
            first = weights_of(0, m.weights_ready)
            pe.wait_ge(low_ready, 1)
            widen(0, 0, 0, first)
            widen(0, 0, 1, first)
            turn_rows(1, 1, 0)
            step(1, 1, 0, True)
            with pe.Fori(1, PAIRS) as j:
                step(2 * j, 0, j, True)
                step(2 * j + 1, 1, j, True)
            step(SLOT_TILES - 1, 0, PAIRS, False)
            turn_hidden(SLOT_TILES - 1, 0)
            turn_hidden(SLOT_TILES - 1, 1)
            narrow(SLOT_TILES - 1, weights_of(SLOT_TILES - 1, wo_ready))

        @block.scalar
        def _(act):
            def load_rows(r, u):
                act.dma_start(x_rows[:, u], slots_x[r]).then_inc(x_loaded[u], 16)

            def turned_rows(r, u, more=True):
                act.wait_ge(xT_psum, r + 1)
                wait(act, up_psum, 2 * (r - 1))
                nc.scalar.copy(xT[:, u, HIGH], ps_xT.rearrange("p (k s) -> p k s", k=KD)).then_inc(high_ready, 1)
                if more:
                    load_rows(r + 2, u)

            def gate(r, c):
                act.wait_ge(gate_psum, 2 * r + c + 1)
                wait(act, hidden_ready, 2 * r - 1 + c)
                nc.scalar.activation(silu[:, c], ps_gate[c], ACT.Silu).then_inc(silu_ready, 1)

            def turned_hidden(r, c):
                act.wait_ge(hT_psum, 2 * r + c + 1)
                wait(act, y_psum, r + 1)
                nc.scalar.copy(hiddenT[:, c], ps_hT[c].rearrange("p (k s) -> p k s", k=4)).then_inc(hT_ready, 1)

            def store(r, u, j, first):
                act.wait_ge(y_psum, r + 2)
                if not first:
                    act.wait_ge(y_out[u], 16 * j)
                nc.scalar.copy(y_rows[:, u], ps_y).then_inc(y_ready, 1)
                act.wait_ge(y_ready, r + 1)
                act.dma_start(slots_y[r], y_rows[:, u]).then_inc(y_out[u], 16)

            def step(r, u, j, more, first=False):
                turned_hidden(r - 1, 0)
                gate(r, 0)
                turned_hidden(r - 1, 1)
                gate(r, 1)
                if more:
                    turned_rows(r + 1, 1 - u, more != "last")
                store(r - 1, 1 - u, j, first)

            load_rows(0, 0)
            load_rows(1, 1)
            turned_rows(0, 0)
            gate(0, 0)
            gate(0, 1)
            turned_rows(1, 1)
            step(1, 1, 0, True, True)
            step(2, 0, 0, True, True)
            step(3, 1, 1, True)
            with act.Fori(2, PAIRS - 1) as j:
                step(2 * j, 0, j - 1, True)
                step(2 * j + 1, 1, j, True)
            step(SLOT_TILES - 3, 0, PAIRS - 2, "last")
            step(SLOT_TILES - 2, 1, PAIRS - 1, "last")
            step(SLOT_TILES - 1, 0, PAIRS - 1, False)
            turned_hidden(SLOT_TILES - 1, 0)
            turned_hidden(SLOT_TILES - 1, 1)
            store(SLOT_TILES - 1, 0, PAIRS, False)
            act.wait_ge(y_out[0], 16 * (PAIRS + 1))
            act.wait_ge(y_out[1], 16 * PAIRS)

        @block.vector
        def _(dve):
            def low_part(r, u):
                dve.wait_ge(high_ready, r + 1)
                nc.vector.tensor_tensor(xT[:, u, LOW], ps_xT.rearrange("p (k s) -> p k s", k=KD), xT[:, u, HIGH],
                                        ALU.subtract).then_inc(low_ready, 1)

            def tile(r, first=False):
                for c in range(2):
                    dve.wait_ge(silu_ready, 2 * r + c + 1)
                    dve.wait_ge(up_psum, 2 * r + c + 1)
                    if not first:
                        dve.wait_ge(hT_psum, 2 * r - 1 + c)
                    nc.vector.tensor_tensor(hidden[:, c], silu[:, c], ps_up[c], ALU.mult).then_inc(hidden_ready, 1)

            low_part(0, 0)
            tile(0, True)
            low_part(1, 1)
            tile(1)
            low_part(2, 0)
            with dve.Fori(1, PAIRS) as j:
                tile(2 * j)
                low_part(2 * j + 1, 1)
                tile(2 * j + 1)
                low_part(2 * j + 2, 0)
            tile(SLOT_TILES - 1)


def combine(nc, core, m, dram):
    RING = 4
    rows = core.at(0, [RING, 2, D])
    gathered = [core.sem(f"gathered{n}") for n in range(RING)]
    scaled, combined, stored, dve_own = (core.sem(n) for n in ("scaled", "combined", "stored", "dve_own_d"))
    QUARTER = TILES // 4
    x1_loaded = [core.sem(f"x1_loaded{n}") for n in range(4)]
    out = dram.out.rearrange("(i p) d -> p i d", p=P)

    with nc.Block() as block:
        @block.gpsimd
        def _(pool):
            for i in range(TILES):
                wait(pool, combined, i - RING + 1)
                for j in range(2):
                    nc.gpsimd.indirect_dma_start(
                        out=rows[:, i % RING, j, :], out_offset=None, in_=dram.slots_y,
                        in_offset=bass.IndirectOffsetOnAxis(ap=m.slots[:, j, i:i + 1], axis=0)
                    ).then_inc(gathered[i % RING], 16)

        @block.scalar
        def _(act):
            for i in range(TILES):
                act.wait_ge(gathered[i % RING], 32 * (i // RING + 1))
                row = rows[:, i % RING, 0, :]
                nc.scalar.activation(row, row, ACT.Copy, scale=m.choice[:, 0, i:i + 1]).then_inc(scaled, 1)

        @block.vector
        def _(dve):
            for i in range(TILES):
                own = Chain(dve, dve_own, 2 * i)
                first, second = rows[:, i % RING, 0, :], rows[:, i % RING, 1, :]
                dve.wait_ge(scaled, i + 1)
                own.done(nc.vector.scalar_tensor_tensor(first, second, m.choice[:, 1, i:i + 1], first,
                                                        ALU.mult, ALU.add))
                own.sync()
                own.done(nc.vector.tensor_tensor(first, first, m.gate_b[:, i // TPB, :], ALU.mult))
                own.sync()
                if i % QUARTER == 0:
                    dve.wait_ge(x1_loaded[i // QUARTER], 16)
                nc.vector.tensor_tensor(m.x[:, i, :], m.x[:, i, :], first, ALU.add).then_inc(combined, 1)

        @block.sync
        def _(sp):
            x1 = dram.x1.rearrange("(i p) d -> p i d", p=P)
            for n in range(4):
                tiles = slice(n * QUARTER, (n + 1) * QUARTER)
                sp.dma_start(m.x[:, tiles, :], x1[:, tiles, :]).then_inc(x1_loaded[n], 16)
            for i in range(TILES):
                sp.wait_ge(combined, i + 1)
                sp.dma_start(out[:, i, :], m.x[:, i, :]).then_inc(stored, 16)
            sp.wait_ge(stored, 16 * TILES)


class Names:
    pass


def constants():
    import numpy as np
    cols = [np.eye(P), np.triu(np.ones((P, P)), 1), np.ones((P, P)),
            np.tile(np.arange(EXPERTS, 0, -1), (P, 1)), np.tile(P * np.arange(16), (P, 1)),
            np.tile(np.tril(np.ones((EXPERTS, EXPERTS)), -1).ravel(), (P, 1)),
            np.tile(np.arange(SLOT_TILES), (P, 1))]
    return np.concatenate(cols, 1).astype(np.float32)


def build(nc, dram):
    with ExitStack() as stack:
        core, m = Core(nc, stack), Names()
        width = 3 * P + EXPERTS + 16 + EXPERTS * EXPERTS + SLOT_TILES
        m.consts = core.sb("consts", [P, width])
        m.ident, m.before, m.ones = (m.consts[:, n * P:(n + 1) * P] for n in range(3))
        at = 3 * P
        m.falling = m.consts[:, at:at + EXPERTS]
        m.steps_of_128 = m.consts[:, at + 8:at + 24]
        m.below = m.consts[:, at + 24:at + 88].rearrange("p (a b) -> p a b", b=EXPERTS)
        m.tile_ids = m.consts[:, at + 88:at + 88 + SLOT_TILES]
        m.ident16 = core.sb("ident16", [P, P], BF16)
        m.gate_b = core.sb("gate_b", [P, BATCH, D])
        m.gate = core.sb("gate", [P, KD, EXPERTS])
        m.c_cols = core.sb("c_cols", [P, KD * BATCH])
        m.c_exp = core.sb("c_exp", [P, KD * BATCH])
        m.mw = core.sb("mw", [P, 4])
        m.mem_den = core.sb("mem_den", [P, NQ])
        m.stats = core.sb("stats", [P, TILES, 6])
        m.mean, m.var, m.std, m.rstd = (core.sb(n, [P, TILES]) for n in ("mean", "var", "std", "rstd"))
        m.choice = core.sb("choice", [P, 2, TILES])
        m.slots = core.sb("slots", [P, 2, TILES], I32)
        m.starts = core.sb("starts", [P, EXPERTS], I32)
        m.tile_expert = core.sb("tile_expert", [P, SLOT_TILES], I32)
        m.gate_loaded, m.slots_ready = core.sem("gate_loaded"), core.sem("slots_ready")
        m.ready_to_turn = core.sem("ready_to_turn")
        m.w_dma = [core.sem(f"w_dma{u}") for u in range(2)]
        m.weights_ready = core.sem("weights_ready")
        core.place_arena()
        m.mod = core.place("mod", AT_MOD, [BATCH, 6, D])
        m.x = core.place("x_tokens", AT_X, [TILES, D])
        m.gate_att = core.place("gate_att", AT_GATE_ATT, [BATCH, D])
        m.w_raw = [core.place(f"w_raw{u}", u * 4 * MATRIX, [2, KD, HIDDEN]) for u in range(2)]
        m.w_parts = core.place("w_parts", 0, [2, 2, 2, KD, HIDDEN], F32R)
        m.wo = core.place("wo", AT_WO, [2, KH, D])
        m.q = core.at(AT_Q, [TILES, D])
        m.kv = core.at(AT_KV, [TILES, 2 * KV])
        m.q_parts = core.at(0, [TPB, NQ, ROWS], BF16)
        m.k_parts = core.at(1536, [TPB, ROWS], BF16)
        m.rest = core.at(1920, [TPB, NQ, DH])
        m.rest_k = core.at(2432, [TPB, DH])
        modulate_and_project(nc, core, m, dram)
        attend(nc, core, m, dram)
        route(nc, core, m, dram)
        experts(nc, core, m, dram)
        combine(nc, core, m, dram)


def kernel(**inputs):
    import numpy as np
    from concourse import bacc
    from concourse.bass_utils import run_bass_kernel_spmd

    a = {k[3:]: np.asarray(v) for k, v in inputs.items()}
    c = a["c"].T.reshape(KD, P, BATCH).transpose(1, 0, 2).reshape(P, KD * BATCH)
    memn = np.concatenate([a["attn_memory"], a["attn_memory_norm"], a["attn_memory_norm"]], 1)
    arrays = {
        "x": a["attn_x"].reshape(BATCH * SEQ, D),
        "wqkv": np.concatenate([a["attn_Wq"].T, a["attn_Wk"].T, a["attn_Wv"].T], 1),
        "memn": memn, "mw": a["attn_memory_weight"], "gate": a["ffn_gate_w"],
        "w0": a["ffn_w0"], "w1": a["ffn_w1"], "wo": a["ffn_wo"], "c": c, "wmod": a["wmod"],
        "consts": constants(),
    }
    arrays = {k: np.ascontiguousarray(v) for k, v in arrays.items()}
    nc = bacc.Bacc("TRN2", target_bir_lowering=False, num_devices=1)
    dram = Names()
    for name, v in arrays.items():
        dram.__dict__[name] = nc.dram_tensor("in_" + name, v.shape, F32, kind="ExternalInput").ap()
    dram.slots_x = nc.dram_tensor("slots_x", (SLOT_TILES * P, D), F32, kind="Internal").ap()
    dram.slots_y = nc.dram_tensor("slots_y", (SLOT_TILES * P, D), F32, kind="Internal").ap()
    dram.x1 = nc.dram_tensor("x1", (BATCH * SEQ, D), F32, kind="Internal").ap()
    dram.out = nc.dram_tensor("out", (BATCH * SEQ, D), F32, kind="ExternalOutput").ap()
    build(nc, dram)
    result = run_bass_kernel_spmd(nc, [{"in_" + k: v for k, v in arrays.items()}], core_ids=[0])
    return result.results[0]["out"].reshape(BATCH, SEQ, D)
```

```python
from contextlib import ExitStack

import concourse.bass as bass
from concourse import mybir

F32 = mybir.dt.float32
BF16 = mybir.dt.bfloat16
F32R = mybir.dt.float32r
I32 = mybir.dt.int32
ALU = mybir.AluOpType
ACT = mybir.ActivationFunctionType
AX = mybir.AxisListType.X

P = 128
BATCH, SEQ, D = 2, 1024, 512
TILES = BATCH * SEQ // P
TPB = SEQ // P
KD = D // P
NQ, NH, DH = 4, 8, 16
KV = NH * DH
GROUPS = BATCH * NH
PARTS = 6
ROWS = PARTS * DH
SHIFT = 3
CHUNK = 512
STEPS = (SEQ // CHUNK) * TPB
EXPERTS, HIDDEN = 8, 1024
KH = HIDDEN // P
SLOT_TILES = 2 * TILES + EXPERTS - 1
EPS = 1e-5
SHIFT_A, SCALE_A, GATE_A, SHIFT_B, SCALE_B, GATE_B = range(6)


def wait(engine, semaphore, value):
    if not isinstance(value, int) or value > 0:
        engine.wait_ge(semaphore, value)


class Chain:

    def __init__(self, engine, semaphore, base=0):
        self.engine, self.semaphore, self.base, self.count = engine, semaphore, base, 0

    def done(self, instruction):
        instruction.then_inc(self.semaphore, 1)
        self.count += 1

    def sync(self):
        self.engine.wait_ge(self.semaphore, self.base + self.count)


class Core:

    def __init__(self, nc, stack):
        self.nc, self.stack = nc, stack
        self.psum = stack.enter_context(nc.psum_tensor("psum", [P, 8, 512], F32))

    def sb(self, name, shape, dtype=F32):
        return self.stack.enter_context(self.nc.sbuf_tensor(name, shape, dtype))

    def place_arena(self):
        self.base = -(-self.nc.sbuf_base // 64) * 64
        self.arena = self.place("arena", 0, [ARENA])

    def place(self, name, word, shape, dtype=F32):
        return self.nc.alloc_sbuf_tensor_at(name, [P] + shape, dtype, offset=self.base + 4 * word)

    def sem(self, name):
        return self.stack.enter_context(self.nc.semaphore(name))

    def at(self, word, shape, dtype=F32):
        n = 1
        for s in shape:
            n *= s
        words = n if dtype is not BF16 else n // 2
        assert word + words <= ARENA
        view = self.arena[:, word:word + words]
        if dtype is not F32:
            view = view.bitcast(dtype)
        if len(shape) > 1:
            names = "abcd"[:len(shape)]
            view = view.rearrange(f"p ({' '.join(names)}) -> p {' '.join(names)}",
                                  **dict(zip(names[1:], shape[1:])))
        return view


ARENA = 35072
AT_PARTS = 5120 + 2 * NQ * CHUNK
AT_KV = 16384
AT_Q = AT_KV + TILES * 2 * KV
AT_STAGE = AT_Q + TILES * D
AT_MOD = ARENA
AT_X = AT_MOD + BATCH * 6 * D
AT_GATE_ATT = AT_X + TILES * D
MATRIX = KD * HIDDEN
CUT = 2 * MATRIX + MATRIX // 2
AT_WO = 2 * 2 * CUT
AT_ROWS = AT_WO + MATRIX


def modulate_and_project(nc, core, m, dram):
    wmod = core.at(0, [3, KD, D])
    wmod_b = core.at(0, [3, KD, D])
    rows_b = core.place("rows_b", AT_PARTS, [D])
    WIDTH = D + 2 * KV
    wqkv = core.at(6 * KD * D, [KD, WIDTH])
    w_low = core.place("wqkv_low", 6 * KD * D, [KD, WIDTH], F32R)
    w_high = core.place("wqkv_high", 3 * KD * D, [KD, WIDTH], F32R)
    hT = core.place("hT_parts", AT_STAGE + 1024, [2, 2, KD, P], F32R)
    LOW, HIGH = 0, 1
    memn = core.at(AT_STAGE + 6144, [KV + 2])
    h_tok = [core.at(AT_STAGE + 512 * u, [D]) for u in range(2)]
    q_min = core.at(AT_PARTS + 2560, [D])
    elu = core.at(AT_STAGE + 3072, [D])
    eluT = core.at(AT_STAGE + 3584, [NQ, P])
    mem_out = core.at(AT_STAGE + 4096, [D])
    m.gate_mem = core.at(AT_STAGE + 4608, [BATCH, D])
    m.zeros = core.at(AT_STAGE + 5632, [D])
    silu_c = core.at(6 * KD * D + KD * WIDTH, [BATCH, KD, P])
    mod_tmp = core.at(AT_STAGE + 4096, [BATCH, D])

    ps_hT = core.psum[:, 0, :]
    ps_q = core.psum[:, 1, :]
    ps_kv = core.psum[:, 2, 0:2 * KV]
    ps_eluT = core.psum[:, 3, :]
    ps_mem = core.psum[:, 4:6, :].rearrange("p b (g n) -> p (b g) n", g=2)
    ps_mod = core.psum[:, 6:8, :]

    c_loaded, mw_loaded, consts_loaded, wqkv_loaded, memn_loaded = (
        core.sem(n) for n in ("c_loaded", "mw_loaded", "consts_loaded", "wqkv_loaded", "memn_loaded"))
    x_loaded = [core.sem(f"x_loaded{b}") for b in range(BATCH)]
    wmod_loaded = [core.sem(f"wmod_loaded{n}") for n in range(3)]
    wmod_b_loaded = core.sem("wmod_b_loaded")
    exp_c, exp_mw, silu_ready, mod_psum, mod_stored = (
        core.sem(n) for n in ("exp_c", "exp_mw", "silu_ready", "mod_psum", "mod_stored"))
    var_ready, std_ready, h_ready, hT_psum, high_ready, low_ready, q_psum, kv_psum, q_stored, kv_stored = (
        core.sem(n) for n in ("var_ready", "std_ready", "h_ready", "hT_psum", "h_high_ready", "h_low_ready", "q_psum",
                              "kv_psum", "q_stored", "kv_stored"))
    min_ready, exp_ready, elu_ready, eluT_psum, eluT_ready, mem_psum, mem_used = (
        core.sem(n) for n in ("min_ready", "exp_ready", "elu_ready", "eluT_psum", "eluT_ready",
                              "mem_psum", "mem_used"))
    dve_own, zeros_set, slots_zeroed, w_high_ready, w_low_ready = (
        core.sem(n) for n in ("dve_own_a", "zeros_set", "slots_zeroed", "w_high_ready", "w_low_ready"))
    order = [SCALE_A, SHIFT_A, GATE_A]
    rows_psum, rows_ready, rows_kept = (core.sem(n) for n in ("rows_psum", "rows_ready", "rows_kept"))
    b_spread = [core.sem(f"b_spread{b}") for b in range(BATCH)]

    with nc.Block() as block:
        @block.sync
        def _(sp):
            sp.dma_start(m.c_cols[:, :], dram.c).then_inc(c_loaded, 16)
            sp.dma_start(m.mw[:, 0:1], dram.mw.partition_broadcast(P)).then_inc(mw_loaded, 16)
            sp.dma_start(m.consts[:, :], dram.consts).then_inc(consts_loaded, 16)
            xs = dram.x.rearrange("(i p) d -> p i d", p=P)
            wm = dram.wmod.rearrange("(k p) (n d) -> n p k d", p=P, n=6)
            sp.dma_start(wmod[:, SCALE_A], wm[SCALE_A]).then_inc(wmod_loaded[SCALE_A], 16)
            sp.dma_start(m.x[:, 0:TPB, :], xs[:, 0:TPB, :]).then_inc(x_loaded[0], 16)
            sp.dma_start(wmod[:, SHIFT_A], wm[SHIFT_A]).then_inc(wmod_loaded[SHIFT_A], 16)
            sp.dma_start(wmod[:, GATE_A], wm[GATE_A]).then_inc(wmod_loaded[GATE_A], 16)
            sp.dma_start(wqkv, dram.wqkv.rearrange("(k p) n -> p k n", p=P)).then_inc(wqkv_loaded, 16)
            sp.dma_start(m.x[:, TPB:TILES, :], xs[:, TPB:TILES, :]).then_inc(x_loaded[1], 16)
            sp.dma_start(memn, dram.memn).then_inc(memn_loaded, 16)
            sp.wait_ge(mod_psum, 2 * len(order))
            for t in range(3):
                sp.dma_start(wmod_b[:, t], wm[3 + t]).then_inc(wmod_b_loaded, 16)
            sp.dma_start(m.gate[:, :, :], dram.gate.rearrange("(k p) e -> p k e", p=P)).then_inc(m.gate_loaded, 16)
            sp.wait_ge(rows_ready, 3)
            for t in range(3):
                sp.dma_start(dram.mod_b[:, t, :], rows_b[32 * t:32 * t + BATCH, :]).then_inc(rows_kept, 16)
            sp.wait_ge(rows_kept, 3 * 16)
            for b in range(BATCH):
                sp.dma_start(m.mod[:, b, 3:6, :], dram.mod_b[b].partition_broadcast(P)).then_inc(b_spread[b], 16)
            sp.wait_ge(zeros_set, 1)
            sp.dma_start(dram.slots_x.rearrange("(r p) d -> p r d", p=P),
                         m.zeros[:, None, :].to_broadcast([P, SLOT_TILES, D])).then_inc(slots_zeroed, 16)
            sp.wait_ge(slots_zeroed, 16)

        @block.gpsimd
        def _(pool):
            nc.gpsimd.memset(m.zeros, 0.0).then_inc(zeros_set, 1)
            pool.wait_ge(rows_kept, 3 * 16)
            pool.wait_ge(q_stored, TPB)
            pool.wait_ge(kv_stored, TPB)
            split_group(nc, pool, m, 0)
            for b in range(BATCH):
                pool.wait_ge(b_spread[b], 16)
            scale, g, sign = m.mod[:, :, SCALE_B, :], m.mod[:, :, GATE_B, :], core.at(0, [BATCH, D])
            nc.gpsimd.tensor_scalar(scale, scale, 1.0, None, ALU.add)
            nc.gpsimd.tensor_scalar(sign, g, 0.0, 2.0, ALU.is_ge, ALU.mult)
            pool.drain()
            nc.gpsimd.tensor_scalar(sign, sign, -1.0, None, ALU.add)
            pool.drain()
            nc.gpsimd.tensor_tensor(g, g, sign, ALU.mult)
            pool.drain()
            nc.gpsimd.tensor_scalar(g, g, 0.25, None, ALU.max)
            pool.drain()
            nc.gpsimd.tensor_tensor(m.gate_b[:, :, :], g, sign, ALU.mult)
            pool.drain()

        @block.scalar
        def _(act):
            act.wait_ge(c_loaded, 16)
            nc.scalar.activation(m.c_exp[:, :], m.c_cols[:, :], ACT.Exp, scale=-1.0).then_inc(exp_c, 1)
            act.wait_ge(mw_loaded, 16)
            nc.scalar.activation(m.mw[:, 1:2], m.mw[:, 0:1], ACT.Exp, scale=-1.0).then_inc(exp_mw, 1)
            act.wait_ge(consts_loaded, 16)
            nc.scalar.copy(m.ident16[:, :], m.ident[:, :])
            def keep_modulation(pieces):
                for n in pieces:
                    for b in range(BATCH):
                        act.wait_ge(mod_psum, 2 * n + b + 1)
                        one = 1.0 if order[n] == SCALE_A else 0.0
                        nc.scalar.activation(m.mod[:, b, order[n], :], ps_mod[:, b, :], ACT.Copy,
                                             bias=one).then_inc(mod_stored, 1)

            def keep_rows():
                act.wait_ge(rows_psum, 1)
                for t in range(3):
                    rows = slice(32 * t, 32 * t + BATCH)
                    nc.scalar.copy(rows_b[rows, :], ps_mod[rows, 0, :]).then_inc(rows_ready, 1)

            def find_std(b):
                tiles = slice(b * TPB, (b + 1) * TPB)
                act.wait_ge(var_ready, b + 1)
                nc.scalar.activation(m.std[:, tiles], m.var[:, tiles], ACT.Sqrt).then_inc(std_ready, 1)

            keep_modulation((0,))
            find_std(0)
            keep_modulation((1,))
            act.wait_ge(wqkv_loaded, 16)
            nc.scalar.copy(w_high[:, :, :], wqkv).then_inc(w_high_ready, 1)
            def turned_tile(i, u):
                act.wait_ge(hT_psum, i + 1)
                wait(act, kv_psum, i - 1)
                nc.scalar.copy(hT[:, u, HIGH], ps_hT.rearrange("p (k s) -> p k s", k=KD)).then_inc(high_ready, 1)

            def store_tile(i):
                act.wait_ge(q_psum, i + 1)
                nc.scalar.copy(m.q[:, i, :], ps_q).then_inc(q_stored, 1)
                act.wait_ge(kv_psum, i + 1)
                nc.scalar.copy(m.kv[:, i, :], ps_kv).then_inc(kv_stored, 1)

            def elu_exp(i):
                act.wait_ge(min_ready, i + 1)
                nc.scalar.activation(q_min, q_min, ACT.Exp).then_inc(exp_ready, 1)

            def elu_turned(i):
                act.wait_ge(eluT_psum, i + 1)
                wait(act, mem_psum, i)
                nc.scalar.activation(eluT, ps_eluT.rearrange("p (k s) -> p k s", k=NQ), ACT.Copy,
                                     bias=-1.0).then_inc(eluT_ready, 1)

            def step(i, u):
                turned_tile(i + 1, 1 - u)
                elu_exp(i - 1)
                store_tile(i)
                elu_turned(i - 1)

            keep_modulation((2,))
            turned_tile(0, 0)
            turned_tile(1, 1)
            store_tile(0)
            step(1, 1)
            find_std(1)
            keep_rows()
            with act.Fori(1, TILES // 2 - 1) as j:
                for u in range(2):
                    step(2 * j + u, u)
            step(TILES - 2, 0)
            elu_exp(TILES - 2)
            store_tile(TILES - 1)
            elu_turned(TILES - 2)
            elu_exp(TILES - 1)
            elu_turned(TILES - 1)

        @block.vector
        def _(dve):
            own = Chain(dve, dve_own)
            dve.wait_ge(exp_c, 1)
            own.done(nc.vector.tensor_scalar(m.c_exp[:, :], m.c_exp[:, :], 1.0, None, ALU.add))
            own.sync()
            own.done(nc.vector.reciprocal(m.c_exp[:, :], m.c_exp[:, :]))
            own.sync()
            own.done(nc.vector.tensor_tensor(m.c_exp[:, :], m.c_exp[:, :], m.c_cols[:, :], ALU.mult))
            own.sync()
            nc.vector.tensor_copy(
                silu_c, m.c_exp[:, :].rearrange("p (k b) -> p b k", b=BATCH)[:, :, :, None]
                .to_broadcast([P, BATCH, KD, P])).then_inc(silu_ready, 1)
            dve.wait_ge(exp_mw, 1)
            own.done(nc.vector.tensor_scalar(m.mw[:, 1:2], m.mw[:, 1:2], 1.0, None, ALU.add))
            own.sync()
            own.done(nc.vector.reciprocal(m.mw[:, 2:3], m.mw[:, 1:2]))
            own.sync()
            own.done(nc.vector.tensor_scalar(m.mw[:, 3:4], m.mw[:, 2:3], -1.0, 1.0, ALU.mult, ALU.add))
            def statistics(b):
                dve.wait_ge(x_loaded[b], 16)
                for i in range(b * TPB, (b + 1) * TPB):
                    own.done(nc.vector.bn_stats(m.stats[:, i, :], m.x[:, i, :]))
                own.sync()
                tiles = slice(b * TPB, (b + 1) * TPB)
                mean_and_variance(nc, own, m, tiles)
                nc.vector.tensor_scalar(m.var[:, tiles], m.var[:, tiles], EPS, None, ALU.add).then_inc(var_ready, 1)

            def invert(b):
                tiles = slice(b * TPB, (b + 1) * TPB)
                dve.wait_ge(std_ready, b + 1)
                own.done(nc.vector.reciprocal(m.rstd[:, tiles], m.std[:, tiles]))
                own.sync()

            statistics(0)
            invert(0)

            def find_gates():
                dve.wait_ge(mod_stored, 2 * len(order))
                g = m.mod[:, :, GATE_A, :]
                own.done(nc.vector.tensor_scalar(mod_tmp, g, 0.0, 2.0, ALU.is_ge, ALU.mult))
                own.sync()
                own.done(nc.vector.tensor_scalar(mod_tmp, mod_tmp, -1.0, None, ALU.add))
                own.done(nc.vector.scalar_tensor_tensor(g, g, -1.0, g, ALU.mult, ALU.max))
                own.sync()
                own.done(nc.vector.scalar_tensor_tensor(g, g, 0.25, mod_tmp, ALU.max, ALU.mult))
                own.sync()
                own.done(nc.vector.tensor_scalar(m.gate_mem[:, :, :], g, m.mw[:, 2:3], None, ALU.mult))
                own.done(nc.vector.tensor_scalar(m.gate_att[:, :, :], g, m.mw[:, 3:4], None, ALU.mult))
                own.sync()

            def normalise(i, u, own):
                wait(dve, hT_psum, i - 1)
                own.done(nc.vector.scalar_tensor_tensor(
                    h_tok[u], m.x[:, i, :], m.mean[:, bass.ds(i, 1)], m.mod[:, i // TPB, SCALE_A, :],
                    ALU.subtract, ALU.mult))
                own.sync()
                nc.vector.scalar_tensor_tensor(
                    h_tok[u], h_tok[u], m.rstd[:, bass.ds(i, 1)], m.mod[:, i // TPB, SHIFT_A, :],
                    ALU.mult, ALU.add).then_inc(h_ready, 1)

            def low_part(i, u):
                dve.wait_ge(high_ready, i + 1)
                nc.vector.tensor_tensor(hT[:, u, LOW], ps_hT.rearrange("p (k s) -> p k s", k=KD), hT[:, u, HIGH],
                                        ALU.subtract).then_inc(low_ready, 1)

            def elu_min(i):
                dve.wait_ge(q_stored, i + 1)
                wait(dve, elu_ready, i)
                nc.vector.tensor_scalar(q_min, m.q[:, i, :], 0.0, None, ALU.min).then_inc(min_ready, 1)

            def elu_sum(i):
                dve.wait_ge(exp_ready, i + 1)
                wait(dve, eluT_psum, i)
                nc.vector.scalar_tensor_tensor(elu, m.q[:, i, :], 0.0, q_min, ALU.max, ALU.add).then_inc(elu_ready, 1)

            def add_memory(i, own):
                dve.wait_ge(mem_psum, i + 1)
                own.done(nc.vector.reciprocal(m.mem_den[:, :], ps_mem[:, :, KV]))
                own.sync()
                for g in range(NQ):
                    last = nc.vector.scalar_tensor_tensor(
                        mem_out[:, g * KV:(g + 1) * KV], ps_mem[:, g, 0:KV], m.mem_den[:, g:g + 1],
                        m.gate_mem[:, i // TPB, g * KV:(g + 1) * KV], ALU.mult, ALU.mult)
                last.then_inc(mem_used, 1)
                dve.wait_ge(mem_used, i + 1)
                own.done(nc.vector.tensor_tensor(m.x[:, i, :], m.x[:, i, :], mem_out, ALU.add))
                own.sync()

            def step(i, u, own):
                elu_min(i - 1)
                normalise(i + 2, u, own)
                low_part(i + 1, 1 - u)
                elu_sum(i - 1)
                add_memory(i - 2, own)

            dve.wait_ge(mod_stored, 4)
            normalise(0, 0, own)
            normalise(1, 1, own)
            dve.wait_ge(w_high_ready, 1)
            nc.vector.tensor_tensor(w_low[:, :, :], wqkv, w_high[:, :, :], ALU.subtract).then_inc(w_low_ready, 1)
            low_part(0, 0)
            normalise(2, 0, own)
            low_part(1, 1)
            elu_min(0)
            normalise(3, 1, own)
            low_part(2, 0)
            elu_sum(0)
            find_gates()
            statistics(1)
            invert(1)
            per_step = 3
            with dve.Fori(1, TILES // 2 - 1) as j:
                in_loop = Chain(dve, dve_own, own.count + (j - 1) * (2 * per_step))
                step(2 * j, 0, in_loop)
                step(2 * j + 1, 1, in_loop)
                assert in_loop.count == 2 * per_step
            own.count += (TILES - 4) * per_step
            for i in range(TILES - 2, TILES + 1):
                elu_min(i - 1)
                if i == TILES - 2:
                    low_part(TILES - 1, 1)
                elu_sum(i - 1)
                add_memory(i - 2, own)
            add_memory(TILES - 1, own)

        @block.tensor
        def _(pe):
            pe.wait_ge(silu_ready, 1)

            def modulate(pieces):
                for n in pieces:
                    pe.wait_ge(wmod_loaded[order[n]], 16)
                    for b in range(BATCH):
                        wait(pe, mod_stored, 2 * (n - 1) + b + 1)
                        for k in range(KD):
                            last = nc.tensor.matmul(ps_mod[:, b, :], silu_c[:, b, k, :],
                                                    wmod[:, order[n], k, :], start=k == 0, stop=k == KD - 1)
                        last.then_inc(mod_psum, 1)

            def modulate_rows():
                pe.wait_ge(wmod_b_loaded, 3 * 16)
                pe.wait_ge(mod_stored, 2 * len(order))
                for k in range(KD):
                    for t in range(3):
                        last = nc.tensor.matmul(ps_mod[32 * t:32 * t + BATCH, 0, :], m.c_exp[:, BATCH * k:BATCH * (k + 1)],
                                                wmod_b[:, t, k, :], start=k == 0, stop=k == KD - 1)
                last.then_inc(rows_psum, 1)

            def turn_tile(i, u):
                pe.wait_ge(h_ready, i + 1)
                wait(pe, low_ready, i)
                for k in range(KD):
                    last = nc.tensor.transpose(ps_hT[:, k * P:(k + 1) * P], h_tok[u][:, k * P:(k + 1) * P],
                                               m.ident)
                last.then_inc(hT_psum, 1)

            def project(ps, u, columns, done):
                for k in range(KD):
                    for p, (h_part, w) in enumerate(((HIGH, w_high), (HIGH, w_low), (LOW, w_high))):
                        last = nc.tensor.matmul(ps, hT[:, u, h_part, k, :], w[:, k, columns],
                                                start=k + p == 0, stop=k == KD - 1 and p == 2)
                last.then_inc(done, 1)

            def project_q(i, u):
                pe.wait_ge(low_ready, i + 1)
                wait(pe, q_stored, i)
                project(ps_q, u, slice(0, D), q_psum)

            def project_kv(i, u):
                wait(pe, kv_stored, i)
                project(ps_kv, u, slice(D, WIDTH), kv_psum)

            def turn_elu(i):
                pe.wait_ge(elu_ready, i + 1)
                wait(pe, eluT_ready, i)
                for g in range(NQ):
                    last = nc.tensor.transpose(ps_eluT[:, g * P:(g + 1) * P], elu[:, g * P:(g + 1) * P], m.ident)
                last.then_inc(eluT_psum, 1)

            def remember(i):
                pe.wait_ge(eluT_ready, i + 1)
                wait(pe, mem_used, i)
                for g in range(NQ):
                    last = nc.tensor.matmul(ps_mem[:, g, 0:KV + 1], eluT[:, g, :], memn[:, 0:KV + 1],
                                            start=True, stop=True)
                last.then_inc(mem_psum, 1)

            def step(i, u):
                turn_tile(i + 1, 1 - u)
                project_q(i, u)
                remember(i - 2)
                project_kv(i, u)
                turn_elu(i - 1)

            modulate((0, 1, 2))
            pe.wait_ge(consts_loaded, 16)
            turn_tile(0, 0)
            pe.wait_ge(memn_loaded, 16)
            turn_tile(1, 1)
            pe.wait_ge(w_low_ready, 1)
            project_q(0, 0)
            project_kv(0, 0)
            turn_tile(2, 0)
            project_q(1, 1)
            project_kv(1, 1)
            turn_elu(0)
            modulate_rows()
            with pe.Fori(1, TILES // 2 - 1) as j:
                for u in range(2):
                    step(2 * j + u, u)
            step(TILES - 2, 0)
            project_q(TILES - 1, 1)
            remember(TILES - 3)
            project_kv(TILES - 1, 1)
            turn_elu(TILES - 2)
            remember(TILES - 2)
            turn_elu(TILES - 1)
            remember(TILES - 1)


def mean_and_variance(nc, own, m, tiles):
    even, odd = m.stats[:, tiles, 1], m.stats[:, tiles, 4]
    mean, var, spread = m.mean[:, tiles], m.var[:, tiles], m.std[:, tiles]
    own.done(nc.vector.tensor_tensor(mean, even, odd, ALU.add))
    own.done(nc.vector.tensor_tensor(var, even, odd, ALU.subtract))
    own.done(nc.vector.tensor_tensor(spread, m.stats[:, tiles, 2], m.stats[:, tiles, 5], ALU.add))
    own.sync()
    own.done(nc.vector.tensor_scalar(mean, mean, 0.5, None, ALU.mult))
    own.done(nc.vector.scalar_tensor_tensor(var, var, 0.25, var, ALU.mult, ALU.mult))
    own.sync()
    own.done(nc.vector.scalar_tensor_tensor(var, spread, 1.0 / D, var, ALU.mult, ALU.add))
    own.sync()


def split_group(nc, pool, m, n):
    b, h = n // NH, n % NH
    q = m.q[:, bass.ds(b * TPB, TPB), :].rearrange("p t (g w) -> p t g w", g=NQ)[:, :, :, bass.ds(h * DH, DH)]
    k = m.kv[:, bass.ds(b * TPB, TPB), bass.ds(h * DH, DH)]
    qp = m.q_parts.rearrange("p t g (j d) -> p t g j d", j=PARTS)
    kp = m.k_parts.rearrange("p t (j d) -> p t j d", j=PARTS)
    nc.gpsimd.tensor_copy(qp[:, :, :, 0, :], q)
    nc.gpsimd.tensor_copy(kp[:, :, 0, :], k)
    pool.drain()
    nc.gpsimd.tensor_tensor(m.rest, q, qp[:, :, :, 0, :], ALU.subtract)
    nc.gpsimd.tensor_tensor(m.rest_k, k, kp[:, :, 0, :], ALU.subtract)
    for j in (1, 2):
        nc.gpsimd.tensor_copy(qp[:, :, :, j, :], qp[:, :, :, 0, :])
    for j in (3, 5):
        nc.gpsimd.tensor_copy(kp[:, :, j, :], kp[:, :, 0, :])
    pool.drain()
    nc.gpsimd.tensor_copy(qp[:, :, :, 3, :], m.rest)
    nc.gpsimd.tensor_copy(kp[:, :, 1, :], m.rest_k)
    pool.drain()
    nc.gpsimd.tensor_tensor(qp[:, :, :, 5, :], m.rest, qp[:, :, :, 3, :], ALU.subtract)
    nc.gpsimd.tensor_tensor(kp[:, :, 2, :], m.rest_k, kp[:, :, 1, :], ALU.subtract)
    nc.gpsimd.tensor_copy(kp[:, :, 4, :], kp[:, :, 1, :])
    nc.gpsimd.tensor_copy(qp[:, :, :, 4, :], qp[:, :, :, 3, :])
    pool.drain().then_inc(m.ready_to_turn, 1)


def attention_order(now, ahead, behind):
    if not now and ahead:
        events = [("turn", 0), ("turn", 1)]
        for head in range(NQ):
            if head < NQ - 1:
                events.append(("turn", head + 2))
            events.extend(("peak", 8 * head + n) for n in range(8))
        return (events + [("peak", n) for n in range(32, 48)] + [("shift", 0)]
                + [("peak", n) for n in range(48, 64)])
    if not now:
        return [("out", -1), ("give", -1)]
    events, peaks = [], iter(range(64))

    def peak(n):
        if ahead:
            events.extend(("peak", x) for _, x in zip(range(n), peaks))

    between = {(0, 2): ("turn", 1), (1, 4): ("give", -1), (2, 2): ("turn", 2),
               (3, 1): ("turn", 3), (4, 1): ("shift", 1), (5, 1): ("turn", 4), (9, 1): ("give", 0),
               (10, 1): ("shift", 0)}
    peaks_in_step = {0: (0, 0, 0, 0, 0), 1: (0, 1, 1, 1, 1), 3: (1, 1, 1, 1, 1), 4: (1, 1, 1, 1, 1),
                     5: (1, 1, 1, 1, 1), 10: (1, 1, 1, 1, 1), 15: (1, 1, 1, 0, 1)}
    if ahead:
        events.append(("turn", 0))
    for k in range(STEPS):
        for n in range(NQ + 1):
            if n == NQ and (k or behind):
                events.append(("out", k - 1))
            peak(peaks_in_step.get(k, (1, 1, 1, 1, 0))[n])
            if n < NQ:
                events.append(("score", NQ * k + n))
            event = between.get((k, n))
            if event and {"turn": ahead, "give": behind or event[1] == 0,
                          "shift": ahead or event[1] == 1}[event[0]]:
                events.append(event)
    return events


def attend(nc, core, m, dram):
    q_parts, k_parts = m.q_parts, m.k_parts
    qT = core.at(0, [2, NQ, SEQ], BF16)
    kT = core.at(4096, [2, SEQ], BF16)
    probs = [core.at(5120 + 2048 * u, [NQ, CHUNK]) for u in range(2)]
    values = core.at(12288, [TPB, 32])
    out_T = core.at(12544, [CHUNK])
    peaks = core.at(13056, [64])
    peak = core.at(13120, [16])
    peak_rest = core.at(13136, [16])
    peak_parts = core.at(13152, [4, SHIFT, NQ], BF16)
    shift_T = core.at(13184, [CHUNK], BF16)
    denom = core.at(13440, [4, NQ])
    minus_peak = core.at(13456, [16])
    no_peak = core.at(13472, [16])

    ps_scores = [core.psum[:, u, :] for u in range(3)]
    ps_peak = [core.psum[:, 3 + u, :] for u in range(3)]
    ps_out = core.psum[:, 6, :]
    ps_turn = core.psum[:, 7, :]
    ps_turn16 = ps_turn.bitcast(BF16)

    (in_turn_bank, out_of_turn_bank, peak_psum, peak_used, peak_found, shift_ready,
     x1_added, shift_loaded, score_psum, exp_done, out_done, values_ready, out_stored, given, taken, kT_ones,
     dve_own) = (
        core.sem(n) for n in (
            "in_turn_bank", "out_of_turn_bank", "peak_psum", "peak_used", "peak_found",
            "shift_ready", "x1_added", "shift_loaded", "score_psum", "exp_done", "out_done", "values_ready",
            "out_stored", "given", "taken", "kT_ones", "dve_own_b"))
    FREE = 2
    UNITS = 64

    def turns_before(g):
        return 0 if isinstance(g, int) and g < 0 else 7 * g + 6

    def unit(n):
        return n // 32, n % 32 // 8, n % 8 // 2, n % 2

    def before_in_bank(n):
        return n - 2 if n >= 3 else (0, -2, -1)[n]

    def all_turns(engine, turn):
        turn(-1, False, True, False)
        turn(0, True, True, False)
        with engine.Fori(1, GROUPS - 1) as g:
            turn(g, True, True, True)
        turn(GROUPS - 1, True, False, True)
        turn(GROUPS, False, False, True)

    with nc.Block() as block:
        @block.sync
        def _(sp):
            def load_shift(n, par, c, passed):
                sp.wait_ge(out_of_turn_bank, passed)
                sp.dma_start(qT[ROWS:ROWS + SHIFT, par, :, c * CHUNK:(c + 1) * CHUNK],
                             shift_T[0:SHIFT * NQ, :]).then_inc(shift_loaded, 16)

            def turn(g, *parts):
                passed = turns_before(g)
                for what, n in attention_order(*parts):
                    if what in ("turn", "shift"):
                        passed = passed + 1
                    if what == "shift":
                        load_shift(2 * g + (1 if n else 2), (g if n else g + 1) % 2, n, passed)

            all_turns(sp, turn)
            sp.wait_ge(shift_loaded, 16 * 2 * GROUPS)

        @block.gpsimd
        def _(pool):
            def split(n):
                lead_in = isinstance(n, int) and n == 1
                pool.wait_ge(in_turn_bank, turns_before(n - 2) + turn_place(not lead_in, True, NQ))
                pool.wait_ge(kT_ones, 3)
                split_group(nc, pool, m, n)

            def stage_values(n):
                wait(pool, out_done, STEPS * n + FREE if not isinstance(n, int) or n else 0)
                pool.wait_ge(kT_ones, 3)
                b, h = n // NH, n % NH
                nc.gpsimd.tensor_copy(values[:, :, 0:DH],
                                      m.kv[:, bass.ds(b * TPB, TPB), bass.ds(h * DH + KV, DH)]).then_inc(values_ready, 1)

            def find_shift(n, c, passed):
                wait(pool, in_turn_bank, passed)
                pool.wait_ge(peak_found, 2 * n + c + 1)
                part = [peak_parts[:, :, j, :] for j in range(SHIFT)]
                whole, left = (v.rearrange("p (h t) -> p t h", t=4) for v in (minus_peak, peak_rest))
                nc.gpsimd.tensor_tensor(minus_peak, no_peak, peak, ALU.subtract)
                pool.drain()
                nc.gpsimd.tensor_copy(part[0], whole)
                pool.drain()
                nc.gpsimd.tensor_tensor(left, whole, part[0], ALU.subtract)
                pool.drain()
                nc.gpsimd.tensor_copy(part[1], left)
                pool.drain()
                nc.gpsimd.tensor_tensor(part[2], left, part[1], ALU.subtract).then_inc(shift_ready, 1)

            nc.gpsimd.memset(values[:, :, :], 0.0).then_inc(kT_ones, 1)
            pool.wait_ge(kT_ones, 1)
            nc.gpsimd.memset(values[:, :, DH:DH + 1], 1.0).then_inc(kT_ones, 1)
            pool.wait_ge(kT_ones, 2)
            nc.gpsimd.memset(kT[ROWS:ROWS + SHIFT, :, :], 1.0).then_inc(kT_ones, 1)
            pool.wait_ge(kT_ones, 3)
            nc.gpsimd.memset(no_peak, 0.0)
            split(1)
            find_shift(0, 0, 0)

            def add_output(g, c):
                pool.wait_ge(taken, 2 * g + c + 1)
                pool.wait_ge(kT_ones, 3)
                b, h = g // NH, g % NH
                tiles = bass.ds(b * TPB + 4 * c, 4)
                part, into = (v[:, tiles, :].rearrange("p t (h w) -> p t h w", h=NQ)[:, :, :, bass.ds(h * DH, DH)]
                              for v in (m.q, m.x))
                gate = m.gate_att[:, b, :].rearrange("p (h w) -> p h w", h=NQ)[:, :, bass.ds(h * DH, DH)]
                nc.gpsimd.tensor_tensor(part, part, gate[:, None].to_broadcast([P, 4, NQ, DH]), ALU.mult)
                pool.drain()
                nc.gpsimd.tensor_tensor(into, into, part, ALU.add).then_inc(x1_added, 1)

            def turn(g, ahead, prepare, behind=True):
                find_shift(g, 1, turns_before(g))
                stage_values(g)
                if behind:
                    add_output(g - 1, 1)
                if ahead:
                    find_shift(g + 1, 0, turns_before(g) + turn_place(True, True, "shift1"))
                if prepare:
                    split(g + 2)
                add_output(g, 0)

            turn(0, True, True, False)
            with pool.Fori(1, GROUPS - 2) as g:
                turn(g, True, True)
            turn(GROUPS - 2, True, False)
            turn(GROUPS - 1, False, False)
            add_output(GROUPS - 1, 1)
            pool.drain()

        @block.tensor
        def _(pe):
            def into_turn_bank(before, g, passed):
                if before == "give":
                    pe.wait_ge(taken, passed)
                elif before == "turn":
                    wait(pe, out_of_turn_bank, passed)

            def turn(g, now, ahead, behind):
                passed = turns_before(g)
                takes = 2 * g - 1 if behind else 0
                before = "turn" if now or ahead else "give"
                for what, n in attention_order(now, ahead, behind):
                    if what == "turn":
                        into_turn_bank(before, g, takes if before == "give" else passed)
                        if n == 0:
                            pe.wait_ge(m.ready_to_turn, g + 2)
                        for t in range(TPB):
                            source = k_parts[:, t, :] if n == 0 else q_parts[:, t, n - 1, :]
                            last = nc.tensor.transpose(ps_turn16[0:ROWS, t * P:(t + 1) * P], source, m.ident16[:, :])
                        last.then_inc(in_turn_bank, 1)
                        passed, before = passed + 1, "turn"
                    elif what == "shift":
                        into_turn_bank(before, g, takes if before == "give" else passed)
                        pe.wait_ge(shift_ready, 2 * g + (2 if n else 3))
                        for t in range(4):
                            last = nc.tensor.transpose(ps_turn16[0:SHIFT * NQ, t * P:(t + 1) * P],
                                                       peak_parts[:, t].rearrange("p j h -> p (j h)"),
                                                       m.ident16[:, :])
                        last.then_inc(in_turn_bank, 1)
                        passed, before = passed + 1, "turn"
                    elif what == "peak":
                        c, head, tile, keys = unit(n)
                        par = (g + 1) % 2
                        if n % 8 == 0 and n < 32:
                            pe.wait_ge(out_of_turn_bank, turns_before(g) + turn_place(now, ahead, head + 1))
                        wait(pe, peak_used, UNITS * (g + 1) + before_in_bank(n))
                        s = (c * 4 + tile) * P
                        nc.tensor.matmul(ps_peak[n % 3], qT[0:ROWS, par, head, s:s + P],
                                         kT[0:ROWS, par, keys * CHUNK:(keys + 1) * CHUNK],
                                         start=True, stop=True).then_inc(peak_psum, 1)
                    elif what == "score":
                        k, head = n // NQ, n % NQ
                        c, t = k // TPB, k % TPB
                        par = g % 2
                        if n == 0:
                            pe.wait_ge(kT_ones, 3)
                        if n % (NQ * TPB) == 0:
                            pe.wait_ge(shift_loaded, 16 * (2 * g + c + 1))
                        wait(pe, exp_done, UNITS * g + before_in_bank(n))
                        nc.tensor.matmul(
                            ps_scores[n % 3], kT[0:ROWS + SHIFT, par, t * P:(t + 1) * P],
                            qT[0:ROWS + SHIFT, par, head, c * CHUNK:(c + 1) * CHUNK],
                            start=True, stop=True).then_inc(score_psum, 1)
                    elif what == "out":
                        c, t = n // TPB, n % TPB
                        if n == 0:
                            pe.wait_ge(values_ready, g + 1)
                        if t == 0:
                            pe.wait_ge(out_stored, 2 * g + c + 1)
                        pe.wait_ge(exp_done, UNITS * g + NQ * (n + 1))
                        for head in range(NQ):
                            last = nc.tensor.matmul(ps_out[32 * head:32 * head + 32, :], values[:, t, :],
                                                    probs[n % 2][:, head, :], start=t == 0, stop=t == TPB - 1)
                        last.then_inc(out_done, 1)
                    elif what == "give":
                        into_turn_bank(before, g, takes if before == "give" else passed)
                        pe.wait_ge(out_stored, 2 * g + n + 2)
                        for t in range(4):
                            last = nc.tensor.transpose(ps_turn[:, t * P:(t + 1) * P], out_T[:, t * P:(t + 1) * P],
                                                       m.ident)
                        last.then_inc(given, 1)
                        takes, before = takes + 1, "give"

            pe.sem_inc(out_done, FREE)
            all_turns(pe, turn)

        @block.scalar
        def _(act):
            def turn(g, *parts):
                passed = turns_before(g)
                par = (g + 1) % 2
                for what, n in attention_order(*parts):
                    if what == "turn":
                        if n != 1:
                            act.wait_ge(in_turn_bank, passed + 1)
                            target = kT[0:ROWS, par, :] if n == 0 else qT[0:ROWS, par, n - 1, :]
                            nc.scalar.copy(target, ps_turn16[0:ROWS, :]).then_inc(out_of_turn_bank, 1)
                        passed = passed + 1
                    elif what == "shift":
                        act.wait_ge(in_turn_bank, passed + 1)
                        wait(act, shift_loaded, 16 * (2 * g + (1 if n else 2)))
                        nc.scalar.copy(shift_T[0:SHIFT * NQ, :], ps_turn16[0:SHIFT * NQ, 0:CHUNK]).then_inc(out_of_turn_bank, 1)
                        passed = passed + 1
                    elif what == "score":
                        k, head = n // NQ, n % NQ
                        act.wait_ge(score_psum, UNITS * g + n + 1)
                        if head == 0:
                            act.wait_ge(out_done, STEPS * g + k - 1 + FREE)
                        nc.scalar.activation(probs[k % 2][:, head, :], ps_scores[n % 3],
                                             ACT.Exp, scale=DH ** -0.5).then_inc(exp_done, 1)
                    elif what == "out" and n in (TPB - 1, -1):
                        act.wait_ge(out_done, STEPS * g + n + 1 + FREE)
                        wait(act, given, 2 * g + n // TPB)
                        nc.scalar.copy(out_T, ps_out).then_inc(out_stored, 1)

            act.sem_inc(out_stored, 1)
            all_turns(act, turn)

        @block.vector
        def _(dve):
            def turn(g, *parts):
                own = Chain(dve, dve_own, 2 * g - 1 if parts[2] else 0)
                passed = turns_before(g)
                par = (g + 1) % 2
                for what, n in attention_order(*parts):
                    if (what, n) == ("turn", 1):
                        dve.wait_ge(in_turn_bank, passed + 1)
                        nc.vector.tensor_copy(qT[0:ROWS, par, 0, :], ps_turn16[0:ROWS, :]).then_inc(out_of_turn_bank, 1)
                    if what in ("turn", "shift"):
                        passed = passed + 1
                    if what == "peak":
                        dve.wait_ge(peak_psum, UNITS * (g + 1) + n + 1)
                        nc.vector.reduce_max(peaks[:, n:n + 1], ps_peak[n % 3], AX).then_inc(peak_used, 1)
                        if n % 32 == 31:
                            c = n // 32
                            dve.wait_ge(peak_used, UNITS * (g + 1) + n + 1)
                            wait(dve, shift_ready, 2 * (g + 1) + c)
                            pairs = peaks[:, 32 * c:32 * c + 32].rearrange("p (n k) -> p n k", k=2)
                            nc.vector.tensor_reduce(peak, pairs, AX, ALU.max).then_inc(peak_found, 1)
                    elif what == "give":
                        dve.wait_ge(given, 2 * g + n + 1)
                        o = ps_turn.rearrange("p (t h w) -> p t h w", t=4, h=NQ)
                        own.done(nc.vector.reciprocal(denom, o[:, :, :, DH]))
                        own.sync()
                        of, c = (g, 0) if n == 0 else (g - 1, 1)
                        b, h = of // NH, of % NH
                        target = m.q[:, bass.ds(b * TPB + 4 * c, 4), :].rearrange(
                            "p t (h w) -> p t h w", h=NQ)[:, :, :, bass.ds(h * DH, DH)]
                        nc.vector.tensor_tensor(target, o[:, :, :, 0:DH],
                                                denom[:, :, :, None].to_broadcast([P, 4, NQ, DH]),
                                                ALU.mult).then_inc(taken, 1)
                if isinstance(g, int) and g == GROUPS - 1:
                    dve.wait_ge(x1_added, 2 * NH)
                    for i in range(TPB):
                        nc.vector.bn_stats(m.stats[:, i, :], m.x[:, i, :])

            all_turns(dve, turn)


def turn_place(now, ahead, what):
    count = 0
    for name, n in attention_order(now, ahead, False):
        if name in ("turn", "shift"):
            count += 1
            if (name, n) == ("turn", what) or (name == "shift" and what == f"shift{n}"):
                return count
    raise ValueError(what)


def route(nc, core, m, dram):
    RING = 4
    h_tok = [core.at(AT_STAGE + 3584 + 512 * u, [D]) for u in range(RING)]
    hT = [core.at(AT_STAGE + 1024 + 512 * u, [KD, P]) for u in range(2)]
    ps_hT = [core.psum[:, n, :] for n in (0, 6)]
    ps_across = [core.psum[0:EXPERTS, n, 0:2 * P] for n in (1, 3)]
    across = [core.at(AT_STAGE + 5632 + 2 * P * u, [2 * P])[0:EXPERTS] for u in range(2)]
    ps_logits = [core.psum[:, n, 0:2 * EXPERTS].rearrange("p (i e) -> p i e", e=EXPERTS) for n in (4, 5)]
    ps_rank = core.psum[:, 2, 0:(TILES + 1) * EXPERTS].rearrange("p (i e) -> p i e", e=EXPERTS)
    R = [P, TILES, EXPERTS]
    lg, pick1, pick2, masked, base = (core.at(AT_STAGE + 2048 + 128 * n, [TILES, EXPERTS]) for n in range(5))
    chosen = core.at(AT_STAGE + 2688, [TILES + 1, EXPERTS])
    top1, top2, slot_f, expo = (core.at(AT_STAGE + 2848 + 16 * n, [TILES]) for n in range(4))
    over = core.at(AT_STAGE + 2912, [EXPERTS, 16])
    lower = core.at(AT_STAGE + 3040, [EXPERTS, EXPERTS])
    counts, starts_f = (core.at(AT_STAGE + 3104 + 8 * n, [EXPERTS]) for n in range(2))
    tile_ge = core.at(AT_STAGE + 3120, [SLOT_TILES, EXPERTS - 1])
    tile_f = core.at(AT_STAGE + 3120 + SLOT_TILES * 7, [SLOT_TILES])

    (var_ready, std_ready, h_ready, h_kept, hT_psum, hT_ready, across_psum, across_ready, logit_psum, logit_used, diff_ready,
     exp_ready, chosen_ready, ranked, scattered, x1_kept, dve_own) = (
        core.sem(n) for n in ("var_ready_b", "std_ready_b", "h_ready_b", "h_kept", "hT_psum_b",
                              "hT_ready_b", "across_psum", "across_ready", "logit_psum", "logit_used", "diff_ready", "exp_ready_b",
                              "chosen_ready", "ranked", "scattered", "x1_kept", "dve_own_c"))

    with nc.Block() as block:
        @block.sync
        def _(sp):
            load_weights(sp, m, dram, 0, (W0, W1))
            sp.dma_start(dram.x1.rearrange("(i p) d -> p i d", p=P), m.x[:, :, :]).then_inc(x1_kept, 16)
            sp.wait_ge(x1_kept, 16)

        @block.gpsimd
        def _(pool):
            cut_weights(nc, pool, m, 0, (W0, W1), m.weights_ready)
            pool.wait_ge(h_kept, TILES)
            pool.wait_ge(m.slots_ready, 1)
            for i in range(TILES):
                for j in range(2):
                    nc.gpsimd.indirect_dma_start(
                        out=dram.slots_x,
                        out_offset=bass.IndirectOffsetOnAxis(ap=m.slots[:, j, i:i + 1], axis=0),
                        in_=m.q[:, i, :], in_offset=None).then_inc(scattered, 16)
            pool.wait_ge(scattered, 16 * 2 * TILES)

        @block.vector
        def _(dve):
            own = Chain(dve, dve_own)
            for i in range(TPB, TILES):
                own.done(nc.vector.bn_stats(m.stats[:, i, :], m.x[:, i, :]))
            own.sync()
            mean_and_variance(nc, own, m, slice(0, TILES))
            nc.vector.tensor_scalar(m.var[:, :], m.var[:, :], EPS, None, ALU.add).then_inc(var_ready, 1)
            dve.wait_ge(std_ready, 1)
            own.done(nc.vector.reciprocal(m.rstd[:, :], m.std[:, :]))
            own.sync()

            def normalise(j, own):
                i = RING * j
                for u in range(RING):
                    wait(dve, hT_psum, i + u - RING + 1)
                    wait(dve, h_kept, i + u - RING + 1)
                    own.done(nc.vector.scalar_tensor_tensor(
                        h_tok[u], m.x[:, i + u, :], m.mean[:, bass.ds(i + u, 1)],
                        m.mod[:, (i + u) // TPB, SCALE_B, :], ALU.subtract, ALU.mult))
                    if u:
                        finish(j, u - 1, own)
                finish(j, RING - 1, own)

            def finish(j, u, own):
                i = RING * j
                dve.wait_ge(dve_own, own.base + own.count - (0 if u == RING - 1 else 1))
                nc.vector.scalar_tensor_tensor(
                    h_tok[u], h_tok[u], m.rstd[:, bass.ds(i + u, 1)], m.mod[:, (i + u) // TPB, SHIFT_B, :],
                    ALU.mult, ALU.add).then_inc(h_ready, 1)
                if u % 2 and not isinstance(j, int):
                    keep_logits(2 * j - 2 + u // 2, u // 2)

            def keep_logits(n, bank):
                dve.wait_ge(logit_psum, n + 1)
                nc.vector.tensor_copy(lg[:, bass.ds(2 * n, 2), :], ps_logits[bank]).then_inc(logit_used, 1)

            normalise(0, own)
            with dve.Fori(1, TILES // RING) as j:
                normalise(j, Chain(dve, dve_own, own.count + (j - 1) * RING))
            own.count += RING * (TILES // RING - 1)
            for n in range(TILES // 2 - 2, TILES // 2):
                keep_logits(n, n % 2)
            dve.wait_ge(logit_used, TILES // 2)

            def pick(source, best, one_hot):
                own.done(nc.vector.tensor_reduce(best, source, AX, ALU.max))
                own.sync()
                own.done(nc.vector.tensor_tensor(one_hot, source, best[:, :, None].to_broadcast(R), ALU.is_equal))
                own.sync()
                own.done(nc.vector.tensor_tensor(one_hot, one_hot, m.falling[:, None, :].to_broadcast(R), ALU.mult))
                own.sync()
                own.done(nc.vector.tensor_reduce(slot_f, one_hot, AX, ALU.max))
                own.sync()
                own.done(nc.vector.tensor_tensor(one_hot, one_hot, slot_f[:, :, None].to_broadcast(R), ALU.is_equal))
                own.sync()

            pick(lg, top1, pick1)
            own.done(nc.vector.scalar_tensor_tensor(masked, pick1, -3e38, lg, ALU.mult, ALU.add))
            own.sync()
            pick(masked, top2, pick2)
            nc.vector.tensor_tensor(expo, top2, top1, ALU.subtract).then_inc(diff_ready, 1)
            own.done(nc.vector.memset(chosen[:, TILES, :], 0.0))
            nc.vector.tensor_tensor(chosen[:, 0:TILES, :], pick1, pick2, ALU.add).then_inc(chosen_ready, 1)
            dve.wait_ge(exp_ready, 1)
            own.done(nc.vector.tensor_scalar(top1, expo, 1.0, None, ALU.add))
            own.sync()
            own.done(nc.vector.reciprocal(m.choice[:, 0, :], top1))
            own.sync()
            own.done(nc.vector.tensor_tensor(m.choice[:, 1, :], m.choice[:, 0, :], expo, ALU.mult))
            dve.wait_ge(ranked, 1)
            own.done(nc.vector.tensor_copy(counts, ps_rank[:, TILES, :]))
            own.sync()
            own.done(nc.vector.tensor_tensor(over, counts[:, :, None].to_broadcast([P, EXPERTS, 16]),
                                             m.steps_of_128[:, None, :].to_broadcast([P, EXPERTS, 16]), ALU.is_gt))
            own.sync()
            own.done(nc.vector.tensor_reduce(counts, over, AX, ALU.add))
            own.sync()
            own.done(nc.vector.tensor_tensor(lower, counts[:, None, :].to_broadcast([P, EXPERTS, EXPERTS]),
                                             m.below, ALU.mult))
            own.sync()
            own.done(nc.vector.tensor_reduce(starts_f, lower, AX, ALU.add))
            own.sync()
            own.done(nc.vector.tensor_copy(m.starts[:, :], starts_f))
            own.done(nc.vector.tensor_tensor(
                tile_ge, m.tile_ids[:, :, None].to_broadcast([P, SLOT_TILES, EXPERTS - 1]),
                starts_f[:, None, 1:EXPERTS].to_broadcast([P, SLOT_TILES, EXPERTS - 1]), ALU.is_ge))
            own.sync()
            own.done(nc.vector.tensor_reduce(tile_f, tile_ge, AX, ALU.add))
            own.sync()
            own.done(nc.vector.tensor_copy(m.tile_expert[:, :], tile_f))
            own.done(nc.vector.tensor_scalar(starts_f, starts_f, float(P), None, ALU.mult))
            own.sync()
            own.done(nc.vector.tensor_tensor(base, ps_rank[:, 0:TILES, :], starts_f[:, None, :].to_broadcast(R), ALU.add))
            own.sync()
            for j, one_hot in enumerate((pick1, pick2)):
                own.done(nc.vector.tensor_tensor(masked, one_hot, base, ALU.mult))
                own.sync()
                own.done(nc.vector.tensor_reduce(slot_f, masked, AX, ALU.add))
                own.sync()
                own.done(nc.vector.tensor_copy(m.slots[:, j, :], slot_f))
            own.sync()
            dve.sem_inc(m.slots_ready, 1)

        @block.scalar
        def _(act):
            act.wait_ge(var_ready, 1)
            nc.scalar.activation(m.std[:, :], m.var[:, :], ACT.Sqrt).then_inc(std_ready, 1)

            def turned(i, u):
                act.wait_ge(hT_psum, i + 1)
                wait(act, across_psum, i - 1)
                nc.scalar.copy(hT[u], ps_hT[u].rearrange("p (k s) -> p k s", k=KD)).then_inc(hT_ready, 1)

            def keep(i, u):
                act.wait_ge(h_ready, i + 1)
                nc.scalar.copy(m.q[:, i, :], h_tok[u]).then_inc(h_kept, 1)

            def across_kept(n, bank):
                act.wait_ge(across_psum, 2 * n + 2)
                wait(act, logit_psum, n - 1)
                nc.scalar.copy(across[bank], ps_across[bank]).then_inc(across_ready, 1)

            def ring(j):
                i = RING * j
                for u in range(RING):
                    turned(i + u, u % 2)
                    if u == 1 and not isinstance(j, int):
                        across_kept(2 * j - 1, 1)
                    if u == 3:
                        across_kept(2 * j, 0)
                    keep(i + u, u)

            ring(0)
            with act.Fori(1, TILES // RING) as j:
                ring(j)
            across_kept(TILES // 2 - 1, 1)
            act.wait_ge(diff_ready, 1)
            nc.scalar.activation(expo, expo, ACT.Exp).then_inc(exp_ready, 1)

        @block.tensor
        def _(pe):
            pe.wait_ge(m.gate_loaded, 16)

            def turn_tile(i, u):
                pe.wait_ge(h_ready, i + 1)
                wait(pe, hT_ready, i - 1)
                for k in range(KD):
                    last = nc.tensor.transpose(ps_hT[u % 2][:, k * P:(k + 1) * P], h_tok[u][:, k * P:(k + 1) * P], m.ident)
                last.then_inc(hT_psum, 1)

            def logits(i, u, n):
                pe.wait_ge(hT_ready, i + 1)
                if u % 2 == 0:
                    wait(pe, across_ready, n - 1)
                for k in range(KD):
                    last = nc.tensor.matmul(ps_across[u // 2][:, u % 2 * P:(u % 2 + 1) * P], m.gate[:, k, :],
                                            hT[u % 2][:, k, :], start=k == 0, stop=k == KD - 1)
                last.then_inc(across_psum, 1)

            def turn_logits(n, bank):
                pe.wait_ge(across_ready, n + 1)
                wait(pe, logit_used, n - 1)
                for t in range(2):
                    last = nc.tensor.matmul(ps_logits[bank][:, t, :], across[bank][:, t * P:(t + 1) * P],
                                            m.ident[0:EXPERTS, 0:EXPERTS], start=True, stop=True)
                last.then_inc(logit_psum, 1)

            def ring(j):
                i, first = RING * j, isinstance(j, int)
                for u in range(RING):
                    turn_tile(i + u, u)
                    if not first or u:
                        logits(i + u - 1, (u - 1) % RING, 2 * j + (u + 1) // 2 - 1)
                    if u == 1 and not first:
                        turn_logits(2 * j - 1, 1)
                    if u == 3:
                        turn_logits(2 * j, 0)

            ring(0)
            with pe.Fori(1, TILES // RING) as j:
                ring(j)
            logits(TILES - 1, RING - 1, TILES // 2 - 1)
            turn_logits(TILES // 2 - 1, 1)
            pe.wait_ge(chosen_ready, 1)
            nc.tensor.matmul(ps_rank[:, 0:TILES, :], m.before, chosen[:, 0:TILES, :], start=True, stop=False,
                             skip_group_check=True)
            for i in range(TILES):
                last = nc.tensor.matmul(ps_rank[:, i + 1:TILES + 1, :], m.ones[:, :],
                                        chosen[:, i:i + 1, :].to_broadcast([P, TILES - i, EXPERTS]),
                                        start=False, stop=i == TILES - 1, skip_group_check=True)
            last.then_inc(ranked, 1)


W0, W1, WO_HALF = (0, MATRIX), (MATRIX, MATRIX), (2 * MATRIX, MATRIX // 2)


def load_weights(sp, m, dram, e, pieces):
    for piece in pieces:
        at, words = piece
        source = {W0: dram.w0[e], W1: dram.w1[e], WO_HALF: dram.wo[e][0:HIDDEN // 2]}[piece]
        sp.dma_start(m.w_raw[e % 2][:, at:at + words].rearrange("p (k n) -> p k n", n=source.shape[-1]),
                     source.rearrange("(k p) n -> p k n", p=P)).then_inc(m.w_dma[e % 2], 16)
        sp.wait_ge(m.w_dma[e % 2], loads_until(e, piece))


def loads_until(e, piece):
    return 16 * (3 * (e // 2) + (W0, W1, WO_HALF).index(piece) + 1)


def cut_weights(nc, pool, m, e, pieces, ready):
    for at, words in pieces:
        raw, (low, high) = m.w_raw[e % 2][:, at:at + words], (m.w_parts[:, e % 2, p, at:at + words] for p in range(2))
        pool.wait_ge(m.w_dma[e % 2], loads_until(e, (at, words)))
        nc.gpsimd.tensor_copy(high, raw)
        pool.drain()
        nc.gpsimd.tensor_tensor(low, raw, high, ALU.subtract)
    pool.drain().then_inc(ready, 1)


def experts(nc, core, m, dram):
    x_rows = core.place("x_rows", AT_ROWS, [2, D])
    hidden = core.place("hidden", AT_ROWS + 2 * D, [2, CHUNK])
    y_rows = core.place("y_rows", AT_ROWS + 2048, [D])
    hiddenT = core.place("hiddenT", AT_ROWS + 2560, [4, P])
    hiddenT_parts = core.place("hiddenT_parts", AT_ROWS + 3072, [2, 4, P], F32R)
    xT = core.place("xT_parts", AT_ROWS + 4096, [2, 2, KD, P], F32R)
    LOW, HIGH = 0, 1

    ps_gate = [core.psum[:, 2 * c, :] for c in range(2)]
    ps_up = [core.psum[:, 2 * c + 1, :] for c in range(2)]
    ps_xT = core.psum[:, 4, :]
    ps_hT = [core.psum[:, 5 + c, :] for c in range(2)]
    ps_y = core.psum[:, 7, :]

    x_loaded = [core.sem(f"x_rows_loaded{u}") for u in range(2)]
    wo_dma = [core.sem(f"wo_dma{u}") for u in range(2)]
    y_out, first_low_ready, half_ready = (core.sem(n) for n in ("y_out", "first_low_ready", "half_ready"))
    (wo_ready, xT_psum, high_ready, low_ready, gate_psum, up_psum, silu_ready, hidden_ready, hT_psum, hT_ready,
     y_psum, y_ready) = (
        core.sem(n) for n in ("wo_ready", "xT_psum", "high_ready", "low_ready", "gate_psum", "up_psum", "silu_ready_m",
                              "hidden_ready", "hidT_psum", "hidT_ready", "y_psum", "y_ready"))
    slots_x = dram.slots_x.rearrange("(r p) d -> r p d", p=P)
    slots_y = dram.slots_y.rearrange("(r p) d -> r p d", p=P)
    PAIRS = SLOT_TILES // 2

    with nc.Block() as block:
        @block.sync
        def _(sp):
            def load_rest(e):
                sp.dma_start(m.wo[:, e % 2], dram.wo[e][HIDDEN // 2:HIDDEN].rearrange("(k p) n -> p k n", p=P)
                             ).then_inc(wo_dma[e % 2], 16)

            def announce(e):
                sp.wait_ge(wo_dma[e % 2], 16 * (e // 2 + 1))
                sp.sem_inc(wo_ready, 1)

            sp.wait_ge(x_loaded[0], 16)
            load_weights(sp, m, dram, 0, (WO_HALF,))
            load_rest(0)
            announce(0)
            load_weights(sp, m, dram, 1, (W0, W1, WO_HALF))
            load_rest(1)
            announce(1)
            for e in range(2, EXPERTS):
                tiles = sp.value_load(m.starts[0:1, e - 1:e], min_val=0, max_val=SLOT_TILES)
                sp.wait_ge(up_psum, 2 * tiles + 1)
                load_weights(sp, m, dram, e, (W0, W1))
                sp.wait_ge(y_psum, tiles + 1)
                load_weights(sp, m, dram, e, (WO_HALF,))
                load_rest(e)
                announce(e)

        @block.gpsimd
        def _(pool):
            cut_weights(nc, pool, m, 0, (WO_HALF,), half_ready)
            for e in range(1, EXPERTS):
                cut_weights(nc, pool, m, e, (W0, W1), m.weights_ready)
                cut_weights(nc, pool, m, e, (WO_HALF,), half_ready)

        @block.tensor
        def _(pe):
            def turn_rows(r, u, j):
                pe.wait_ge(x_loaded[u], 16 * (j + 1))
                wait(pe, low_ready, r)
                for k in range(KD):
                    last = nc.tensor.transpose(ps_xT[:, k * P:(k + 1) * P], x_rows[:, u, k * P:(k + 1) * P], m.ident)
                last.then_inc(xT_psum, 1)

            def weights_of(r, *ready):
                e = pe.value_load(m.tile_expert[0:1, bass.ds(r, 1)], min_val=0, max_val=EXPERTS - 1)
                for semaphore in ready:
                    pe.wait_ge(semaphore, e + 1)
                return e % 2

            def widen(r, u, c, buffer):
                wait(pe, hidden_ready, 2 * r - 1 + c)
                for ps, n, psum_sem in ((ps_gate[c], 0, gate_psum), (ps_up[c], 1, up_psum)):
                    for k in range(KD):
                        for p, (x_part, w_part) in enumerate(((HIGH, HIGH), (HIGH, LOW), (LOW, HIGH))):
                            at = w_part * CUT + (n * KD + k) * HIDDEN + c * CHUNK
                            last = nc.tensor.matmul(ps, xT[:, u, x_part, k, :],
                                                    parts[:, buffer, at:at + CHUNK],
                                                    start=k + p == 0, stop=k == KD - 1 and p == 2)
                    last.then_inc(psum_sem, 1)

            def turn_hidden(r, c):
                pe.wait_ge(hidden_ready, 2 * r + c + 1)
                if c == 0:
                    wait(pe, first_low_ready, r)
                else:
                    wait(pe, hT_ready, 2 * r)
                for k in range(4):
                    last = nc.tensor.transpose(ps_hT[c][:, k * P:(k + 1) * P], hidden[:, c, k * P:(k + 1) * P], m.ident)
                last.then_inc(hT_psum, 1)

            def narrow(r, buffer):
                wait(pe, y_ready, r)
                pe.wait_ge(first_low_ready, r + 1)
                for k in range(4):
                    for p, (h_part, w_part) in enumerate(((HIGH, HIGH), (HIGH, LOW), (LOW, HIGH))):
                        at = w_part * CUT + 2 * MATRIX + k * D
                        nc.tensor.matmul(ps_y, hiddenT_parts[:, h_part, k, :], parts[:, buffer, at:at + D],
                                         start=k + p == 0, stop=False)
                pe.wait_ge(hT_ready, 2 * r + 2)
                for k in range(4):
                    last = nc.tensor.matmul(ps_y, hiddenT[:, k, :], wo[:, buffer, k * D:(k + 1) * D],
                                            start=False, stop=k == 3)
                last.then_inc(y_psum, 1)

            def step(r, u, j, more):
                turn_hidden(r - 1, 0)
                now = weights_of(r, m.weights_ready)
                pe.wait_ge(low_ready, r + 1)
                widen(r, u, 0, now)
                turn_hidden(r - 1, 1)
                widen(r, u, 1, now)
                if more:
                    turn_rows(r + 1, 1 - u, j + u)
                past = weights_of(r - 1, half_ready, wo_ready)
                narrow(r - 1, past)

            parts = m.w_parts[:, :, :, :].rearrange("p b h w -> p b (h w)")
            wo = m.wo[:, :, :, :].rearrange("p b k n -> p b (k n)")
            pe.sem_inc(y_psum, 1)
            pe.sem_inc(up_psum, 1)
            turn_rows(0, 0, 0)
            first = weights_of(0, m.weights_ready)
            pe.wait_ge(low_ready, 1)
            widen(0, 0, 0, first)
            widen(0, 0, 1, first)
            turn_rows(1, 1, 0)
            step(1, 1, 0, True)
            with pe.Fori(1, PAIRS) as j:
                step(2 * j, 0, j, True)
                step(2 * j + 1, 1, j, True)
            step(SLOT_TILES - 1, 0, PAIRS, False)
            turn_hidden(SLOT_TILES - 1, 0)
            turn_hidden(SLOT_TILES - 1, 1)
            past = weights_of(SLOT_TILES - 1, half_ready, wo_ready)
            narrow(SLOT_TILES - 1, past)

        @block.scalar
        def _(act):
            def load_rows(r, u):
                act.dma_start(x_rows[:, u], slots_x[r]).then_inc(x_loaded[u], 16)

            def turned_rows(r, u, more=True):
                act.wait_ge(xT_psum, r + 1)
                wait(act, up_psum, 2 * (r - 1) + 1 if not isinstance(r, int) or r > 1 else 0)
                nc.scalar.copy(xT[:, u, HIGH], ps_xT.rearrange("p (k s) -> p k s", k=KD)).then_inc(high_ready, 1)
                if more:
                    load_rows(r + 2, u)

            def gate(r, c):
                act.wait_ge(gate_psum, 2 * r + c + 1)
                nc.scalar.activation(hidden[:, c], ps_gate[c], ACT.Silu).then_inc(silu_ready, 1)

            def turned_hidden(r, c):
                act.wait_ge(hT_psum, 2 * r + c + 1)
                wait(act, y_psum, r + 1)
                target = hiddenT_parts[:, HIGH] if c == 0 else hiddenT[:, :, :]
                nc.scalar.copy(target, ps_hT[c].rearrange("p (k s) -> p k s", k=4)).then_inc(hT_ready, 1)

            def store(r):
                act.wait_ge(y_psum, r + 2)
                wait(act, y_out, 16 * r)
                nc.scalar.copy(y_rows[:, :], ps_y).then_inc(y_ready, 1)
                act.wait_ge(y_ready, r + 1)
                act.dma_start(slots_y[r], y_rows[:, :]).then_inc(y_out, 16)

            def step(r, u, more):
                turned_hidden(r - 1, 0)
                gate(r, 0)
                turned_hidden(r - 1, 1)
                gate(r, 1)
                if more:
                    turned_rows(r + 1, 1 - u, more != "last")
                store(r - 1)

            load_rows(0, 0)
            load_rows(1, 1)
            turned_rows(0, 0)
            gate(0, 0)
            gate(0, 1)
            turned_rows(1, 1)
            step(1, 1, True)
            with act.Fori(1, PAIRS - 1) as j:
                step(2 * j, 0, True)
                step(2 * j + 1, 1, True)
            step(SLOT_TILES - 3, 0, "last")
            step(SLOT_TILES - 2, 1, "last")
            step(SLOT_TILES - 1, 0, False)
            turned_hidden(SLOT_TILES - 1, 0)
            turned_hidden(SLOT_TILES - 1, 1)
            store(SLOT_TILES - 1)
            act.wait_ge(y_out, 16 * SLOT_TILES)

        @block.vector
        def _(dve):
            def low_part(r, u):
                dve.wait_ge(high_ready, r + 1)
                nc.vector.tensor_tensor(xT[:, u, LOW], ps_xT.rearrange("p (k s) -> p k s", k=KD), xT[:, u, HIGH],
                                        ALU.subtract).then_inc(low_ready, 1)

            def first_low(r):
                dve.wait_ge(hT_ready, 2 * r + 1)
                nc.vector.tensor_tensor(hiddenT_parts[:, LOW], ps_hT[0].rearrange("p (k s) -> p k s", k=4),
                                        hiddenT_parts[:, HIGH], ALU.subtract).then_inc(first_low_ready, 1)

            def widened(r):
                for c in range(2):
                    dve.wait_ge(silu_ready, 2 * r + c + 1)
                    dve.wait_ge(up_psum, 2 * r + c + 2)
                    nc.vector.tensor_tensor(hidden[:, c], hidden[:, c], ps_up[c], ALU.mult).then_inc(hidden_ready, 1)

            def step(r, u):
                first_low(r - 1)
                widened(r)
                low_part(r + 1, 1 - u)

            low_part(0, 0)
            widened(0)
            low_part(1, 1)
            step(1, 1)
            with dve.Fori(1, PAIRS) as j:
                step(2 * j, 0)
                step(2 * j + 1, 1)
            first_low(SLOT_TILES - 2)
            widened(SLOT_TILES - 1)
            first_low(SLOT_TILES - 1)


def combine(nc, core, m, dram):
    RING = 4
    rows = core.at(0, [RING, 2, D])
    gathered = [core.sem(f"gathered{n}") for n in range(RING)]
    scaled, combined, stored, dve_own = (core.sem(n) for n in ("scaled", "combined", "stored", "dve_own_d"))
    QUARTER = TILES // 4
    x1_loaded = [core.sem(f"x1_loaded{n}") for n in range(4)]
    out = dram.out.rearrange("(i p) d -> p i d", p=P)

    with nc.Block() as block:
        @block.gpsimd
        def _(pool):
            for i in range(TILES):
                wait(pool, combined, i - RING + 1)
                for j in range(2):
                    nc.gpsimd.indirect_dma_start(
                        out=rows[:, i % RING, j, :], out_offset=None, in_=dram.slots_y,
                        in_offset=bass.IndirectOffsetOnAxis(ap=m.slots[:, j, i:i + 1], axis=0)
                    ).then_inc(gathered[i % RING], 16)

        @block.scalar
        def _(act):
            for i in range(TILES):
                act.wait_ge(gathered[i % RING], 32 * (i // RING + 1))
                row = rows[:, i % RING, 0, :]
                nc.scalar.activation(row, row, ACT.Copy, scale=m.choice[:, 0, i:i + 1]).then_inc(scaled, 1)

        @block.vector
        def _(dve):
            for i in range(TILES):
                own = Chain(dve, dve_own, 2 * i)
                first, second = rows[:, i % RING, 0, :], rows[:, i % RING, 1, :]
                dve.wait_ge(scaled, i + 1)
                own.done(nc.vector.scalar_tensor_tensor(first, second, m.choice[:, 1, i:i + 1], first,
                                                        ALU.mult, ALU.add))
                own.sync()
                own.done(nc.vector.tensor_tensor(first, first, m.gate_b[:, i // TPB, :], ALU.mult))
                own.sync()
                if i % QUARTER == 0:
                    dve.wait_ge(x1_loaded[i // QUARTER], 16)
                nc.vector.tensor_tensor(m.x[:, i, :], m.x[:, i, :], first, ALU.add).then_inc(combined, 1)

        @block.sync
        def _(sp):
            x1 = dram.x1.rearrange("(i p) d -> p i d", p=P)
            for n in range(4):
                tiles = slice(n * QUARTER, (n + 1) * QUARTER)
                sp.dma_start(m.x[:, tiles, :], x1[:, tiles, :]).then_inc(x1_loaded[n], 16)
            for i in range(TILES):
                sp.wait_ge(combined, i + 1)
                sp.dma_start(out[:, i, :], m.x[:, i, :]).then_inc(stored, 16)
            sp.wait_ge(stored, 16 * TILES)


class Names:
    pass


def constants():
    import numpy as np
    cols = [np.eye(P), np.triu(np.ones((P, P)), 1), np.ones((P, P)),
            np.tile(np.arange(EXPERTS, 0, -1), (P, 1)), np.tile(P * np.arange(16), (P, 1)),
            np.tile(np.tril(np.ones((EXPERTS, EXPERTS)), -1).ravel(), (P, 1)),
            np.tile(np.arange(SLOT_TILES), (P, 1))]
    return np.concatenate(cols, 1).astype(np.float32)


def build(nc, dram):
    with ExitStack() as stack:
        core, m = Core(nc, stack), Names()
        width = 3 * P + EXPERTS + 16 + EXPERTS * EXPERTS + SLOT_TILES
        m.consts = core.sb("consts", [P, width])
        m.ident, m.before, m.ones = (m.consts[:, n * P:(n + 1) * P] for n in range(3))
        at = 3 * P
        m.falling = m.consts[:, at:at + EXPERTS]
        m.steps_of_128 = m.consts[:, at + 8:at + 24]
        m.below = m.consts[:, at + 24:at + 88].rearrange("p (a b) -> p a b", b=EXPERTS)
        m.tile_ids = m.consts[:, at + 88:at + 88 + SLOT_TILES]
        m.ident16 = core.sb("ident16", [P, P], BF16)
        m.gate_b = core.sb("gate_b", [P, BATCH, D])
        m.gate = core.sb("gate", [P, KD, EXPERTS])
        m.c_cols = core.sb("c_cols", [P, KD * BATCH])
        m.c_exp = core.sb("c_exp", [P, KD * BATCH])
        m.mw = core.sb("mw", [P, 4])
        m.mem_den = core.sb("mem_den", [P, NQ])
        m.stats = core.sb("stats", [P, TILES, 6])
        m.mean, m.var, m.std, m.rstd = (core.sb(n, [P, TILES]) for n in ("mean", "var", "std", "rstd"))
        m.choice = core.sb("choice", [P, 2, TILES])
        m.slots = core.sb("slots", [P, 2, TILES], I32)
        m.starts = core.sb("starts", [P, EXPERTS], I32)
        m.tile_expert = core.sb("tile_expert", [P, SLOT_TILES], I32)
        m.gate_loaded, m.slots_ready = core.sem("gate_loaded"), core.sem("slots_ready")
        m.ready_to_turn = core.sem("ready_to_turn")
        m.w_dma = [core.sem(f"w_dma{u}") for u in range(2)]
        m.weights_ready = core.sem("weights_ready")
        core.place_arena()
        m.mod = core.place("mod", AT_MOD, [BATCH, 6, D])
        m.x = core.place("x_tokens", AT_X, [TILES, D])
        m.gate_att = core.place("gate_att", AT_GATE_ATT, [BATCH, D])
        m.w_raw = [core.place(f"w_raw{u}", 2 * u * CUT, [CUT]) for u in range(2)]
        m.w_parts = core.place("w_parts", 0, [2, 2, CUT], F32R)
        m.wo = core.place("wo_half", AT_WO, [2, KH // 2, D])
        m.q = core.at(AT_Q, [TILES, D])
        m.kv = core.at(AT_KV, [TILES, 2 * KV])
        m.q_parts = core.at(AT_PARTS, [TPB, NQ, ROWS], BF16)
        m.k_parts = core.at(AT_PARTS + 1536, [TPB, ROWS], BF16)
        m.rest = core.at(AT_PARTS + 1920, [TPB, NQ, DH])
        m.rest_k = core.at(AT_PARTS + 2432, [TPB, DH])
        modulate_and_project(nc, core, m, dram)
        attend(nc, core, m, dram)
        route(nc, core, m, dram)
        experts(nc, core, m, dram)
        combine(nc, core, m, dram)


def kernel(**inputs):
    import numpy as np
    from concourse import bacc
    from concourse.bass_utils import run_bass_kernel_spmd

    a = {k[3:]: np.asarray(v) for k, v in inputs.items()}
    c = a["c"].T.reshape(KD, P, BATCH).transpose(1, 0, 2).reshape(P, KD * BATCH)
    memn = np.concatenate([a["attn_memory"], a["attn_memory_norm"], a["attn_memory_norm"]], 1)
    arrays = {
        "x": a["attn_x"].reshape(BATCH * SEQ, D),
        "wqkv": np.concatenate([a["attn_Wq"].T, a["attn_Wk"].T, a["attn_Wv"].T], 1),
        "memn": memn, "mw": a["attn_memory_weight"], "gate": a["ffn_gate_w"],
        "w0": a["ffn_w0"], "w1": a["ffn_w1"], "wo": a["ffn_wo"], "c": c, "wmod": a["wmod"],
        "consts": constants(),
    }
    arrays = {k: np.ascontiguousarray(v) for k, v in arrays.items()}
    nc = bacc.Bacc("TRN2", target_bir_lowering=False, num_devices=1)
    dram = Names()
    for name, v in arrays.items():
        dram.__dict__[name] = nc.dram_tensor("in_" + name, v.shape, F32, kind="ExternalInput").ap()
    dram.slots_x = nc.dram_tensor("slots_x", (SLOT_TILES * P, D), F32, kind="Internal").ap()
    dram.slots_y = nc.dram_tensor("slots_y", (SLOT_TILES * P, D), F32, kind="Internal").ap()
    dram.mod_b = nc.dram_tensor("mod_b", (BATCH, 3, D), F32, kind="Internal").ap()
    dram.x1 = nc.dram_tensor("x1", (BATCH * SEQ, D), F32, kind="Internal").ap()
    dram.out = nc.dram_tensor("out", (BATCH * SEQ, D), F32, kind="ExternalOutput").ap()
    build(nc, dram)
    result = run_bass_kernel_spmd(nc, [{"in_" + k: v for k, v in arrays.items()}], core_ids=[0])
    return result.results[0]["out"].reshape(BATCH, SEQ, D)
```
